# Optimizing a Trainium2 kernel written in Bass

```python
import numpy as np
import jax
import jax.numpy as jnp

def _softmax(x, axis=-1):
    return jax.nn.softmax(x, axis=axis)
def _gelu(x):
    return jax.nn.gelu(x, approximate=True)
def _silu(x):
    return jax.nn.silu(x)
def _sigmoid(x):
    return jax.nn.sigmoid(x)
def _layernorm(x, axis=-1, eps=1e-5):
    m = jnp.mean(x, axis=axis, keepdims=True)
    v = jnp.var(x, axis=axis, keepdims=True)
    return (x - m) / jnp.sqrt(v + eps)
def _scatter_add(tgt, idx, src, axis=0):
    return tgt.at[idx].add(src)
def _segment_sum(src, seg, n):
    return jax.ops.segment_sum(src, seg, n)

kernel_name = 'mk_conv_preact_d4_conv_nchw128_2e9b8b'

def setup_inputs(seed: int = 0):
    np.random.seed(seed)
    _w = jnp.asarray
    def _rec_inputs():
        import jax
        import jax.numpy as jnp
        _gk = jax.random.key(seed)
        x = -0.0009438 + 1 * jax.random.normal(jax.random.fold_in(_gk, 1), (1, 128, 96, 96), jnp.float32)
        return x
    x = _rec_inputs()
    def _L0_conv_setup():
        import jax, jax.numpy as jnp
        import numpy as np
        DIM = 128
        HEADS = 8
        HD = DIM // HEADS
        KS = 8
        STRIDE = 2
        DIL = 2

        def axis_indices(L, k, s, d):
            idx = np.zeros((L, k), dtype=np.int32)
            for i in range(L):
                ic = min(i // s * s + (s - 1) // 2, L - 1)
                r = ic % d
                Lsub = (L - r + d - 1) // d
                ii = ic // d
                start = min(max(ii - (k - 1) // 2, 0), max(Lsub - k, 0))
                for j in range(k):
                    idx[i, j] = r + d * min(start + j, Lsub - 1)
            return idx
        key = jax.random.key(seed)
        ks = jax.random.split(key, 5)
        x = jax.random.normal(ks[0], (1, DIM, 96, 96), jnp.float32)
        qkv_w = jax.random.normal(ks[1], (3 * DIM, 1, 3, 3), jnp.float32) * 0.1
        qkv_b = jax.random.normal(ks[2], (3 * DIM,), jnp.float32) * 0.02
        proj_w = jax.random.normal(ks[3], (DIM, DIM, 1, 1), jnp.float32) * DIM ** (-0.5)
        proj_b = jax.random.normal(ks[4], (DIM,), jnp.float32) * 0.02
        return {'x': x, 'qkv_w': qkv_w, 'qkv_b': qkv_b, 'proj_w': proj_w, 'proj_b': proj_b}
    _L0_conv_all = _L0_conv_setup()
    _L0_conv_in = {k: v for k, v in _L0_conv_all.items() if k in ('qkv_w', 'qkv_b', 'proj_w', 'proj_b', )}
    del _L0_conv_all

    def _L1_conv_setup():
        import jax, jax.numpy as jnp
        import numpy as np
        EPS = 1e-05

        def _message_pass(inputs, conv_w, gamma, beta, run_mean, run_var):
            scale = gamma / jnp.sqrt(run_var + EPS)
            shift = beta - run_mean * scale

            def f(s):
                y = jax.lax.conv_general_dilated(s, conv_w, window_strides=(1,), padding=[(4, 4)], dimension_numbers=('NCW', 'OIW', 'NCW'))
                return jax.nn.relu(y * scale[None, :, None] + shift[None, :, None])

            def step(carry, old_slice):
                new = f(carry) + old_slice
                return (new, new)
            xs = jnp.moveaxis(inputs, 2, 0)
            _, ys = jax.lax.scan(step, xs[0], xs[1:])
            new = jnp.concatenate([xs[:1], ys], axis=0)
            _, ys2 = jax.lax.scan(step, new[-1], new[:-1], reverse=True)
            out = jnp.concatenate([ys2, new[-1:]], axis=0)
            return jnp.moveaxis(out, 0, 2)
        key = jax.random.key(seed)
        ks = jax.random.split(key, 6)
        B, C, H, W = (16, 128, 64, 256)
        inputs = jax.random.normal(ks[0], (B, C, H, W), jnp.float32)
        conv_w = jax.random.normal(ks[1], (C, C, 9), jnp.float32) * (1.0 / np.sqrt(C * 9))
        gamma = jax.random.uniform(ks[2], (C,), jnp.float32, minval=0.5, maxval=1.5)
        beta = jax.random.normal(ks[3], (C,), jnp.float32) * 0.1
        run_mean = jax.random.normal(ks[4], (C,), jnp.float32) * 0.1
        run_var = jax.random.uniform(ks[5], (C,), jnp.float32, minval=0.5, maxval=1.5)
        return dict(inputs=inputs, conv_w=conv_w, gamma=gamma, beta=beta, run_mean=run_mean, run_var=run_var)
    _L1_conv_all = _L1_conv_setup()
    _L1_conv_in = {k: v for k, v in _L1_conv_all.items() if k in ('conv_w', 'gamma', 'beta', 'run_mean', 'run_var', )}
    del _L1_conv_all

    def _L2_conv_setup():
        import jax, jax.numpy as jnp
        import numpy as np
        PAD = 1
        key = jax.random.key(seed)
        k1, k2, k3 = jax.random.split(key, 3)
        N, C, F, H, W, HH, WW = (32, 128, 128, 32, 32, 3, 3)
        x = jax.random.normal(k1, (N, C, H, W), dtype=jnp.float32)
        weight = jax.random.normal(k2, (F, C, HH, WW), dtype=jnp.float32) * 0.05
        bias = jax.random.normal(k3, (F,), dtype=jnp.float32) * 0.05
        return {'x': x, 'weight': weight, 'bias': bias}
    _L2_conv_all = _L2_conv_setup()
    _L2_conv_in = {k: v for k, v in _L2_conv_all.items() if k in ('weight', 'bias', )}
    del _L2_conv_all

    def _L3_conv_setup():
        import jax, jax.numpy as jnp
        import numpy as np
        DG = 8
        K = 9

        def _conv3x3(x, w, b):
            y = jax.lax.conv_general_dilated(x, w, (1, 1), ((1, 1), (1, 1)), dimension_numbers=('NCHW', 'OIHW', 'NCHW'))
            return y + b[None, :, None, None]

        def _deform_conv_v2(x, off_y, off_x, mask, w, b):
            B, C, H, W = x.shape
            cpg = C // DG
            k = jnp.arange(K)
            ky = (k // 3 - 1).astype(x.dtype)[None, None, :, None, None]
            kx = (k % 3 - 1).astype(x.dtype)[None, None, :, None, None]
            hh = jnp.arange(H, dtype=x.dtype)[None, None, None, :, None]
            ww = jnp.arange(W, dtype=x.dtype)[None, None, None, None, :]
            py = hh + ky + off_y
            px = ww + kx + off_x
            y0 = jnp.floor(py)
            x0 = jnp.floor(px)
            ly = py - y0
            lx = px - x0
            xf = x.reshape(B, DG, cpg, H * W)

            def corner(yi, xi):
                valid = ((yi >= 0) & (yi < H) & (xi >= 0) & (xi < W)).astype(x.dtype)
                idx = (jnp.clip(yi, 0, H - 1) * W + jnp.clip(xi, 0, W - 1)).astype(jnp.int32)
                idxb = jnp.broadcast_to(idx.reshape(B, DG, 1, K * H * W), (B, DG, cpg, K * H * W))
                v = jnp.take_along_axis(xf, idxb, axis=3).reshape(B, DG, cpg, K, H, W)
                return (v, valid)
            v00, m00 = corner(y0, x0)
            v01, m01 = corner(y0, x0 + 1)
            v10, m10 = corner(y0 + 1, x0)
            v11, m11 = corner(y0 + 1, x0 + 1)
            w00 = ((1 - ly) * (1 - lx) * m00)[:, :, None]
            w01 = ((1 - ly) * lx * m01)[:, :, None]
            w10 = (ly * (1 - lx) * m10)[:, :, None]
            w11 = (ly * lx * m11)[:, :, None]
            val = (v00 * w00 + v01 * w01 + v10 * w10 + v11 * w11) * mask[:, :, None]
            wr = w.reshape(w.shape[0], DG, cpg, K)
            return jnp.einsum('bgckhw,ogck->bohw', val, wr) + b[None, :, None, None]
        key = jax.random.key(seed)
        ks = jax.random.split(key, 9)
        B, C, H, W = (8, 128, 64, 64)
        return {'feat_l': jax.random.normal(ks[0], (B, C, H, W), jnp.float32), 'feat_s': jax.random.normal(ks[1], (B, C, H // 2, W // 2), jnp.float32), 'w_atten': jax.random.normal(ks[2], (C, C), jnp.float32) / np.sqrt(C), 'w_fsm': jax.random.normal(ks[3], (C, C), jnp.float32) / np.sqrt(C), 'w_off': jax.random.normal(ks[4], (C, 2 * C), jnp.float32) / np.sqrt(2 * C), 'w_cm': jax.random.normal(ks[5], (DG * 3 * K, C, 3, 3), jnp.float32) * 0.01, 'b_cm': jnp.zeros((DG * 3 * K,), jnp.float32), 'w_dcn': jax.random.normal(ks[6], (C, C, 3, 3), jnp.float32) / np.sqrt(C * 9), 'b_dcn': jax.random.normal(ks[7], (C,), jnp.float32) * 0.01}
    _L3_conv_all = _L3_conv_setup()
    _L3_conv_in = {k: v for k, v in _L3_conv_all.items() if k in ('feat_s', 'w_atten', 'w_fsm', 'w_off', 'w_cm', 'b_cm', 'w_dcn', 'b_dcn', )}
    del _L3_conv_all

    return {
        "x": x,
        "L0_conv_qkv_w": _L0_conv_in["qkv_w"],
        "L0_conv_qkv_b": _L0_conv_in["qkv_b"],
        "L0_conv_proj_w": _L0_conv_in["proj_w"],
        "L0_conv_proj_b": _L0_conv_in["proj_b"],
        "L1_conv_conv_w": _L1_conv_in["conv_w"],
        "L1_conv_gamma": _L1_conv_in["gamma"],
        "L1_conv_beta": _L1_conv_in["beta"],
        "L1_conv_run_mean": _L1_conv_in["run_mean"],
        "L1_conv_run_var": _L1_conv_in["run_var"],
        "L2_conv_weight": _L2_conv_in["weight"],
        "L2_conv_bias": _L2_conv_in["bias"],
        "L3_conv_feat_s": _L3_conv_in["feat_s"],
        "L3_conv_w_atten": _L3_conv_in["w_atten"],
        "L3_conv_w_fsm": _L3_conv_in["w_fsm"],
        "L3_conv_w_off": _L3_conv_in["w_off"],
        "L3_conv_w_cm": _L3_conv_in["w_cm"],
        "L3_conv_b_cm": _L3_conv_in["b_cm"],
        "L3_conv_w_dcn": _L3_conv_in["w_dcn"],
        "L3_conv_b_dcn": _L3_conv_in["b_dcn"],
    }

def reference(x, L0_conv_qkv_w, L0_conv_qkv_b, L0_conv_proj_w, L0_conv_proj_b, L1_conv_conv_w, L1_conv_gamma, L1_conv_beta, L1_conv_run_mean, L1_conv_run_var, L2_conv_weight, L2_conv_bias, L3_conv_feat_s, L3_conv_w_atten, L3_conv_w_fsm, L3_conv_w_off, L3_conv_w_cm, L3_conv_b_cm, L3_conv_w_dcn, L3_conv_b_dcn):
    import jax
    import jax.numpy as jnp
    def _L0_conv_ref(x, qkv_w, qkv_b, proj_w, proj_b):
        import jax, jax.numpy as jnp
        import numpy as np
        DIM = 128
        HEADS = 8
        HD = DIM // HEADS
        KS = 8
        STRIDE = 2
        DIL = 2

        def axis_indices(L, k, s, d):
            idx = np.zeros((L, k), dtype=np.int32)
            for i in range(L):
                ic = min(i // s * s + (s - 1) // 2, L - 1)
                r = ic % d
                Lsub = (L - r + d - 1) // d
                ii = ic // d
                start = min(max(ii - (k - 1) // 2, 0), max(Lsub - k, 0))
                for j in range(k):
                    idx[i, j] = r + d * min(start + j, Lsub - 1)
            return idx
        B, C, H, W = x.shape
        qkv = jax.lax.conv_general_dilated(x, qkv_w, window_strides=(1, 1), padding=[(1, 1), (1, 1)], dimension_numbers=('NCHW', 'OIHW', 'NCHW'), feature_group_count=C)
        qkv = qkv + qkv_b[None, :, None, None]
        qkv = qkv.reshape(B, 3, C, H, W)

        def to_heads(t):
            return t.reshape(B, HEADS, HD, H, W).transpose(0, 3, 4, 1, 2)
        q = to_heads(qkv[:, 0])
        k = to_heads(qkv[:, 1])
        v = to_heads(qkv[:, 2])
        scale = HD ** (-0.5)
        ri = jnp.asarray(axis_indices(H, KS, STRIDE, DIL))
        ci = jnp.asarray(axis_indices(W, KS, STRIDE, DIL))
        R = ri[:, :, None, None]
        Cc = ci[None, None, :, :]
        k_win = k[:, R, Cc]
        v_win = v[:, R, Cc]
        logits = jnp.einsum('bijnd,bipjqnd->bijnpq', q * scale, k_win)
        attn = jax.nn.softmax(logits.reshape(B, H, W, HEADS, KS * KS), axis=-1)
        attn = attn.reshape(B, H, W, HEADS, KS, KS)
        out = jnp.einsum('bijnpq,bipjqnd->bijnd', attn, v_win)
        out = out.transpose(0, 3, 4, 1, 2).reshape(B, C, H, W)
        out = jnp.einsum('bchw,oc->bohw', out, proj_w[:, :, 0, 0]) + proj_b[None, :, None, None]
        return out

    def _L1_conv_ref(inputs, conv_w, gamma, beta, run_mean, run_var):
        import jax, jax.numpy as jnp
        import numpy as np
        EPS = 1e-05

        def _message_pass(inputs, conv_w, gamma, beta, run_mean, run_var):
            scale = gamma / jnp.sqrt(run_var + EPS)
            shift = beta - run_mean * scale

            def f(s):
                y = jax.lax.conv_general_dilated(s, conv_w, window_strides=(1,), padding=[(4, 4)], dimension_numbers=('NCW', 'OIW', 'NCW'))
                return jax.nn.relu(y * scale[None, :, None] + shift[None, :, None])

            def step(carry, old_slice):
                new = f(carry) + old_slice
                return (new, new)
            xs = jnp.moveaxis(inputs, 2, 0)
            _, ys = jax.lax.scan(step, xs[0], xs[1:])
            new = jnp.concatenate([xs[:1], ys], axis=0)
            _, ys2 = jax.lax.scan(step, new[-1], new[:-1], reverse=True)
            out = jnp.concatenate([ys2, new[-1:]], axis=0)
            return jnp.moveaxis(out, 0, 2)
        return _message_pass(inputs, conv_w, gamma, beta, run_mean, run_var)

    def _L2_conv_ref(x, weight, bias):
        import jax, jax.numpy as jnp
        import numpy as np
        PAD = 1
        N, C, H, W = x.shape
        F, _, HH, WW = weight.shape
        pad = PAD
        out_H = H - HH + 1 + 2 * pad
        out_W = W - WW + 1 + 2 * pad
        HHH = max(out_H, HH)
        WWW = max(out_W, WW)
        init_H = H + 2 * pad + HHH - 1
        init_W = W + 2 * pad + WWW - 1
        xp = jnp.pad(x, ((0, 0), (0, 0), (pad, init_H - pad - H), (pad, init_W - pad - W)))
        wp = jnp.pad(weight, ((0, 0), (0, 0), (0, init_H - HH), (0, init_W - WW)))
        xf = jnp.fft.rfft2(xp)
        wf = jnp.fft.rfft2(wp)
        of = jnp.einsum('nchw,fchw->nfhw', xf, jnp.conj(wf))
        out = jnp.fft.irfft2(of, s=(init_H, init_W))[..., :out_H, :out_W]
        return out + bias[None, :, None, None]

    def _L3_conv_ref(feat_l, feat_s, w_atten, w_fsm, w_off, w_cm, b_cm, w_dcn, b_dcn):
        import jax, jax.numpy as jnp
        import numpy as np
        DG = 8
        K = 9

        def _conv3x3(x, w, b):
            y = jax.lax.conv_general_dilated(x, w, (1, 1), ((1, 1), (1, 1)), dimension_numbers=('NCHW', 'OIHW', 'NCHW'))
            return y + b[None, :, None, None]

        def _deform_conv_v2(x, off_y, off_x, mask, w, b):
            B, C, H, W = x.shape
            cpg = C // DG
            k = jnp.arange(K)
            ky = (k // 3 - 1).astype(x.dtype)[None, None, :, None, None]
            kx = (k % 3 - 1).astype(x.dtype)[None, None, :, None, None]
            hh = jnp.arange(H, dtype=x.dtype)[None, None, None, :, None]
            ww = jnp.arange(W, dtype=x.dtype)[None, None, None, None, :]
            py = hh + ky + off_y
            px = ww + kx + off_x
            y0 = jnp.floor(py)
            x0 = jnp.floor(px)
            ly = py - y0
            lx = px - x0
            xf = x.reshape(B, DG, cpg, H * W)

            def corner(yi, xi):
                valid = ((yi >= 0) & (yi < H) & (xi >= 0) & (xi < W)).astype(x.dtype)
                idx = (jnp.clip(yi, 0, H - 1) * W + jnp.clip(xi, 0, W - 1)).astype(jnp.int32)
                idxb = jnp.broadcast_to(idx.reshape(B, DG, 1, K * H * W), (B, DG, cpg, K * H * W))
                v = jnp.take_along_axis(xf, idxb, axis=3).reshape(B, DG, cpg, K, H, W)
                return (v, valid)
            v00, m00 = corner(y0, x0)
            v01, m01 = corner(y0, x0 + 1)
            v10, m10 = corner(y0 + 1, x0)
            v11, m11 = corner(y0 + 1, x0 + 1)
            w00 = ((1 - ly) * (1 - lx) * m00)[:, :, None]
            w01 = ((1 - ly) * lx * m01)[:, :, None]
            w10 = (ly * (1 - lx) * m10)[:, :, None]
            w11 = (ly * lx * m11)[:, :, None]
            val = (v00 * w00 + v01 * w01 + v10 * w10 + v11 * w11) * mask[:, :, None]
            wr = w.reshape(w.shape[0], DG, cpg, K)
            return jnp.einsum('bgckhw,ogck->bohw', val, wr) + b[None, :, None, None]
        B, C, H, W = feat_l.shape
        feat_up = jax.image.resize(feat_s, (B, feat_s.shape[1], H, W), method='bilinear')
        gap = feat_l.mean(axis=(2, 3))
        atten = jax.nn.sigmoid(gap @ w_atten.T)[:, :, None, None]
        xg = feat_l * (1.0 + atten)
        feat_arm = jnp.einsum('bchw,oc->bohw', xg, w_fsm)
        cat = jnp.concatenate([feat_arm, feat_up * 2.0], axis=1)
        off_feat = jnp.einsum('bchw,oc->bohw', cat, w_off)
        om = _conv3x3(off_feat, w_cm, b_cm)
        n = DG * K
        off_y = om[:, :n].reshape(B, DG, K, H, W)
        off_x = om[:, n:2 * n].reshape(B, DG, K, H, W)
        mask = jax.nn.sigmoid(om[:, 2 * n:]).reshape(B, DG, K, H, W)
        out = _deform_conv_v2(feat_up, off_y, off_x, mask, w_dcn, b_dcn)
        return jax.nn.relu(out) + feat_arm

    def _gn(v, G=32, eps=1e-5):
        B_, C_, H_, W_ = v.shape
        g = v.reshape(B_, G, C_ // G, H_, W_)
        m = jnp.mean(g, axis=(2, 3, 4), keepdims=True)
        s = jnp.var(g, axis=(2, 3, 4), keepdims=True)
        return ((g - m) / jnp.sqrt(s + eps)).reshape(v.shape)

    def _ln_c(v, eps=1e-6):
        m = jnp.mean(v, axis=1, keepdims=True)
        s = jnp.var(v, axis=1, keepdims=True)
        return (v - m) / jnp.sqrt(s + eps)

    def _ln_t(v, eps=1e-5):
        m = jnp.mean(v, axis=-1, keepdims=True)
        s = jnp.var(v, axis=-1, keepdims=True)
        return (v - m) / jnp.sqrt(s + eps)

    def _to_tokens(v):
        B_, C_, H_, W_ = v.shape
        return v.reshape(B_, C_, H_ * W_).transpose(0, 2, 1)
    def _from_tokens(t, like):
        B_, C_, H_, W_ = like.shape
        return t.transpose(0, 2, 1).reshape(B_, C_, H_, W_)

    x = x + _L0_conv_ref(_gn(x), L0_conv_qkv_w, L0_conv_qkv_b, L0_conv_proj_w, L0_conv_proj_b)
    x = x + _L1_conv_ref(_gn(x), L1_conv_conv_w, L1_conv_gamma, L1_conv_beta, L1_conv_run_mean, L1_conv_run_var)
    x = x + _L2_conv_ref(_gn(x), L2_conv_weight, L2_conv_bias)
    x = x + _L3_conv_ref(_gn(x), L3_conv_feat_s, L3_conv_w_atten, L3_conv_w_fsm, L3_conv_w_off, L3_conv_w_cm, L3_conv_b_cm, L3_conv_w_dcn, L3_conv_b_dcn)
    return x


_drawn_inputs = setup_inputs


def setup_inputs(seed=0):
    import zlib

    import numpy as np

    out = dict(_drawn_inputs(seed))
    spreads = {'L3_conv_b_cm': (0.0, 0.8)}
    factors = {'L2_conv_bias': 4.087,
     'L3_conv_feat_s': 3.209,
     'L3_conv_w_off': 8.0,
     'L3_conv_w_cm': 8.0,
     'L3_conv_w_dcn': 3.205,
     'L3_conv_b_dcn': 33.032}
    for name, (base, spread) in spreads.items():
        noise = np.random.default_rng([zlib.crc32(name.encode()), seed]).standard_normal(out[name].shape)
        drawn = base * np.exp(spread * noise) if base else spread * noise
        out[name] = jnp.asarray(drawn.astype(out[name].dtype))
    for name, factor in factors.items():
        out[name] = (out[name] * factor).astype(out[name].dtype)
    return out
```

```python
from contextlib import ExitStack

import numpy as np

import concourse.bass as bass
from concourse import mybir

ALU = mybir.AluOpType
ACT = mybir.ActivationFunctionType
AX = mybir.AxisListType
F32 = mybir.dt.float32
BF16 = mybir.dt.bfloat16

C, H, W = 128, 96, 96
PIX = H * W
PW = W + 2
ROWS = 4
STEPS = H // ROWS
HEADS, HD, KS = 8, 16, 8
SUB = 48
QR, QC = 4, 8
TR, TC = SUB // QR, SUB // QC
KR, KC = QR + KS, QC + KS - 1
KEYS = KR * KC
KHALF = KEYS // 2
PADK = 4
KPH, KPW = PADK + SUB + 4, 3 + SUB + 4
FAR = -float(2 ** 99)
RP = W + 8
FH = 32
WA, WB = 12, 10
NA, NB = 3, 4
WINS = NA * NB
WK = WA * WB
FPH, FPW = (NA - 1) * (WA - 1) + WA, (NB - 1) * (WB - 1) + WB
DG, TAPS = 8, 9
SAMP = DG * TAPS
TILES = PIX // 128
CH = 6
CHUNKS = SAMP // CH
CPG = C // DG
EPS = 1e-5


def attention_masks():
    row = np.full((C, TR, KR), 0.0, np.float32)
    col = np.full((C, TC, KC), 0.0, np.float32)
    for t in range(TR):
        for a in range(QR):
            start = min(max(QR * t + a - 3, 0), SUB - KS)
            for r in range(KR):
                if not start <= QR * t - PADK + r < start + KS:
                    row[a, t, r] = FAR
    for t in range(TC):
        for a in range(QC):
            start = min(max(QC * t + a - 3, 0), SUB - KS)
            for r in range(KC):
                if not start <= QC * t - 3 + r < start + KS:
                    col[a, t, r] = FAR
    q = np.arange(128)
    inrow = np.zeros((C, 128), np.float32)
    incol = np.zeros((C, 128), np.float32)
    inrow[(q // 16) // 2, q] = 1.0
    incol[(q % 16) // 2, q] = 1.0
    return row, col, inrow, incol


def shape_constants():
    p = np.arange(C)
    out = {}
    out["ident"] = np.eye(C, dtype=np.float32)
    out["gmean"] = (p[:, None] // 4 == p[None, :] // 4).astype(np.float32) / 4
    o = np.arange(3 * C)
    out["own3"] = (o[None, :] // 3 == p[:, None]).astype(np.float32)
    out["headq"] = (p[:, None] // HD == np.arange(HEADS)[None, :]).astype(np.float32) * HD ** -0.5
    row, col, inrow, incol = attention_masks()
    out["mrow"], out["mcol"] = row.reshape(C, -1), col.reshape(C, -1)
    out["inrow"], out["incol"] = inrow, incol
    lin = 128 * np.arange(3)[None, :, None] + p[:, None, None]
    k = (np.arange(SAMP) % TAPS)[None, None, :]
    out["basey"] = (lin // W + k // 3 - 1).astype(np.float32).reshape(C, -1)
    out["basex"] = (lin % W + k % 3 - 1).astype(np.float32).reshape(C, -1)
    out["iota"] = np.tile(np.arange(12, dtype=np.float32)[None, :], (C, 1))
    return out


CONSTS = ["ident", "gmean", "own3", "headq", "mrow", "mcol", "inrow", "incol", "basey", "basex", "iota"]
CWIDTH = dict(ident=C, gmean=C, own3=3 * C, headq=HEADS, mrow=TR * KR, mcol=TC * KC, inrow=C, incol=C,
              basey=3 * SAMP, basex=3 * SAMP, iota=12)
BATCHW = [1 - abs(i - 3.5) / 8 for i in range(8)]
BATCHW = [w / sum(BATCHW) for w in BATCHW]


def build_program(nc, d, consts, out):
    with ExitStack() as ctx:
        def sb(name, shape, dt=F32):
            return ctx.enter_context(nc.sbuf_tensor(name, shape, dt))

        def sem(name):
            return ctx.enter_context(nc.semaphore(name))

        X = sb("X", [C, PIX])
        pad = sb("pad", [C, H * RP])
        work = sb("work", [C, 22000])
        w1T = sb("w1T", [C, TAPS, C])
        w2T = sb("w2T", [C, TAPS, C])
        wcmT = sb("wcmT", [C, TAPS, 3 * SAMP])
        wdT = sb("wdT", [C, TAPS, C])
        sqT = sb("sqT", [C, 5, C])
        Fwin = sb("Fwin", [WK, DG, WINS, CPG])
        cst = sb("cst", [C, sum(CWIDTH.values())])
        vec = sb("vec", [C, 12])
        mrow16 = sb("mrow16", [C, TR, KR], BF16)
        mcol16 = sb("mcol16", [C, TC, KC], BF16)
        inrow16 = sb("inrow16", [C, C], BF16)
        incol16 = sb("incol16", [C, C], BF16)
        tiny = sb("tiny", [C, 64])
        stats = sb("stats", [C, 18, 6])
        shiftd = sb("shiftd", [C, C])
        ones = sb("ones", [C, W])
        ps = ctx.enter_context(nc.psum_tensor("ps", [C, 8, 512], F32))

        off = 0
        con = {}
        for name in CONSTS:
            con[name] = cst[:, off:off + CWIDTH[name]]
            off += CWIDTH[name]
        ident = con["ident"]

        Xr = X[:].rearrange("p (h w) -> p h w", w=W)
        padm = pad[:, 0:(H + 2) * PW].rearrange("p (h w) -> p h w", w=PW)
        rows = pad[:].rearrange("p (h w) -> p h w", w=RP)

        raw = {}
        at = 0
        for name, n in (("w1", 1152), ("w2", 1152), ("wd", 1152), ("cma", 1152), ("cmb", 1152), ("fsm", C),
                        ("att", C), ("off", 2 * C), ("proj", C), ("qkv", 3 * C * 9)):
            raw[name] = pad[:, at:at + n]
            at += n
        Q = work[:, 0:PIX]
        Qr = Q.rearrange("p (h w) -> p h w", w=W)
        kP = work[:, PIX:PIX + KPH * KPW].rearrange("p (h w) -> p h w", w=KPW)
        o2 = PIX + KPH * KPW
        vP = work[:, o2:o2 + KPH * KPW].rearrange("p (h w) -> p h w", w=KPW)
        o3 = o2 + KPH * KPW
        qkvT = work[:, o3:o3 + 9 * 3 * C].rearrange("p (t o) -> p t o", t=9)
        fs = work[:, 0:8 * FH * FH].rearrange("p (b n) -> p b n", b=8)
        Fpad = work[:, 8192:8192 + FPH * FPW].rearrange("p (h w) -> p h w", w=FPW)
        wdr = work[:, 9600:9600 + 1152]
        Fcut = work[:, 10752:10752 + WINS * WK].rearrange("p (w k) -> p w k", w=WINS)
        Fmap = sb("Fmap", [C, FH * FH])
        ao = [0]

        def carve(n, base=pad):
            v = base[:, ao[0]:ao[0] + n]
            ao[0] += n
            return v
        Qm = [carve(HEADS * 128).rearrange("p (h q) -> p h q", h=HEADS) for _ in range(2)]
        vw = [carve(KEYS) for _ in range(2)]
        Sx = [carve(HEADS * KEYS).rearrange("p (h k) -> p h k", h=HEADS) for _ in range(2)]
        PT = [carve(512) for _ in range(4)]
        vT = [carve(2 * HEADS * 17).rearrange("p (c h d) -> p c h d", c=2, h=HEADS) for _ in range(2)]
        On = carve(128)
        OT = carve(128)
        smax = carve(HEADS)
        srec = carve(HEADS)
        assert ao[0] <= H * RP
        yr = work[:, 0:H * FH].rearrange("p (h w) -> p h w", w=FH)
        ys = work[:, 3072:3072 + FH * FH].rearrange("p (h w) -> p h w", w=FH)
        yd = work[:, 4096:4096 + FH * FH].rearrange("p (h w) -> p h w", w=FH)
        cd = work[:, 5120:5120 + H * FH].rearrange("p (h w) -> p h w", w=FH)
        xg = [work[:, 8192 + 384 * i:8192 + 384 * (i + 1)] for i in range(2)]
        fa = [work[:, 8960 + 384 * i:8960 + 384 * (i + 1)] for i in range(2)]
        NS = TILES * SAMP
        UL, VL, MS, WI = (work[:, i * NS:(i + 1) * NS] for i in range(4))
        flat1 = w1T[:].rearrange("p a b -> p (a b)")
        flat2 = w2T[:].rearrange("p a b -> p (a b)")
        oms = [flat1[:, 384 * i:384 * (i + 1)] for i in range(2)]
        yx = flat2[:, 0:432].rearrange("p (a n) -> p a n", a=2)
        ee = flat2[:, 432:864].rearrange("p (a n) -> p a n", a=2)
        wia = flat2[:, 864:1080]
        sg = flat1[:, 768:984]
        wja = work[:, 4 * NS:4 * NS + 216]
        uv = work[:, 4 * NS + 216:4 * NS + 648].rearrange("p (a n) -> p a n", a=2)
        ma = work[:, 4 * NS + 648:4 * NS + 864]
        ao[0] = 0
        DA = carve(SAMP * WA)
        HA = [carve(SAMP * WA) for _ in range(2)]
        HB = [carve(SAMP * WB) for _ in range(2)]
        OH = carve(SAMP * WINS)
        PR = [carve(CH * WK) for _ in range(2)]
        PTS = [carve(384) for _ in range(4)]
        val0 = carve(SAMP * CPG)
        mst = carve(SAMP)
        orelu = carve(128)
        assert ao[0] <= H * RP
        val = [val0, work[:, 4 * NS:4 * NS + SAMP * CPG]]
        valT = flat1
        GM = flat2

        names = """x_in w_in c_in zeroed gn_stats gn_mean gn_var gn_sd gn_apply gn_dve_apply l1c_var l1c_sd
        raw_done wt_ps wt_ev wprep fmean l1diag
        cv_ps cv_ev kv_ps kv_ev
        qm_ready s_ready vt_ps vt_ev s_sub p_ready pt_ps pt_act pt_dve o_ready o_norm ot_ps ot_ev pj_ps l0_x
        row_ps row_new
        c2_ps c2_x gap_in att_ps att_sg gn_scale y_ps y_ev y_up xg_ready fa_ps fa_ev of_ps of_ev fx
        om_ps om_ev omt_ps omt_xy om_sig om_abs coord
        pr_ready t_ps t_ev g_ready g_used val_ready d_ready d_hat ha_ready x_out stored""".split()
        S = {n: sem(n) for n in names}
        block = ctx.enter_context(nc.Block())

        def weight_jobs():
            jobs = []
            for src, dst in (("w1", w1T), ("w2", w2T)):
                v = raw[src].rearrange("p (c t) -> p c t", t=9)
                for j in range(3):
                    jobs.append(([(v[:, :, 3 * j + i], 128 * i) for i in range(3)],
                                 dst[:, 3 * j:3 * j + 3, :].rearrange("p a b -> p (a b)"), C, 384))
            for j in range(3):
                jobs.append(([(wdr[:, 128 * (3 * j + i):128 * (3 * j + i + 1)], 128 * i) for i in range(3)],
                             wdT[:, 3 * j:3 * j + 3, :].rearrange("p a b -> p (a b)"), C, 384))
            va = raw["cma"].rearrange("p (c t) -> p c t", t=9)
            vb = raw["cmb"].rearrange("p (c t) -> p c t", t=9)
            for j in range(5):
                ts = [t for t in (2 * j, 2 * j + 1) if t < 9]
                src = []
                for n, t in enumerate(ts):
                    src += [(va[:, :, t], 216 * n), (vb[0:88, :, t], 216 * n + 128)]
                jobs.append((src, wcmT[:, ts[0]:ts[-1] + 1, :].rearrange("p a b -> p (a b)"), C, 216 * len(ts)))
            ro = raw["off"]
            jobs.append(([(raw["proj"], 0), (raw["fsm"], 128), (raw["att"], 256)],
                         sqT[:, 0:3, :].rearrange("p a b -> p (a b)"), C, 384))
            jobs.append(([(ro[:, 0:C], 0), (ro[:, C:2 * C], 128)],
                         sqT[:, 3:5, :].rearrange("p a b -> p (a b)"), C, 256))
            for j in range(3):
                src = []
                for i in range(4):
                    w = 4 * j + i
                    src.append((Fcut[:, w, :], 128 * i))
                jobs.append((src, Fwin[:, :, 4 * j:4 * j + 4, :].rearrange("p g w c -> p w g c"), WK, 512))
            return jobs
        JOBS = weight_jobs()

        def first_job(t):
            return 0 if isinstance(t, int) and t == 0 else t * 28 - 4

        def chunk_job(c, first):
            return 2 * c + (0 if first else 3 * (c > 3) + (c > 4))

        @block.sync
        def _(sp):
            for h in range(4):
                sp.dma_start(X[:, 2304 * h:2304 * (h + 1)],
                             d["x"].rearrange("a c h w -> (a c) (h w)")[:, 2304 * h:2304 * (h + 1)]
                             ).then_inc(S["x_in"], 16)
            sp.dma_start(cst[:], consts).then_inc(S["c_in"], 16)
            sp.dma_start(fs, d["L3_conv_feat_s"].rearrange("b c h w -> c b (h w)")).then_inc(S["w_in"], 16)
            sp.dma_start(raw["qkv"], d["L0_conv_qkv_w"].rearrange("o a b c -> (o a b c)").partition_broadcast(C)
                         ).then_inc(S["w_in"], 16)
            sp.dma_start(raw["w1"], d["L1_conv_conv_w"].rearrange("o c t -> o (c t)")).then_inc(S["w_in"], 16)
            sp.dma_start(raw["w2"], d["L2_conv_weight"].rearrange("o c a b -> o (c a b)")).then_inc(S["w_in"], 16)
            sp.dma_start(raw["wd"], d["L3_conv_w_dcn"].rearrange("o c a b -> o (c a b)")).then_inc(S["w_in"], 16)
            cm = d["L3_conv_w_cm"].rearrange("o c a b -> o (c a b)")
            sp.dma_start(raw["cma"], cm[0:C, :]).then_inc(S["w_in"], 16)
            sp.dma_start(raw["cmb"][0:88, :], cm[C:216, :]).then_inc(S["w_in"], 16)
            sp.dma_start(raw["fsm"], d["L3_conv_w_fsm"]).then_inc(S["w_in"], 16)
            sp.dma_start(raw["att"], d["L3_conv_w_atten"]).then_inc(S["w_in"], 16)
            sp.dma_start(raw["off"], d["L3_conv_w_off"]).then_inc(S["w_in"], 16)
            sp.dma_start(raw["proj"], d["L0_conv_proj_w"].rearrange("o c a b -> o (c a b)")).then_inc(S["w_in"], 16)
            sp.dma_start(vec[:, 0:3], d["L0_conv_qkv_b"].rearrange("(t c) -> c t", t=3),
                         allow_slow_non_contiguous=True).then_inc(S["w_in"], 16)
            for i, n in enumerate(("L0_conv_proj_b", "L1_conv_gamma", "L1_conv_beta", "L1_conv_run_mean",
                                   "L1_conv_run_var", "L2_conv_bias", "L3_conv_b_dcn")):
                sp.dma_start(vec[:, 3 + i:4 + i], d[n].rearrange("(c a) -> c a", a=1)).then_inc(S["w_in"], 16)
            bcm = d["L3_conv_b_cm"].rearrange("(a c) -> c a", a=2)
            sp.dma_start(vec[0:108, 10:12], bcm, allow_slow_non_contiguous=True).then_inc(S["w_in"], 16)
            sp.wait_ge(S["x_out"], TILES)
            o = out.rearrange("a c h w -> (a c) (h w)")
            sp.dma_start(o, X[:]).then_inc(S["stored"], 16)
            sp.wait_ge(S["stored"], 16)
        W_IN = 16 * 20
        qb, kb, vb_ = vec[:, 0:1], vec[:, 1:2], vec[:, 2:3]
        pjb, gam, bet, rmean, rvar = (vec[:, i:i + 1] for i in range(3, 8))
        b2, bdc = vec[:, 8:9], vec[:, 9:10]
        T = lambda i, n=1: tiny[:, i:i + n]
        mv, t2, gm, nv, var, sd, rstd, nb = T(0, 2), T(2, 2), T(4, 2), T(6), T(7), T(8), T(9), T(10)
        s3, b3, gapn, att, att1 = T(11), T(12), T(13), T(14), T(15)
        lv, lsd, lrs, lsc, lsh = T(16), T(17), T(18), T(19), T(20)
        DVE_ROWS = 60

        @block.gpsimd
        def _(g):
            g.wait_ge(S["raw_done"], 1)
            nc.gpsimd.memset(kP, 0.0)
            nc.gpsimd.memset(vP, 0.0).then_inc(S["zeroed"], 1)
            g.wait_ge(S["kv_ev"], 12)
            g.wait_ge(S["cv_ev"], STEPS)
            with g.Fori(0, TR) as tr:
                for tc in range(TC):
                    par = tc % 2
                    n = tr * TC + tc
                    g.drain()
                    g.wait_ge(S["vt_ps"], n - 1 if tc >= 2 else tr * TC)
                    nc.gpsimd.tensor_tensor(T(40), T(41), T(41), ALU.mult)
                    nc.gpsimd.tensor_copy(
                        vw[par].rearrange("p (a b) -> p a b", b=KC),
                        vP[:, bass.ds(tr * QR, KR), bass.ds(QC * tc, KC)])
                    nc.gpsimd.tensor_tensor(
                        Qm[par].rearrange("p h (a b) -> p h a b", b=16),
                        Qr[:, bass.ds(tr * (2 * QR), 8), 16 * tc:16 * tc + 16].unsqueeze(1)
                        .broadcast_to([C, HEADS, 8, 16]),
                        con["headq"].unsqueeze(2).unsqueeze(3).broadcast_to([C, HEADS, 8, 16]),
                        ALU.mult).then_inc(S["qm_ready"], 1)
            g.wait_ge(S["coord"], STEPS)

            def offsets_of(t, par):
                g.drain()
                u = UL[:, bass.ts(t, SAMP)].unsqueeze(2).broadcast_to([C, SAMP, WA])
                v = VL[:, bass.ts(t, SAMP)].unsqueeze(2).broadcast_to([C, SAMP, WB])
                nc.gpsimd.tensor_tensor(DA.rearrange("p (s a) -> p s a", a=WA), u,
                                        con["iota"].unsqueeze(1).broadcast_to([C, SAMP, WA]), ALU.subtract)
                nc.gpsimd.tensor_copy(mst, MS[:, bass.ts(t, SAMP)])
                nc.gpsimd.tensor_tensor(HB[par].rearrange("p (s a) -> p s a", a=WB), v,
                                        con["iota"][:, 0:WB].unsqueeze(1).broadcast_to([C, SAMP, WB]),
                                        ALU.subtract).then_inc(S["d_ready"], 1)

            def masked_hat(t, par):
                g.wait_ge(S["d_hat"], t + 1)
                nc.gpsimd.tensor_tensor(HA[par].rearrange("p (s a) -> p s a", a=WA),
                                        DA.rearrange("p (s a) -> p s a", a=WA),
                                        mst.unsqueeze(2).broadcast_to([C, SAMP, WA]), ALU.mult)

            def tile(t, par, first=False, last=False):
                job = first_job(t)
                a3 = HA[par].rearrange("p (s a) -> p s a", a=WA)
                b3_ = HB[par].rearrange("p (s a) -> p s a", a=WB)
                g.drain()
                for c in range(CHUNKS):
                    if c >= 2:
                        g.wait_ge(S["t_ps"], job + (chunk_job(c - 2, first) + 2))
                    elif not first:
                        g.wait_ge(S["t_ps"], job - (2 - 2 * c))
                    sl = slice(CH * c, CH * c + CH)
                    nc.gpsimd.tensor_tensor(
                        PR[c % 2].rearrange("p (s a b) -> p s a b", a=WA, b=WB),
                        a3[:, sl, :].unsqueeze(3).broadcast_to([C, CH, WA, WB]),
                        b3_[:, sl, :].unsqueeze(2).broadcast_to([C, CH, WA, WB]),
                        ALU.mult).then_inc(S["pr_ready"], 1)
                    if c == 4 and not last:
                        offsets_of(t + 1, 1 - par)
                    if c == 8 and not last:
                        masked_hat(t + 1, 1 - par)
            offsets_of(0, 0)
            masked_hat(0, 0)
            tile(0, 0, first=True)
            with g.Fori(0, (TILES - 2) // 2) as pair:
                t = pair * 2 + 1
                tile(t, 1)
                tile(t + 1, 0)
            tile(TILES - 1, 1, last=True)

        @block.scalar
        def _(act):
            def gn_root(n):
                act.wait_ge(S["gn_var"], n + 1)
                nc.scalar.activation(sd, var, ACT.Sqrt).then_inc(S["gn_sd"], 1)

            def gn_apply(n, dst):
                act.wait_ge(S["gn_scale"], n + 1)
                nc.scalar.activation(dst[:, DVE_ROWS:H, :], Xr[:, DVE_ROWS:H, :], ACT.Identity, scale=rstd,
                                     bias=nb).then_inc(S["gn_apply"], 1)
            act.wait_ge(S["l1c_var"], 1)
            nc.scalar.activation(lsd, lv, ACT.Sqrt).then_inc(S["l1c_sd"], 1)
            for n, (src, dst, m, width) in enumerate(JOBS):
                act.wait_ge(S["wt_ps"], n + 1)
                if width == 512:
                    sv = ps[0:m, n % 4, 0:512].rearrange("p (w g c) -> p w g c", w=4, g=DG)
                    for w in range(4):
                        i = nc.scalar.activation(dst[:, w], sv[:, w], ACT.Copy)
                    i.then_inc(S["wt_ev"], 1)
                else:
                    nc.scalar.activation(dst, ps[0:m, n % 4, 0:width], ACT.Copy).then_inc(S["wt_ev"], 1)
            gn_root(0)
            act.wait_ge(S["raw_done"], 1)
            gn_apply(0, padm[:, 1:H + 1, 1:W + 1])
            act.wait_ge(S["zeroed"], 1)
            for n in range(12):
                i, kv = n // 2, n % 2
                act.wait_ge(S["kv_ps"], n + 1)
                nc.scalar.activation((kP, vP)[kv][:, PADK + 8 * i:PADK + 8 * i + 8, 3:3 + SUB],
                                     ps[:, 4 + n % 4, 0:384].rearrange("p (a b) -> p a b", b=SUB),
                                     ACT.Identity, bias=(kb, vb_)[kv]).then_inc(S["kv_ev"], 1)
            with act.Fori(0, TR) as tr:
                for tc in range(TC + 2):
                    n = tr * TC + tc
                    if tc < TC:
                        par = tc % 2
                        act.wait_ge(S["vt_ps"], n + 1)
                        nc.scalar.activation(
                            vT[par][0:KHALF, :, :, 0:HD],
                            ps[0:KHALF, 6, 0:256].rearrange("p (c h d) -> p c h d", c=2, h=HEADS),
                            ACT.Copy).then_inc(S["vt_ev"], 1)
                    if tc >= 2:
                        act.wait_ge(S["ot_ps"], n - 1)
                        nc.scalar.activation(OT, ps[:, 7, 0:128], ACT.Copy).then_inc(S["ot_ev"], 1)
                    if tc < TC:
                        act.wait_ge(S["s_sub"], n + 1)
                        nc.scalar.activation(Sx[par].rearrange("p h k -> p (h k)"),
                                             Sx[par].rearrange("p h k -> p (h k)"),
                                             ACT.Exp).then_inc(S["p_ready"], 1)
                    if 1 <= tc <= TC:
                        for j in (0, 2):
                            act.wait_ge(S["pt_ps"], (n - 1) * 4 + j + 1)
                            nc.scalar.activation(PT[j][0:KHALF, :], ps[0:KHALF, 4, 0:512],
                                                 ACT.Copy).then_inc(S["pt_act"], 1)
            gn_root(1)
            gn_apply(1, rows[:, :, 4:4 + W])
            gn_root(2)
            gn_apply(2, padm[:, 1:H + 1, 1:W + 1])
            gn_root(3)
            act.wait_ge(S["att_ps"], 1)
            nc.scalar.activation(att, ps[:, 7, 0:1], ACT.Sigmoid).then_inc(S["att_sg"], 1)
            act.wait_ge(S["y_ps"], 1)
            for hh in range(2):
                i = nc.scalar.activation(ys[:, 16 * hh:16 * hh + 16, :].rearrange("p a b -> p (a b)"),
                                         ps[:, 5 + hh, :], ACT.Copy, scale=2.0)
            i.then_inc(S["y_ev"], 1)
            with act.Fori(0, STEPS // 2) as r:
                for i in range(2):
                    n = r * 2 + i
                    act.wait_ge(S["fx"], r * 2)
                    act.wait_ge(S["fa_ps"], n + 1)
                    nc.scalar.activation(fa[i], ps[:, i, 0:384], ACT.Copy).then_inc(S["fa_ev"], 1)
            with act.Fori(0, STEPS) as r:
                act.wait_ge(S["om_ps"], r + 1)
                for hf in range(2):
                    i = nc.scalar.activation(oms[hf][0:108, :], ps[0:108, hf, 0:384], ACT.Identity,
                                             bias=vec[0:108, 10 + hf:11 + hf])
                i.then_inc(S["om_ev"], 1)
                act.wait_ge(S["coord"], r)
                act.wait_ge(S["omt_xy"], r + 1)
                for hf in range(3):
                    i = nc.scalar.activation(sg[:, SAMP * hf:SAMP * hf + SAMP],
                                             ps[:, 2 + hf // 2, 256 * (hf % 2) + 144:256 * (hf % 2) + 216],
                                             ACT.Sigmoid)
                i.then_inc(S["om_sig"], 1)
                nc.scalar.activation(ee, ee, ACT.Abs).then_inc(S["om_abs"], 1)

            def hats(t, par):
                act.wait_ge(S["d_ready"], t + 1)
                nc.scalar.activation(DA, DA, ACT.Abs)
                nc.scalar.activation(HB[par], HB[par], ACT.Abs)
                act.drain()
                nc.scalar.activation(HB[par], HB[par], ACT.Relu, scale=-1.0, bias=1.0)
                nc.scalar.activation(DA, DA, ACT.Relu, scale=-1.0, bias=1.0).then_inc(S["d_hat"], 1)

            def evac(job, dst, src):
                act.wait_ge(S["t_ps"], job + 1)
                nc.scalar.activation(dst, src, ACT.Copy).then_inc(S["t_ev"], 1)

            def value_jobs(job):
                for j in range(3):
                    evac(job + j, valT[:, 384 * j:384 * (j + 1)], ps[:, 6 + j % 2, 0:384])

            def out_job(t, job, bank):
                if not (isinstance(t, int) and t == 0):
                    act.wait_ge(S["x_out"], t)
                act.wait_ge(S["t_ps"], job + 1)
                nc.scalar.activation(orelu, ps[:, bank, 0:128], ACT.Relu, bias=bdc).then_inc(S["t_ev"], 1)

            def tile(t, par, first=False, last=False):
                job = first_job(t)
                k = 0
                for c in range(CHUNKS):
                    if not (first and c < 2):
                        act.wait_ge(S["g_ready"], t * CHUNKS + c - 1)
                    for j in range(2):
                        evac(job + k, PTS[(2 * c + j) % 4][0:WK, :], ps[0:WK, 6 + k % 2, 0:384])
                        k += 1
                    if c == 3 and not first:
                        for j in range(3):
                            evac(job + k, valT[:, 384 * j:384 * (j + 1)], ps[:, 6 + k % 2, 0:384])
                            k += 1
                    if c == 4 and not first:
                        out_job(t - 1, job + k, 6 + k % 2)
                        k += 1
                    if c == 5 and not last:
                        hats(t + 1, 1 - par)
            hats(0, 0)
            tile(0, 0, first=True)
            with act.Fori(0, (TILES - 2) // 2) as pair:
                t = pair * 2 + 1
                tile(t, 1)
                tile(t + 1, 0)
            tile(TILES - 1, 1, last=True)
            job = TILES * 28 - 4
            value_jobs(job)
            out_job(TILES - 1, job + 3, 7)

        @block.tensor
        def _(pe):
            mm = nc.tensor.matmul

            def gn_mean(n):
                pe.wait_ge(S["gn_stats"], n + 1)
                mm(ps[:, 7, 0:2], con["gmean"], t2, start=True, stop=True).then_inc(S["gn_mean"], 1)
            pe.wait_ge(S["c_in"], 16)
            pe.wait_ge(S["w_in"], W_IN)
            pe.wait_ge(S["wprep"], 1)
            for n, (src, dst, m, width) in enumerate(JOBS):
                if n >= 4:
                    pe.wait_ge(S["wt_ev"], n - 3)
                for s, col in src:
                    k = s.shape[0]
                    i = nc.tensor.transpose(ps[0:m, n % 4, col:col + k], s, ident[0:k, 0:k])
                i.then_inc(S["wt_ps"], 1)
            gn_mean(0)
            pe.wait_ge(S["gn_apply"], 1)
            pe.wait_ge(S["gn_dve_apply"], 1)
            with pe.Fori(0, STEPS // 4) as r:
                for i in range(4):
                    pe.wait_ge(S["cv_ev"], r * 4)
                    for t in range(9):
                        m = mm(ps[:, i, 0:384], qkvT[:, t, 0:C],
                               padm[:, bass.ds(r * 16 + (4 * i + t // 3), ROWS), t % 3:t % 3 + W],
                               start=(t == 0), stop=(t == 8))
                    m.then_inc(S["cv_ps"], 1)
            for n in range(12):
                i, kv = n // 2, n % 2
                if n >= 4:
                    pe.wait_ge(S["kv_ev"], n - 3)
                for t in range(9):
                    a, b = 16 * i + t // 3, t % 3
                    m = mm(ps[:, 4 + n % 4, 0:384], qkvT[:, t, C * (1 + kv):C * (2 + kv)],
                           padm[:, a:a + 15:2, b:b + 95:2], start=(t == 0), stop=(t == 8))
                m.then_inc(S["kv_ps"], 1)

            def scores(tr, tc):
                n = tr * TC + tc
                par = tc % 2
                pe.wait_ge(S["vt_ev"], n)
                pe.wait_ge(S["qm_ready"], n + 1)
                pe.wait_ge(S["s_sub"], n)
                for h in range(HEADS):
                    o = ps[:, h // 2, 256 * (h % 2):256 * (h % 2) + KEYS]
                    mm(o, Qm[par][:, h, :], kP[:, bass.ds(tr * QR, KR), QC * tc:QC * tc + KC],
                       start=True, stop=False)
                    mm(o, inrow16[:], mrow16[:, bass.ds(tr, 1), :].rearrange("p a k -> p (a k)").unsqueeze(2)
                       .broadcast_to([C, KR, KC]), start=False, stop=False)
                    i = mm(o, incol16[:], mcol16[:, tc, :].unsqueeze(1).broadcast_to([C, KR, KC]),
                           start=False, stop=True)
                i.then_inc(S["s_ready"], 1)
                pe.wait_ge(S["o_norm"], n - 1 if tc else n)
                for c in range(2):
                    i = nc.tensor.transpose(ps[0:KHALF, 6, 128 * c:128 * c + 128],
                                            vw[par][:, KHALF * c:KHALF * c + KHALF], ident)
                i.then_inc(S["vt_ps"], 1)

            def attend(tr, tc):
                n = tr * TC + tc
                par = tc % 2
                O = ps[:, 6, 256:256 + 17 * HEADS].rearrange("p (h d) -> p h d", h=HEADS)

                def probs(j):
                    if j == 2:
                        pe.wait_ge(S["pt_act"], n * 2 + 1)
                    if j == 3:
                        pe.wait_ge(S["pt_dve"], n * 2 + 1)
                    for q in range(4):
                        h, c = 2 * j + q // 2, q % 2
                        i = nc.tensor.transpose(ps[0:KHALF, 4 + j % 2, 128 * q:128 * q + 128],
                                                Sx[par][:, h, KHALF * c:KHALF * c + KHALF], ident)
                    i.then_inc(S["pt_ps"], 1)

                def values(j):
                    pe.wait_ge(S["pt_dve" if j % 2 else "pt_act"], n * 2 + j // 2 + 1)
                    for q in range(4):
                        h, c = 2 * j + q // 2, q % 2
                        i = mm(O[:, h, :], PT[j][0:KHALF, 128 * q:128 * q + 128], vT[par][0:KHALF, c, h, :],
                               start=(c == 0), stop=(c == 1))
                    return i
                pe.wait_ge(S["p_ready"], n + 1)
                pe.wait_ge(S["pt_dve"], n * 2)
                probs(0)
                probs(1)
                pe.wait_ge(S["vt_ev"], n + (2 if tc + 1 < TC else 1))
                pe.wait_ge(S["o_norm"], n)
                values(0)
                probs(2)
                values(1)
                probs(3)
                values(2)
                values(3).then_inc(S["o_ready"], 1)

            def project(tr, tc):
                n = tr * TC + tc
                pe.wait_ge(S["o_norm"], n + 1)
                pe.wait_ge(S["l0_x"], n)
                nc.tensor.transpose(ps[:, 7, 0:128], On, ident).then_inc(S["ot_ps"], 1)
                pe.wait_ge(S["ot_ev"], n + 1)
                mm(ps[:, 7, 128:256], sqT[:, 0, :], OT, start=True, stop=True).then_inc(S["pj_ps"], 1)

            pe.wait_ge(S["kv_ev"], 12)
            with pe.Fori(0, TR) as tr:
                for tc in range(TC + 2):
                    if tc < TC:
                        scores(tr, tc)
                    if tc >= 2:
                        project(tr, tc - 2)
                    if 1 <= tc <= TC:
                        attend(tr, tc - 1)
            gn_mean(1)

            pe.wait_ge(S["gn_apply"], 2)
            pe.wait_ge(S["gn_dve_apply"], 2)
            pe.wait_ge(S["l1diag"], 1)

            def message(k, bank, src):
                mm(ps[:, bank, 0:W], shiftd[:], ones[:], start=True, stop=False)
                pe.wait_ge(S["row_new"], k)
                for t in range(9):
                    m = mm(ps[:, bank, 0:W], w1T[:, t, :], rows[:, src, t:t + W], start=False, stop=(t == 8))
                m.then_inc(S["row_ps"], 1)
            message(0, 0, slice(0, 1))
            with pe.Fori(0, (H - 2) // 2) as pair:
                i = pair * 2 + 1
                message(i, 1, bass.ds(i, 1))
                message(i + 1, 0, bass.ds(i + 1, 1))
            message(H - 1, 1, slice(H - 1, H))
            with pe.Fori(0, (H - 2) // 2) as pair:
                i = pair * 2 + 1
                message(i + (H - 1), 0, bass.ds(i * -1 + (H - 1), 1))
                message(i + H, 1, bass.ds(i * -1 + (H - 2), 1))
            gn_mean(2)

            pe.wait_ge(S["gn_apply"], 3)
            pe.wait_ge(S["gn_dve_apply"], 3)
            with pe.Fori(0, STEPS // 4) as r:
                for i in range(4):
                    pe.wait_ge(S["c2_x"], r * 4)
                    for t in range(9):
                        m = mm(ps[:, i, 0:384], w2T[:, t, :],
                               padm[:, bass.ds(r * 16 + (4 * i + t // 3), ROWS), t % 3:t % 3 + W],
                               start=(t == 0), stop=(t == 8))
                    m.then_inc(S["c2_ps"], 1)
            for hh in range(2):
                m = mm(ps[:, 5 + hh, :], sqT[:, 4, :], Fmap[:, 512 * hh:512 * hh + 512], start=True, stop=True)
            m.then_inc(S["y_ps"], 1)
            gn_mean(3)
            pe.wait_ge(S["gap_in"], 1)
            mm(ps[:, 7, 0:1], sqT[:, 2, :], gapn, start=True, stop=True).then_inc(S["att_ps"], 1)

            def arm(n, i):
                pe.wait_ge(S["xg_ready"], n + 1)
                mm(ps[:, i, 0:384], sqT[:, 1, :], xg[i], start=True, stop=True).then_inc(S["fa_ps"], 1)

            def off1(n, i):
                pe.wait_ge(S["fa_ev"], n + 1)
                mm(ps[:, 2 + i, 0:384], sqT[:, 3, :], fa[i], start=True, stop=True).then_inc(S["of_ps"], 1)
            arm(0, 0)
            with pe.Fori(0, (STEPS - 2) // 2) as pair:
                r = pair * 2 + 1
                arm(r, 1)
                off1(r - 1, 0)
                arm(r + 1, 0)
                off1(r, 1)
            arm(STEPS - 1, 1)
            off1(STEPS - 2, 0)
            off1(STEPS - 1, 1)
            pe.wait_ge(S["of_ev"], STEPS)
            with pe.Fori(0, STEPS) as r:
                pe.wait_ge(S["om_ev"], r)
                for hf in range(2):
                    for t in range(9):
                        m = mm(ps[0:108, hf, 0:384], wcmT[:, t, 108 * hf:108 * hf + 108],
                               padm[:, bass.ds(r * ROWS + t // 3, ROWS), t % 3:t % 3 + W],
                               start=(t == 0), stop=(t == 8))
                m.then_inc(S["om_ps"], 1)
                pe.wait_ge(S["om_sig"], r)
                pe.wait_ge(S["omt_xy"], r)
                pe.wait_ge(S["om_ev"], r + 1)
                for i in range(3):
                    for hf in range(2):
                        m = nc.tensor.transpose(
                            ps[:, 2 + i // 2, 256 * (i % 2) + 108 * hf:256 * (i % 2) + 108 * hf + 108],
                            oms[hf][0:108, 128 * i:128 * i + 128], ident[0:108, 0:108])
                m.then_inc(S["omt_ps"], 1)

            def turn(job, k, srcs, rows_out):
                if not (isinstance(job, int) and job + k < 2):
                    pe.wait_ge(S["t_ev"], job + (k - 1))
                for j, s in enumerate(srcs):
                    i = nc.tensor.transpose(ps[0:rows_out, 6 + k % 2, 128 * j:128 * j + 128], s, ident)
                return i

            def contract(n, c, jobs_done):
                if not (isinstance(n, int) and n < 2):
                    pe.wait_ge(S["g_used"], n - 1)
                pe.wait_ge(S["t_ev"], jobs_done)
                for j in range(CH):
                    s = CH * c + j
                    i = mm(ps[:, 3 * (c % 2) + j // 2, 256 * (j % 2):256 * (j % 2) + WINS * CPG],
                           PTS[(2 * c + j // 3) % 4][0:WK, 128 * (j % 3):128 * (j % 3) + 128],
                           Fwin[:, s // TAPS, :, :].rearrange("p w c -> p (w c)"), start=True, stop=True)
                i.then_inc(S["g_ready"], 1)

            def values_of(par, job, k):
                for j in range(3):
                    turn(job, k + j, [val[par][:, 128 * (3 * j + i):128 * (3 * j + i) + 128] for i in range(3)],
                         C).then_inc(S["t_ps"], 1)

            def output_of(job, k):
                pe.wait_ge(S["t_ev"], job + k)
                for j in range(9):
                    i = mm(ps[:, 6 + k % 2, 0:128], wdT[:, j, :], valT[:, 128 * j:128 * j + 128],
                           start=(j == 0), stop=(j == 8))
                i.then_inc(S["t_ps"], 1)

            def tile(t, par, first=False):
                job = first_job(t)
                k = 0
                for c in range(CHUNKS):
                    n = t * CHUNKS + c
                    pe.wait_ge(S["pr_ready"], n + 1)
                    for j in range(2):
                        src = [PR[c % 2][:, WK * (3 * j + i):WK * (3 * j + i + 1)] for i in range(3)]
                        i = turn(job, k, src, WK)
                        i.then_inc(S["t_ps"], 1)
                        k += 1
                    if c == 0:
                        if not first:
                            contract(n - 1, CHUNKS - 1, job)
                    else:
                        contract(n - 1, c - 1, job + (chunk_job(c - 1, first) + 2))
                    if c == 3 and not first:
                        pe.wait_ge(S["val_ready"], t)
                        values_of(1 - par, job, k)
                        k += 3
                    if c == 4 and not first:
                        output_of(job, k)
                        k += 1
            tile(0, 0, first=True)
            with pe.Fori(0, (TILES - 2) // 2) as pair:
                t = pair * 2 + 1
                tile(t, 1)
                tile(t + 1, 0)
            tile(TILES - 1, 1)
            job = TILES * 28 - 4
            contract(TILES * CHUNKS - 1, CHUNKS - 1, job)
            pe.wait_ge(S["val_ready"], TILES)
            values_of(1, job, 0)
            output_of(job, 3)

        @block.vector
        def _(v):
            V = nc.vector

            def gn_stats(n):
                v.drain()
                for i in range(18):
                    V.bn_stats(stats[:, i, :], X[:, 512 * i:512 * i + 512])
                v.drain()
                V.bn_aggr(mv, stats[:].rearrange("p a b -> p (a b)"))
                v.drain()
                V.tensor_copy(t2[:, 0:1], mv[:, 0:1])
                V.scalar_tensor_tensor(out=t2[:, 1:2], in0=mv[:, 0:1], scalar=mv[:, 0:1], in1=mv[:, 1:2],
                                       op0=ALU.mult, op1=ALU.add).then_inc(S["gn_stats"], 1)
                v.wait_ge(S["gn_mean"], n + 1)
                V.tensor_copy(gm, ps[:, 7, 0:2])
                v.drain()
                V.scalar_tensor_tensor(out=nv, in0=gm[:, 0:1], scalar=gm[:, 0:1], in1=gm[:, 1:2],
                                       op0=ALU.mult, op1=ALU.subtract)
                v.drain()
                V.tensor_scalar(var, nv, -1.0, EPS, ALU.mult, ALU.add).then_inc(S["gn_var"], 1)
                v.wait_ge(S["gn_sd"], n + 1)
                V.reciprocal(rstd, sd)
                v.drain()
                V.scalar_tensor_tensor(out=nb, in0=gm[:, 0:1], scalar=-1.0, in1=rstd, op0=ALU.mult,
                                       op1=ALU.mult).then_inc(S["gn_scale"], 1)
                v.drain()

            def gn_apply(dst):
                V.tensor_scalar(dst[:, 0:DVE_ROWS, :], Xr[:, 0:DVE_ROWS, :], rstd, nb, ALU.mult,
                                ALU.add).then_inc(S["gn_dve_apply"], 1)

            def zero_border():
                V.memset(padm[:, 0:1, :], 0.0)
                V.memset(padm[:, H + 1:H + 2, :], 0.0)
                V.memset(padm[:, 1:H + 1, 0:1], 0.0)
                V.memset(padm[:, 1:H + 1, PW - 1:PW], 0.0)
            V.memset(ones[:], 1.0)
            V.memset(tiny[:, 40:44], 0.0)
            v.wait_ge(S["c_in"], 16)
            v.wait_ge(S["w_in"], W_IN)
            V.tensor_scalar(lv, rvar, EPS, None, ALU.add).then_inc(S["l1c_var"], 1)
            V.memset(Fpad, 0.0)
            V.tensor_copy(wdr.rearrange("p (g k c) -> p g c k", g=DG, c=CPG),
                          raw["wd"].rearrange("p (g c k) -> p g c k", g=DG, c=CPG))
            V.tensor_scalar(Fmap[:], fs[:, 0, :], BATCHW[0], None, ALU.mult)
            for b in range(1, 8):
                v.drain()
                V.scalar_tensor_tensor(out=Fmap[:], in0=fs[:, b, :], scalar=BATCHW[b], in1=Fmap[:],
                                       op0=ALU.mult, op1=ALU.add)
            v.drain()
            V.tensor_copy(Fpad[:, 0:FH, 0:FH], Fmap[:].rearrange("p (a b) -> p a b", b=FH))
            v.drain()
            for w in range(WINS):
                a, b = (WA - 1) * (w // NB), (WB - 1) * (w % NB)
                V.tensor_copy(Fcut[:, w, :].rearrange("p (a b) -> p a b", b=WB), Fpad[:, a:a + WA, b:b + WB])
            v.wait_ge(S["l1c_sd"], 1)
            V.reciprocal(lrs, lsd)
            v.drain()
            V.tensor_tensor(lsc, gam, lrs, ALU.mult)
            v.drain()
            V.tensor_scalar(raw["w1"], raw["w1"], lsc, None, ALU.mult).then_inc(S["wprep"], 1)
            V.scalar_tensor_tensor(out=lsh, in0=rmean, scalar=lsc, in1=bet, op0=ALU.mult, op1=ALU.subtract)
            v.drain()
            V.tensor_scalar(shiftd[:], ident, lsh, -1.0, ALU.mult, ALU.mult).then_inc(S["l1diag"], 1)
            for a, b in ((mrow16[:].rearrange("p a b -> p (a b)"), "mrow"),
                         (mcol16[:].rearrange("p a b -> p (a b)"), "mcol"), (inrow16[:], "inrow"),
                         (incol16[:], "incol")):
                V.tensor_copy(a, con[b])
            v.wait_ge(S["x_in"], 64)
            gn_stats(0)
            v.wait_ge(S["wt_ev"], len(JOBS))
            V.tensor_tensor(qkvT.rearrange("p t o -> p o t"), raw["qkv"].rearrange("p (o t) -> p o t", t=9),
                            con["own3"].unsqueeze(2).broadcast_to([C, 3 * C, 9]), ALU.mult)
            v.drain()
            zero_border()
            v.drain().then_inc(S["raw_done"], 1)
            gn_apply(padm[:, 1:H + 1, 1:W + 1])
            with v.Fori(0, STEPS // 4) as r:
                for i in range(4):
                    n = r * 4 + i
                    v.wait_ge(S["cv_ps"], n + 1)
                    V.tensor_scalar(Q[:, bass.ts(n, 384)], ps[:, i, 0:384], qb, None,
                                    ALU.add).then_inc(S["cv_ev"], 1)
            v.wait_ge(S["kv_ps"], 12)
            for b in range(2):
                V.memset(vT[b][:, :, :, HD:HD + 1], 1.0)
            v.drain()

            def softmax_max(n, par):
                sc = ps[:, 0:4, :].rearrange("p b (h k) -> p (b h) k", h=2)[:, :, 0:KEYS]
                v.drain()
                v.wait_ge(S["s_ready"], n + 1)
                V.tensor_reduce(smax, sc, AX.X, ALU.max)
                v.drain()
                V.tensor_tensor(Sx[par], sc, smax.unsqueeze(2).broadcast_to([C, HEADS, KEYS]),
                                ALU.subtract).then_inc(S["s_sub"], 1)

            def evac_probs(n):
                for j in (1, 3):
                    v.wait_ge(S["pt_ps"], n * 4 + j + 1)
                    V.tensor_scalar(PT[j][0:KHALF, :], ps[0:KHALF, 5, 0:512], 0.0, None,
                                    ALU.add).then_inc(S["pt_dve"], 1)

            def normalise(n):
                O = ps[:, 6, 256:256 + 17 * HEADS].rearrange("p (h d) -> p h d", h=HEADS)
                v.wait_ge(S["o_ready"], n + 1)
                V.reciprocal(srec.unsqueeze(2), O[:, :, HD:HD + 1])
                v.drain()
                v.wait_ge(S["ot_ps"], n)
                V.tensor_tensor(On.rearrange("p (h d) -> p h d", h=HEADS), O[:, :, 0:HD],
                                srec.unsqueeze(2).broadcast_to([C, HEADS, HD]), ALU.mult).then_inc(S["o_norm"], 1)

            def add_attention(tr, tc):
                n = tr * TC + tc
                v.wait_ge(S["pj_ps"], n + 1)
                xw = Xr[:, bass.ds(tr * 8, 8), 16 * tc:16 * tc + 16]
                V.scalar_tensor_tensor(out=xw, in0=ps[:, 7, 128:256].rearrange("p (a b) -> p a b", b=16),
                                       scalar=pjb, in1=xw, op0=ALU.add, op1=ALU.add).then_inc(S["l0_x"], 1)
            with v.Fori(0, TR) as tr:
                for tc in range(TC + 2):
                    n = tr * TC + tc
                    if tc < TC:
                        softmax_max(n, tc % 2)
                    if 1 <= tc <= TC:
                        if tc >= 2:
                            add_attention(tr, tc - 2)
                        evac_probs(n - 1)
                        normalise(n - 1)
                    if tc == TC + 1:
                        add_attention(tr, tc - 2)

            gn_stats(1)
            V.memset(rows[:, :, 0:4], 0.0)
            V.memset(rows[:, :, 4 + W:RP], 0.0)
            gn_apply(rows[:, :, 4:4 + W])
            v.drain()
            v.wait_ge(S["gn_apply"], 2)

            def add_row(k, bank, dst):
                v.wait_ge(S["row_ps"], k + 1)
                rw = rows[:, dst, 4:4 + W]
                V.scalar_tensor_tensor(out=rw, in0=ps[:, bank, 0:W].unsqueeze(1), scalar=0.0, in1=rw, op0=ALU.max,
                                       op1=ALU.add).then_inc(S["row_new"], 1)
            add_row(0, 0, slice(1, 2))
            with v.Fori(0, (H - 2) // 2) as pair:
                i = pair * 2 + 1
                add_row(i, 1, bass.ds(i + 1, 1))
                add_row(i + 1, 0, bass.ds(i + 2, 1))
            add_row(H - 1, 1, slice(H - 2, H - 1))
            with v.Fori(0, (H - 2) // 2) as pair:
                i = pair * 2 + 1
                add_row(i + (H - 1), 0, bass.ds(i * -1 + (H - 2), 1))
                add_row(i + H, 1, bass.ds(i * -1 + (H - 3), 1))
            v.drain()
            V.tensor_tensor(Xr, Xr, rows[:, :, 4:4 + W], ALU.add)
            gn_stats(2)
            zero_border()
            gn_apply(padm[:, 1:H + 1, 1:W + 1])
            with v.Fori(0, STEPS // 4) as r:
                for i in range(4):
                    n = r * 4 + i
                    v.wait_ge(S["c2_ps"], n + 1)
                    xw = X[:, bass.ts(n, 384)]
                    V.scalar_tensor_tensor(out=xw, in0=ps[:, i, 0:384], scalar=b2, in1=xw, op0=ALU.add,
                                           op1=ALU.add).then_inc(S["c2_x"], 1)
            gn_stats(3)
            V.scalar_tensor_tensor(out=gapn, in0=mv[:, 0:1], scalar=rstd, in1=nb, op0=ALU.mult,
                                   op1=ALU.add).then_inc(S["gap_in"], 1)
            third = 1.0 / 3.0

            def upsample(src, diff, dst):
                V.tensor_tensor(diff[:, 0:FH - 1], src[:, 1:FH], src[:, 0:FH - 1], ALU.subtract)
                V.tensor_copy(dst[:, 1:3 * FH:3], src)
                V.tensor_copy(dst[:, 0:1], src[:, 0:1])
                V.tensor_copy(dst[:, 3 * FH - 1:3 * FH], src[:, FH - 1:FH])
                v.drain()
                for k in (1, 2):
                    V.scalar_tensor_tensor(out=dst[:, 1 + k:3 * FH - 1:3], in0=diff[:, 0:FH - 1],
                                           scalar=k * third, in1=src[:, 0:FH - 1], op0=ALU.mult, op1=ALU.add)
                v.drain()
            v.wait_ge(S["y_ev"], 1)
            upsample(ys, yd, yr)
            upsample(yr.rearrange("p a b -> p b a"), cd.rearrange("p a b -> p b a"),
                     padm[:, 1:H + 1, 1:W + 1].rearrange("p a b -> p b a"))
            v.wait_ge(S["att_sg"], 1)
            V.tensor_scalar(att1, att, 1.0, None, ALU.add)
            v.drain()
            V.tensor_tensor(s3, rstd, att1, ALU.mult)
            V.tensor_tensor(b3, nb, att1, ALU.mult)
            v.drain()

            def gated(n, i):
                V.tensor_scalar(xg[i], X[:, bass.ts(n, 384)], s3, b3, ALU.mult, ALU.add).then_inc(S["xg_ready"], 1)

            def add_arm(n, i):
                v.wait_ge(S["fa_ev"], n + 1)
                xw = X[:, bass.ts(n, 384)]
                V.tensor_tensor(xw, xw, fa[i], ALU.add)
                v.wait_ge(S["of_ps"], n + 1)
                m = padm[:, bass.ds(n * ROWS + 1, ROWS), 1:W + 1]
                V.tensor_tensor(m, ps[:, 2 + i, 0:384].rearrange("p (a b) -> p a b", b=W), m,
                                ALU.add).then_inc(S["of_ev"], 1)
                v.drain().then_inc(S["fx"], 1)
            gated(0, 0)
            gated(1, 1)
            with v.Fori(0, (STEPS - 2) // 2) as pair:
                for i in range(2):
                    add_arm(pair * 2 + i, i)
                    gated(pair * 2 + (2 + i), i)
            add_arm(STEPS - 2, 0)
            add_arm(STEPS - 1, 1)
            v.drain()
            by = con["basey"].rearrange("p (i s) -> p i s", i=3)
            bx = con["basex"].rearrange("p (i s) -> p i s", i=3)
            with v.Fori(0, STEPS) as r:
                pt = ps[:, 2:4, :].rearrange("p b (i s) -> p (b i) s", i=2)[:, 0:3, :]
                v.wait_ge(S["omt_ps"], r + 1)
                V.tensor_tensor(yx[:, 0, :].rearrange("p (i s) -> p i s", i=3), pt[:, :, 0:SAMP], by, ALU.add)
                V.tensor_tensor(yx[:, 1, :].rearrange("p (i s) -> p i s", i=3), pt[:, :, SAMP:2 * SAMP], bx,
                                ALU.add)
                v.drain()
                V.tensor_scalar(con["basey"], con["basey"], float(ROWS), None, ALU.add)
                V.tensor_scalar(ee, yx, -47.5, None, ALU.add).then_inc(S["omt_xy"], 1)
                V.tensor_scalar(uv, yx, 1.0, float(H - 2), ALU.max, ALU.min)
                v.drain()
                V.tensor_scalar(uv, uv, 1.0, third, ALU.subtract, ALU.mult)
                v.drain()
                V.tensor_scalar(wia, uv[:, 0, :], float(WA - 1), None, ALU.is_ge)
                V.tensor_scalar(wja, uv[:, 1, :], float(WB - 1), None, ALU.is_ge)
                v.drain()
                V.scalar_tensor_tensor(out=wia, in0=uv[:, 0, :], scalar=2.0 * (WA - 1), in1=wia, op0=ALU.is_ge,
                                       op1=ALU.add)
                V.scalar_tensor_tensor(out=wja, in0=uv[:, 1, :], scalar=2.0 * (WB - 1), in1=wja, op0=ALU.is_ge,
                                       op1=ALU.add)
                v.drain()
                V.scalar_tensor_tensor(out=wja, in0=uv[:, 1, :], scalar=3.0 * (WB - 1), in1=wja, op0=ALU.is_ge,
                                       op1=ALU.add)
                V.scalar_tensor_tensor(out=UL[:, bass.ts(r, 216)], in0=wia, scalar=-float(WA - 1),
                                       in1=uv[:, 0, :], op0=ALU.mult, op1=ALU.add)
                v.drain()
                V.scalar_tensor_tensor(out=VL[:, bass.ts(r, 216)], in0=wja, scalar=-float(WB - 1),
                                       in1=uv[:, 1, :], op0=ALU.mult, op1=ALU.add)
                V.scalar_tensor_tensor(out=WI[:, bass.ts(r, 216)], in0=wia, scalar=float(NB), in1=wja,
                                       op0=ALU.mult, op1=ALU.add)
                v.wait_ge(S["om_sig"], r + 1)
                v.wait_ge(S["om_abs"], r + 1)
                V.tensor_scalar(ee, ee, -1.0, 48.5, ALU.mult, ALU.add)
                v.drain()
                V.tensor_scalar(ee, ee, 0.0, 1.0, ALU.max, ALU.min)
                v.drain()
                V.tensor_tensor(ma, sg, ee[:, 0, :], ALU.mult)
                v.drain()
                V.tensor_tensor(MS[:, bass.ts(r, 216)], ma, ee[:, 1, :], ALU.mult).then_inc(S["coord"], 1)
                v.drain()

            oh3 = OH.rearrange("p (s w) -> p s w", w=WINS)

            def add_out(t, job):
                v.wait_ge(S["t_ev"], job)
                xw = X[:, bass.ts(t, 128)]
                V.tensor_tensor(xw, xw, orelu, ALU.add).then_inc(S["x_out"], 1)

            def tile(t, par, first=False):
                v.drain()
                V.tensor_tensor(oh3, WI[:, bass.ts(t, SAMP)].unsqueeze(2).broadcast_to([C, SAMP, WINS]),
                                con["iota"].unsqueeze(1).broadcast_to([C, SAMP, WINS]), ALU.is_equal)
                for c in range(CHUNKS):
                    n = t * CHUNKS + c
                    v.drain()
                    v.wait_ge(S["g_ready"], n + 1)
                    V.tensor_tensor(
                        GM.rearrange("p (s w c) -> p s w c", s=CH, w=WINS),
                        ps[:, 3 * (c % 2):3 * (c % 2) + 3, :].rearrange("p b (s n) -> p (b s) n", s=2)
                        [:, :, 0:WINS * CPG].rearrange("p s (w c) -> p s w c", w=WINS),
                        oh3[:, CH * c:CH * c + CH, :].unsqueeze(3).broadcast_to([C, CH, WINS, CPG]),
                        ALU.mult).then_inc(S["g_used"], 1)
                    v.drain()
                    i = V.tensor_reduce(val[par][:, CH * CPG * c:CH * CPG * (c + 1)].rearrange(
                        "p (s c) -> p s c", s=CH), GM.rearrange("p (s w c) -> p s c w", s=CH, w=WINS),
                        AX.X, ALU.add)
                    if c == CHUNKS - 1:
                        i.then_inc(S["val_ready"], 1)
                    if c == 6 and not first:
                        add_out(t - 1, (t * 28 - 4) + 14)
            tile(0, 0, first=True)
            with v.Fori(0, (TILES - 2) // 2) as pair:
                t = pair * 2 + 1
                tile(t, 1)
                tile(t + 1, 0)
            tile(TILES - 1, 1)
            add_out(TILES - 1, TILES * 28)


_INS = ["x", "L0_conv_qkv_w", "L0_conv_qkv_b", "L0_conv_proj_w", "L0_conv_proj_b", "L1_conv_conv_w",
        "L1_conv_gamma", "L1_conv_beta", "L1_conv_run_mean", "L1_conv_run_var", "L2_conv_weight", "L2_conv_bias",
        "L3_conv_feat_s", "L3_conv_w_atten", "L3_conv_w_fsm", "L3_conv_w_off", "L3_conv_w_cm", "L3_conv_b_cm",
        "L3_conv_w_dcn", "L3_conv_b_dcn"]


def kernel(**inputs):
    import concourse.bacc as bacc
    from concourse.bass_utils import run_bass_kernel_spmd

    nc = bacc.Bacc("TRN2", target_bir_lowering=False, num_devices=1)
    arrays, d = {}, {}
    for name in _INS:
        a = np.ascontiguousarray(inputs[name])
        arrays[f"in_{name}"] = a
        d[name] = nc.dram_tensor(f"in_{name}", a.shape, mybir.dt.from_np(a.dtype), kind="ExternalInput").ap()
    made = shape_constants()
    arrays["in_consts"] = np.ascontiguousarray(np.concatenate([made[n] for n in CONSTS], axis=1))
    consts = nc.dram_tensor("in_consts", arrays["in_consts"].shape, F32, kind="ExternalInput").ap()
    out = nc.dram_tensor("out_0_dram", (1, C, H, W), F32, kind="ExternalOutput").ap()
    build_program(nc, d, consts, out)
    r = run_bass_kernel_spmd(nc, [arrays], core_ids=[0])
    return r.results[0]["out_0_dram"]
```

```python
from contextlib import ExitStack

import numpy as np

import concourse.bass as bass
from concourse import mybir

ALU = mybir.AluOpType
ACT = mybir.ActivationFunctionType
AX = mybir.AxisListType
F32 = mybir.dt.float32
BF16 = mybir.dt.bfloat16

C, H, W = 128, 96, 96
PIX = H * W
PW = W + 2
ROWS = 4
STEPS = H // ROWS
HEADS, HD, KS = 8, 16, 8
SUB = 48
QR, QC = 4, 8
TR, TC = SUB // QR, SUB // QC
KR, KC = QR + KS, QC + KS - 1
KEYS = KR * KC
KPAD = 192
BLOCKS = HEADS * KPAD // 128
VW = HD + 1
TILES0 = TR * TC
PADK = 4
KPH, KPW = PADK + SUB + 4, 3 + SUB + 4
FAR = -float(2 ** 99)
RP = W + 8
FH = 32
WA, WB = FH, 4
WSTEP = WB - 1
WINS = -(-(FH - 1) // WSTEP)
WK = WA * WB
FPW = WSTEP * WINS + 1
ROUND = 1.5 * 2 ** 23
DG, TAPS = 8, 9
SAMP = DG * TAPS
TILES = PIX // 128
CH = 6
PARTS = 8
PS = SAMP // PARTS
CHUNKS = SAMP // CH
CPG = C // DG
EPS = 1e-5


def attention_masks():
    row = np.full((C, TR, KR), 0.0, np.float32)
    col = np.full((C, TC, KC), 0.0, np.float32)
    for t in range(TR):
        for a in range(QR):
            start = min(max(QR * t + a - 3, 0), SUB - KS)
            for r in range(KR):
                if not start <= QR * t - PADK + r < start + KS:
                    row[a, t, r] = FAR
    for t in range(TC):
        for a in range(QC):
            start = min(max(QC * t + a - 3, 0), SUB - KS)
            for r in range(KC):
                if not start <= QC * t - 3 + r < start + KS:
                    col[a, t, r] = FAR
    q = np.arange(128)
    inrow = np.zeros((C, 128), np.float32)
    incol = np.zeros((C, 128), np.float32)
    inrow[(q // 16) // 2, q] = 1.0
    incol[(q % 16) // 2, q] = 1.0
    return row, col, inrow, incol


def shape_constants():
    p = np.arange(C)
    out = {}
    out["ident"] = np.eye(C, dtype=np.float32)
    out["gmean"] = (p[:, None] // 4 == p[None, :] // 4).astype(np.float32) / 4
    o = np.arange(3 * C)
    out["own3"] = (o[None, :] // 3 == p[:, None]).astype(np.float32)
    out["headq"] = (p[:, None] // HD == np.arange(HEADS)[None, :]).astype(np.float32) * HD ** -0.5
    row, col, inrow, incol = attention_masks()
    out["mrow"], out["mcol"] = row.reshape(C, -1), col.reshape(C, -1)
    out["inrow"], out["incol"] = inrow, incol
    lin = 128 * np.arange(3)[None, :, None] + p[:, None, None]
    k = (np.arange(SAMP) % TAPS)[None, None, :]
    out["basey"] = (lin // W + k // 3 - 1).astype(np.float32).reshape(C, -1)
    out["basex"] = (lin % W + k % 3 - 1).astype(np.float32).reshape(C, -1)
    out["iota"] = np.tile(np.arange(WA, dtype=np.float32)[None, :], (C, 1))
    return out


CONSTS = ["ident", "gmean", "own3", "headq", "mrow", "mcol", "inrow", "incol", "basey", "basex", "iota"]
CWIDTH = dict(ident=C, gmean=C, own3=3 * C, headq=HEADS, mrow=TR * KR, mcol=TC * KC, inrow=C, incol=C,
              basey=3 * SAMP, basex=3 * SAMP, iota=WA)
BATCHW = [1 - abs(i - 3.5) / 8 for i in range(8)]
BATCHW = [w / sum(BATCHW) for w in BATCHW]


def build_program(nc, d, consts, out):
    with ExitStack() as ctx:
        def sb(name, shape, dt=F32):
            return ctx.enter_context(nc.sbuf_tensor(name, shape, dt))

        def sem(name):
            return ctx.enter_context(nc.semaphore(name))

        X = sb("X", [C, PIX])
        pad = sb("pad", [C, H * RP])
        work = sb("work", [C, 22000])
        w1T = sb("w1T", [C, TAPS, C])
        w2T = sb("w2T", [C, TAPS, C])
        wcmT = sb("wcmT", [C, TAPS, 3 * SAMP])
        wdT = sb("wdT", [C, TAPS, C])
        sqT = sb("sqT", [C, 5, C])
        Fwin = sb("Fwin", [WK, DG, WINS, CPG])
        cst = sb("cst", [C, sum(CWIDTH.values())])
        vec = sb("vec", [C, 12])
        mrow16 = sb("mrow16", [C, TR, KR], BF16)
        mcol16 = sb("mcol16", [C, TC, KC], BF16)
        inrow16 = sb("inrow16", [C, C], BF16)
        incol16 = sb("incol16", [C, C], BF16)
        tiny = sb("tiny", [C, 64])
        stats = sb("stats", [C, 18, 6])
        shiftd = sb("shiftd", [C, C])
        ones = sb("ones", [C, W])
        ps = ctx.enter_context(nc.psum_tensor("ps", [C, 8, 512], F32))

        off = 0
        con = {}
        for name in CONSTS:
            con[name] = cst[:, off:off + CWIDTH[name]]
            off += CWIDTH[name]
        ident = con["ident"]

        Xr = X[:].rearrange("p (h w) -> p h w", w=W)
        padm = pad[:, 0:(H + 2) * PW].rearrange("p (h w) -> p h w", w=PW)
        rows = pad[:].rearrange("p (h w) -> p h w", w=RP)

        raw = {}
        at = 0
        for name, n in (("w1", 1152), ("w2", 1152), ("wd", 1152), ("cma", 1152), ("cmb", 1152), ("fsm", C),
                        ("att", C), ("off", 2 * C), ("proj", C), ("qkv", 3 * C * 9)):
            raw[name] = pad[:, at:at + n]
            at += n
        Q = work[:, 0:PIX]
        Qr = Q.rearrange("p (h w) -> p h w", w=W)
        kP = work[:, PIX:PIX + KPH * KPW].rearrange("p (h w) -> p h w", w=KPW)
        o2 = PIX + KPH * KPW
        vP = work[:, o2:o2 + KPH * KPW].rearrange("p (h w) -> p h w", w=KPW)
        o3 = o2 + KPH * KPW
        qkvT = work[:, o3:o3 + 9 * 3 * C].rearrange("p (t o) -> p t o", t=9)
        fs = work[:, 0:8 * FH * FH].rearrange("p (b n) -> p b n", b=8)
        Fpad = work[:, 8192:8192 + FH * FPW].rearrange("p (h w) -> p h w", w=FPW)
        wdr = work[:, 9600:9600 + 1152]
        Fcut = work[:, 10752:10752 + WINS * WK].rearrange("p (w k) -> p w k", w=WINS)
        Fmap = sb("Fmap", [C, FH * FH])
        ao = [0]

        def carve(n, base=pad):
            v = base[:, ao[0]:ao[0] + n]
            ao[0] += n
            return v
        Qm = [carve(HEADS * 128).rearrange("p (h q) -> p h q", h=HEADS) for _ in range(2)]
        vw = [carve(KPAD) for _ in range(2)]
        Sx = [carve(HEADS * KPAD).rearrange("p (h k) -> p h k", h=HEADS) for _ in range(2)]
        PT = [carve(512) for _ in range(BLOCKS // 4)]
        On = carve(128)
        OT = carve(128)
        smax = carve(HEADS)
        srec = carve(HEADS)
        assert ao[0] <= H * RP
        PAIR = 3 * VW * HEADS + 2 * VW
        Vm = [work[:, o3 + HEADS // 2 * PAIR * i:o3 + HEADS // 2 * PAIR * (i + 1)] for i in range(2)]
        yr = work[:, 0:H * FH].rearrange("p (h w) -> p h w", w=FH)
        ys = work[:, 3072:3072 + FH * FH].rearrange("p (h w) -> p h w", w=FH)
        yd = work[:, 4096:4096 + FH * FH].rearrange("p (h w) -> p h w", w=FH)
        cd = work[:, 5120:5120 + H * FH].rearrange("p (h w) -> p h w", w=FH)
        xg = [work[:, 8192 + 384 * i:8192 + 384 * (i + 1)] for i in range(2)]
        fa = [work[:, 8960 + 384 * i:8960 + 384 * (i + 1)] for i in range(2)]
        NS = TILES * SAMP
        UL, VL, MS, WI = (work[:, i * NS:(i + 1) * NS] for i in range(4))
        flat1 = w1T[:].rearrange("p a b -> p (a b)")
        flat2 = w2T[:].rearrange("p a b -> p (a b)")
        oms = [flat1[:, 384 * i:384 * (i + 1)] for i in range(2)]
        yx = flat2[:, 0:432].rearrange("p (a n) -> p a n", a=2)
        ee = flat2[:, 432:864].rearrange("p (a n) -> p a n", a=2)
        sg = flat1[:, 768:984]
        wja = work[:, 4 * NS:4 * NS + 216]
        uv = work[:, 4 * NS + 216:4 * NS + 648].rearrange("p (a n) -> p a n", a=2)
        ma = work[:, 4 * NS + 648:4 * NS + 864]
        ao[0] = 0
        HU = [carve(SAMP * WA).rearrange("p (s a) -> p s a", a=WA) for _ in range(2)]
        DV = carve(SAMP * WB)
        HV = [carve(SAMP * WB).rearrange("p (s a) -> p s a", a=WB) for _ in range(2)]
        PR = [carve(CH * WK) for _ in range(2)]
        PTS = [carve(384) for _ in range(4)]
        val0 = carve(SAMP * CPG)
        mst = carve(SAMP)
        orelu = carve(128)
        assert ao[0] <= H * RP
        val = [val0, work[:, 4 * NS:4 * NS + SAMP * CPG]]
        valT = flat1
        flatc = wcmT[:].rearrange("p a b -> p (a b)")
        GM = [flat2[:, 0:CH * WINS * CPG], flatc[:, 0:CH * WINS * CPG]]
        OH = flatc[:, CH * WINS * CPG:CH * WINS * CPG + SAMP * WINS]

        names = """x_in w_in c_in zeroed gn_stats gn_mean gn_var gn_sd gn_apply gn_dve_apply l1c_var l1c_sd
        raw_done wt_ps wt_ev wprep fmean l1diag
        cv_ps cv_ev kv_ps kv_ev
        vm_ready qm_ready s_ready vt_ps vt_ev s_sub p_ready pt_ps pt_ev o_ready o_norm ot_ps ot_ev pj_ps l0_x
        row_ps row_new
        c2_ps c2_x gap_in att_ps att_sg gn_scale y_ps y_ev y_up xg_ready fa_ps fa_ev of_ps of_ev fx
        om_ps om_ev omt_ps omt_xy om_sig om_abs coord
        pr_ready t_ps t_ev g_ready g_used onehot summed du_ready dv_ready u_hat v_hat x_out stored""".split()
        S = {n: sem(n) for n in names}
        PRIMED = "fx coord cv_ev c2_x om_ev om_sig omt_xy".split()
        block = ctx.enter_context(nc.Block())

        def weight_jobs():
            jobs = []
            for src, dst in (("w1", w1T), ("w2", w2T)):
                v = raw[src].rearrange("p (c t) -> p c t", t=9)
                for j in range(3):
                    jobs.append(([(v[:, :, 3 * j + i], 128 * i) for i in range(3)],
                                 dst[:, 3 * j:3 * j + 3, :].rearrange("p a b -> p (a b)"), C, 384))
            for j in range(3):
                jobs.append(([(wdr[:, 128 * (3 * j + i):128 * (3 * j + i + 1)], 128 * i) for i in range(3)],
                             wdT[:, 3 * j:3 * j + 3, :].rearrange("p a b -> p (a b)"), C, 384))
            va = raw["cma"].rearrange("p (c t) -> p c t", t=9)
            vb = raw["cmb"].rearrange("p (c t) -> p c t", t=9)
            for j in range(5):
                ts = [t for t in (2 * j, 2 * j + 1) if t < 9]
                src = []
                for n, t in enumerate(ts):
                    src += [(va[:, :, t], 216 * n), (vb[0:88, :, t], 216 * n + 128)]
                jobs.append((src, wcmT[:, ts[0]:ts[-1] + 1, :].rearrange("p a b -> p (a b)"), C, 216 * len(ts)))
            ro = raw["off"]
            jobs.append(([(raw["proj"], 0), (raw["fsm"], 128), (raw["att"], 256)],
                         sqT[:, 0:3, :].rearrange("p a b -> p (a b)"), C, 384))
            jobs.append(([(ro[:, 0:C], 0), (ro[:, C:2 * C], 128)],
                         sqT[:, 3:5, :].rearrange("p a b -> p (a b)"), C, 256))
            for j in range(3):
                src = []
                ws = range(4 * j, min(4 * j + 4, WINS))
                for i, w in enumerate(ws):
                    src.append((Fcut[:, w, :], 128 * i))
                jobs.append((src, Fwin[:, :, ws[0]:ws[-1] + 1, :].rearrange("p g w c -> p w g c"), None,
                             128 * len(ws)))
            return jobs
        JOBS = weight_jobs()

        def first_job(t):
            return 0 if isinstance(t, int) and t == 0 else t * 28 - 4

        def chunk_job(c, first):
            return 2 * c + (0 if first else min(max(c - 3, 0), 4))

        def slots(e, slot):
            for tc in range(TC):
                slot(0, tc, tc)
            with e.Fori(1, TR) as tr:
                for tc in range(TC):
                    slot(tr, tc, tr * TC + tc)
            slot(TR, 0, TILES0)
            slot(TR, 1, TILES0 + 1)

        def before(tr, tc, k):
            return (tr, tc - k) if tc >= k else (tr - 1, tc - k + TC)

        def there(n, k=0):
            return not isinstance(n, int) or 0 <= n - k < TILES0

        @block.sync
        def _(sp):
            for n in PRIMED:
                sp.sem_inc(S[n], 1)
            for h in range(4):
                sp.dma_start(X[:, 2304 * h:2304 * (h + 1)],
                             d["x"].rearrange("a c h w -> (a c) (h w)")[:, 2304 * h:2304 * (h + 1)]
                             ).then_inc(S["x_in"], 16)
            sp.dma_start(cst[:], consts).then_inc(S["c_in"], 16)
            sp.dma_start(fs, d["L3_conv_feat_s"].rearrange("b c h w -> c b (h w)")).then_inc(S["w_in"], 16)
            sp.dma_start(raw["qkv"], d["L0_conv_qkv_w"].rearrange("o a b c -> (o a b c)").partition_broadcast(C)
                         ).then_inc(S["w_in"], 16)
            sp.dma_start(raw["w1"], d["L1_conv_conv_w"].rearrange("o c t -> o (c t)")).then_inc(S["w_in"], 16)
            sp.dma_start(raw["w2"], d["L2_conv_weight"].rearrange("o c a b -> o (c a b)")).then_inc(S["w_in"], 16)
            sp.dma_start(raw["wd"], d["L3_conv_w_dcn"].rearrange("o c a b -> o (c a b)")).then_inc(S["w_in"], 16)
            cm = d["L3_conv_w_cm"].rearrange("o c a b -> o (c a b)")
            sp.dma_start(raw["cma"], cm[0:C, :]).then_inc(S["w_in"], 16)
            sp.dma_start(raw["cmb"][0:88, :], cm[C:216, :]).then_inc(S["w_in"], 16)
            sp.dma_start(raw["fsm"], d["L3_conv_w_fsm"]).then_inc(S["w_in"], 16)
            sp.dma_start(raw["att"], d["L3_conv_w_atten"]).then_inc(S["w_in"], 16)
            sp.dma_start(raw["off"], d["L3_conv_w_off"]).then_inc(S["w_in"], 16)
            sp.dma_start(raw["proj"], d["L0_conv_proj_w"].rearrange("o c a b -> o (c a b)")).then_inc(S["w_in"], 16)
            sp.dma_start(vec[:, 0:3], d["L0_conv_qkv_b"].rearrange("(t c) -> c t", t=3),
                         allow_slow_non_contiguous=True).then_inc(S["w_in"], 16)
            for i, n in enumerate(("L0_conv_proj_b", "L1_conv_gamma", "L1_conv_beta", "L1_conv_run_mean",
                                   "L1_conv_run_var", "L2_conv_bias", "L3_conv_b_dcn")):
                sp.dma_start(vec[:, 3 + i:4 + i], d[n].rearrange("(c a) -> c a", a=1)).then_inc(S["w_in"], 16)
            bcm = d["L3_conv_b_cm"].rearrange("(a c) -> c a", a=2)
            sp.dma_start(vec[0:108, 10:12], bcm, allow_slow_non_contiguous=True).then_inc(S["w_in"], 16)
            sp.wait_ge(S["x_out"], TILES)
            o = out.rearrange("a c h w -> (a c) (h w)")
            sp.dma_start(o, X[:]).then_inc(S["stored"], 16)
            sp.wait_ge(S["stored"], 16)
        W_IN = 16 * 20
        qb, kb, vb_ = vec[:, 0:1], vec[:, 1:2], vec[:, 2:3]
        pjb, gam, bet, rmean, rvar = (vec[:, i:i + 1] for i in range(3, 8))
        b2, bdc = vec[:, 8:9], vec[:, 9:10]
        T = lambda i, n=1: tiny[:, i:i + n]
        mv, t2, gm, nv, var, sd, rstd, nb = T(0, 2), T(2, 2), T(4, 2), T(6), T(7), T(8), T(9), T(10)
        s3, b3, gapn, att, att1 = T(11), T(12), T(13), T(14), T(15)
        lv, lsd, lrs, lsc, lsh = T(16), T(17), T(18), T(19), T(20)
        DVE_ROWS = 60

        @block.gpsimd
        def _(g):
            g.wait_ge(S["raw_done"], 1)
            nc.gpsimd.memset(kP, 0.0)
            nc.gpsimd.memset(vP, 0.0).then_inc(S["zeroed"], 1)
            g.wait_ge(S["kv_ev"], 12)
            g.wait_ge(S["cv_ev"], 1 + STEPS)
            for b in range(2):
                nc.gpsimd.memset(vw[b][:, KEYS:KPAD], 0.0)

            def prepare(tr, tc, n):
                if not there(n):
                    return
                par = tc % 2
                if there(n, 2):
                    g.drain()
                    g.wait_ge(S["vt_ps"], n - 1)
                    nc.gpsimd.tensor_tensor(T(40), T(41), T(41), ALU.mult)
                nc.gpsimd.tensor_copy(
                    vw[par][:, 0:KEYS].rearrange("p (a b) -> p a b", b=KC),
                    vP[:, bass.ds(tr * QR, KR), bass.ds(QC * tc, KC)])
                nc.gpsimd.tensor_tensor(
                    Qm[par].rearrange("p h (a b) -> p h a b", b=16),
                    Qr[:, bass.ds(tr * (2 * QR), 8), 16 * tc:16 * tc + 16].unsqueeze(1)
                    .broadcast_to([C, HEADS, 8, 16]),
                    con["headq"].unsqueeze(2).unsqueeze(3).broadcast_to([C, HEADS, 8, 16]),
                    ALU.mult).then_inc(S["qm_ready"], 1)
            slots(g, prepare)
            g.wait_ge(S["coord"], 1 + STEPS)

            def column_offsets(t):
                g.drain()
                nc.gpsimd.tensor_copy(mst, MS[:, bass.ts(t, SAMP)])
                nc.gpsimd.tensor_tensor(
                    DV.rearrange("p (s a) -> p s a", a=WB),
                    VL[:, bass.ts(t, SAMP)].unsqueeze(2).broadcast_to([C, SAMP, WB]),
                    con["iota"][:, 0:WB].unsqueeze(1).broadcast_to([C, SAMP, WB]),
                    ALU.subtract).then_inc(S["dv_ready"], 1)

            def row_offsets(t, par, j):
                nc.gpsimd.tensor_tensor(
                    HU[par][:, PS * j:PS * j + PS, :],
                    UL[:, bass.ds(t * SAMP + PS * j, PS)].unsqueeze(2).broadcast_to([C, PS, WA]),
                    con["iota"].unsqueeze(1).broadcast_to([C, PS, WA]), ALU.subtract).then_inc(S["du_ready"], 1)

            def masked_hat(t, par):
                g.wait_ge(S["v_hat"], t + 1)
                nc.gpsimd.tensor_tensor(HV[par], DV.rearrange("p (s a) -> p s a", a=WB),
                                        mst.unsqueeze(2).broadcast_to([C, SAMP, WB]), ALU.mult)

            def add_out(t, job):
                g.drain()
                g.wait_ge(S["t_ev"], job)
                xw = X[:, bass.ts(t, 128)]
                nc.gpsimd.tensor_tensor(xw, xw, orelu, ALU.add).then_inc(S["x_out"], 1)

            def tile(t, par, first=False, last=False):
                job = first_job(t)
                g.drain()
                g.wait_ge(S["u_hat"], t + 1)
                for c in range(CHUNKS):
                    if c >= 2:
                        g.wait_ge(S["t_ps"], job + (chunk_job(c - 2, first) + 2))
                    elif not first:
                        g.wait_ge(S["t_ps"], job - (2 - 2 * c))
                    sl = slice(CH * c, CH * c + CH)
                    nc.gpsimd.tensor_tensor(
                        PR[c % 2].rearrange("p (s a b) -> p s a b", a=WA, b=WB),
                        HU[par][:, sl, :].unsqueeze(3).broadcast_to([C, CH, WA, WB]),
                        HV[par][:, sl, :].unsqueeze(2).broadcast_to([C, CH, WA, WB]),
                        ALU.mult).then_inc(S["pr_ready"], 1)
                    if c == 0 and not last:
                        column_offsets(t + 1)
                    if 1 <= c <= PARTS and not last:
                        row_offsets(t + 1, 1 - par, c - 1)
                    if c == 4 and not last:
                        masked_hat(t + 1, 1 - par)
                    if c == 9 and not first:
                        add_out(t - 1, job + 18)
            column_offsets(0)
            for j in range(PARTS):
                row_offsets(0, 0, j)
            masked_hat(0, 0)
            tile(0, 0, first=True)
            with g.Fori(0, (TILES - 2) // 2) as pair:
                t = pair * 2 + 1
                tile(t, 1)
                tile(t + 1, 0)
            tile(TILES - 1, 1, last=True)
            add_out(TILES - 1, TILES * 28)

        @block.scalar
        def _(act):
            def gn_root(n):
                act.wait_ge(S["gn_var"], n + 1)
                nc.scalar.activation(sd, var, ACT.Sqrt).then_inc(S["gn_sd"], 1)

            def gn_apply(n, dst):
                act.wait_ge(S["gn_scale"], n + 1)
                nc.scalar.activation(dst[:, DVE_ROWS:H, :], Xr[:, DVE_ROWS:H, :], ACT.Identity, scale=rstd,
                                     bias=nb).then_inc(S["gn_apply"], 1)
            act.wait_ge(S["l1c_var"], 1)
            nc.scalar.activation(lsd, lv, ACT.Sqrt).then_inc(S["l1c_sd"], 1)
            for n, (src, dst, m, width) in enumerate(JOBS):
                act.wait_ge(S["wt_ps"], n + 1)
                if m is None:
                    sv = ps[:, n % 4, 0:width].rearrange("p (w g c) -> p w g c", g=DG, c=CPG)
                    for w in range(width // 128):
                        i = nc.scalar.activation(dst[:, w], sv[:, w], ACT.Copy)
                    i.then_inc(S["wt_ev"], 1)
                else:
                    nc.scalar.activation(dst, ps[:, n % 4, 0:width], ACT.Copy).then_inc(S["wt_ev"], 1)
            gn_root(0)
            act.wait_ge(S["raw_done"], 1)
            gn_apply(0, padm[:, 1:H + 1, 1:W + 1])
            act.wait_ge(S["zeroed"], 1)
            for n in range(12):
                i, kv = n // 2, n % 2
                act.wait_ge(S["kv_ps"], n + 1)
                nc.scalar.activation((kP, vP)[kv][:, PADK + 8 * i:PADK + 8 * i + 8, 3:3 + SUB],
                                     ps[:, 4 + n % 4, 0:384].rearrange("p (a b) -> p a b", b=SUB),
                                     ACT.Identity, bias=(kb, vb_)[kv]).then_inc(S["kv_ev"], 1)
            def slot(tr, tc, n):
                par = tc % 2
                if there(n, 2):
                    act.wait_ge(S["ot_ps"], n - 1)
                    nc.scalar.activation(OT, ps[:, 7, 136:264], ACT.Copy).then_inc(S["ot_ev"], 1)
                if there(n):
                    act.wait_ge(S["vt_ps"], n + 1)
                    tv = ps[:, 6, 0:384].rearrange("p (k m d) -> p k m d", k=3, m=HEADS // 2)
                    vm = Vm[par].rearrange("p (m x) -> p m x", x=PAIR)
                    B = VW * HEADS
                    for dst, at, rows_, k, odd in ((slice(0, C), 0, slice(0, C), 0, 0),
                                                   (slice(0, 64), B, slice(0, 64), 1, 0),
                                                   (slice(64, C), B + VW, slice(0, 64), 0, 1),
                                                   (slice(0, C), 2 * B + VW, slice(0, C), 2, 1)):
                        i = nc.scalar.activation(vm[dst, :, at:at + HD],
                                                 tv[rows_, k, :, HD * odd:HD * odd + HD], ACT.Copy)
                    i.then_inc(S["vt_ev"], 1)
                if there(n, 1):
                    for j in range(BLOCKS // 4):
                        act.wait_ge(S["pt_ps"], (n - 1) * (BLOCKS // 4) + j + 1)
                        nc.scalar.activation(PT[j], ps[:, 4 + j % 2, 0:512], ACT.Copy).then_inc(S["pt_ev"], 1)
                if there(n):
                    act.wait_ge(S["s_sub"], n + 1)
                    nc.scalar.activation(Sx[par][:, :, 0:KEYS], Sx[par][:, :, 0:KEYS],
                                         ACT.Exp).then_inc(S["p_ready"], 1)
            act.wait_ge(S["vm_ready"], 1)
            slots(act, slot)
            gn_root(1)
            gn_apply(1, rows[:, :, 4:4 + W])
            gn_root(2)
            gn_apply(2, padm[:, 1:H + 1, 1:W + 1])
            gn_root(3)
            act.wait_ge(S["att_ps"], 1)
            nc.scalar.activation(att, ps[:, 7, 0:1], ACT.Sigmoid).then_inc(S["att_sg"], 1)
            act.wait_ge(S["y_ps"], 1)
            for hh in range(2):
                i = nc.scalar.activation(ys[:, 16 * hh:16 * hh + 16, :].rearrange("p a b -> p (a b)"),
                                         ps[:, 5 + hh, :], ACT.Copy, scale=2.0)
            i.then_inc(S["y_ev"], 1)
            with act.Fori(0, STEPS // 2) as r:
                for i in range(2):
                    n = r * 2 + i
                    act.wait_ge(S["fx"], 1 + r * 2)
                    act.wait_ge(S["fa_ps"], n + 1)
                    nc.scalar.activation(fa[i], ps[:, i, 0:384], ACT.Copy).then_inc(S["fa_ev"], 1)
            with act.Fori(0, STEPS) as r:
                act.wait_ge(S["om_ps"], r + 1)
                for hf in range(2):
                    i = nc.scalar.activation(oms[hf][0:108, :], ps[0:108, hf, 0:384], ACT.Identity,
                                             bias=vec[0:108, 10 + hf:11 + hf])
                i.then_inc(S["om_ev"], 1)
                act.wait_ge(S["coord"], 1 + r)
                act.wait_ge(S["omt_xy"], 1 + r + 1)
                for hf in range(3):
                    i = nc.scalar.activation(sg[:, SAMP * hf:SAMP * hf + SAMP],
                                             ps[:, 2 + hf // 2, 256 * (hf % 2) + 144:256 * (hf % 2) + 216],
                                             ACT.Sigmoid)
                i.then_inc(S["om_sig"], 1)
                nc.scalar.activation(ee, ee, ACT.Abs).then_inc(S["om_abs"], 1)

            def hat(part):
                nc.scalar.activation(part, part, ACT.Abs)
                act.drain()
                return nc.scalar.activation(part, part, ACT.Relu, scale=-1.0, bias=1.0)

            def column_hats(t):
                act.wait_ge(S["dv_ready"], t + 1)
                hat(DV).then_inc(S["v_hat"], 1)

            def row_hats(t, par, j):
                act.wait_ge(S["du_ready"], t * PARTS + (j + 1))
                i = hat(HU[par][:, PS * j:PS * j + PS, :].rearrange("p s a -> p (s a)"))
                if j == PARTS - 1:
                    i.then_inc(S["u_hat"], 1)

            def evac(job, dst, src):
                act.wait_ge(S["t_ps"], job + 1)
                nc.scalar.activation(dst, src, ACT.Copy).then_inc(S["t_ev"], 1)

            def value_jobs(job):
                for j in range(3):
                    evac(job + j, valT[:, 384 * j:384 * (j + 1)], ps[:, 6 + j % 2, 0:384])

            def out_job(t, job, bank):
                if not (isinstance(t, int) and t == 0):
                    act.wait_ge(S["x_out"], t)
                act.wait_ge(S["t_ps"], job + 1)
                nc.scalar.activation(orelu, ps[:, bank, 0:128], ACT.Relu, bias=bdc).then_inc(S["t_ev"], 1)

            def tile(t, par, first=False, last=False):
                job = first_job(t)
                k = 0
                for c in range(CHUNKS):
                    if not (first and c < 2):
                        act.wait_ge(S["g_ready"], t * CHUNKS + c - 1)
                    for j in range(2):
                        evac(job + k, PTS[(2 * c + j) % 4][0:WK, :], ps[0:WK, 6 + k % 2, 0:384])
                        k += 1
                    if 3 <= c < 6 and not first:
                        evac(job + k, valT[:, 384 * (c - 3):384 * (c - 2)], ps[:, 6 + k % 2, 0:384])
                        k += 1
                    if c == 6 and not first:
                        out_job(t - 1, job + k, 6 + k % 2)
                        k += 1
                    if c == 2 and not last:
                        column_hats(t + 1)
                    if 3 <= c < 3 + PARTS and not last:
                        row_hats(t + 1, 1 - par, c - 3)
            column_hats(0)
            for j in range(PARTS):
                row_hats(0, 0, j)
            tile(0, 0, first=True)
            with act.Fori(0, (TILES - 2) // 2) as pair:
                t = pair * 2 + 1
                tile(t, 1)
                tile(t + 1, 0)
            tile(TILES - 1, 1, last=True)
            job = TILES * 28 - 4
            value_jobs(job)
            out_job(TILES - 1, job + 3, 7)

        @block.tensor
        def _(pe):
            mm = nc.tensor.matmul

            def gn_mean(n):
                pe.wait_ge(S["gn_stats"], n + 1)
                mm(ps[:, 7, 0:2], con["gmean"], t2, start=True, stop=True).then_inc(S["gn_mean"], 1)
            pe.wait_ge(S["c_in"], 16)
            pe.wait_ge(S["w_in"], W_IN)
            pe.wait_ge(S["wprep"], 1)
            for n, (src, dst, m, width) in enumerate(JOBS):
                if n >= 4:
                    pe.wait_ge(S["wt_ev"], n - 3)
                for s, col in src:
                    k = s.shape[0]
                    i = nc.tensor.transpose(ps[:, n % 4, col:col + k], s, ident[0:k, 0:k])
                i.then_inc(S["wt_ps"], 1)
            gn_mean(0)
            pe.wait_ge(S["gn_apply"], 1)
            pe.wait_ge(S["gn_dve_apply"], 1)
            with pe.Fori(0, STEPS // 4) as r:
                for i in range(4):
                    pe.wait_ge(S["cv_ev"], 1 + r * 4)
                    for t in range(9):
                        m = mm(ps[:, i, 0:384], qkvT[:, t, 0:C],
                               padm[:, bass.ds(r * 16 + (4 * i + t // 3), ROWS), t % 3:t % 3 + W],
                               start=(t == 0), stop=(t == 8))
                    m.then_inc(S["cv_ps"], 1)
            for n in range(12):
                i, kv = n // 2, n % 2
                if n >= 4:
                    pe.wait_ge(S["kv_ev"], n - 3)
                for t in range(9):
                    a, b = 16 * i + t // 3, t % 3
                    m = mm(ps[:, 4 + n % 4, 0:384], qkvT[:, t, C * (1 + kv):C * (2 + kv)],
                           padm[:, a:a + 15:2, b:b + 95:2], start=(t == 0), stop=(t == 8))
                m.then_inc(S["kv_ps"], 1)

            def scores(tr, tc, heads):
                for h in heads:
                    o = ps[:, h // 2, 256 * (h % 2):256 * (h % 2) + KEYS]
                    mm(o, Qm[tc % 2][:, h, :], kP[:, bass.ds(tr * QR, KR), QC * tc:QC * tc + KC],
                       start=True, stop=False)
                    mm(o, inrow16[:], mrow16[:, bass.ds(tr, 1), :].rearrange("p a k -> p (a k)").unsqueeze(2)
                       .broadcast_to([C, KR, KC]), start=False, stop=False)
                    i = mm(o, incol16[:], mcol16[:, tc, :].unsqueeze(1).broadcast_to([C, KR, KC]),
                           start=False, stop=True)
                return i

            def transpose_values(n, par):
                if there(n, 1):
                    pe.wait_ge(S["vt_ev"], n)
                for k, (a, b) in enumerate(((0, 128), (128, KPAD), (64, KPAD))):
                    i = nc.tensor.transpose(ps[0:b - a, 6, 128 * k:128 * k + 128], vw[par][:, a:b], ident)
                i.then_inc(S["vt_ps"], 1)

            def attend(n, par):
                J = BLOCKS // 4

                def probs(j):
                    if j == 2:
                        pe.wait_ge(S["pt_ev"], n * J + 1)
                    for q in range(4):
                        i = nc.tensor.transpose(ps[:, 4 + j % 2, 128 * q:128 * q + 128],
                                                flat[:, 128 * (4 * j + q):128 * (4 * j + q + 1)], ident)
                    i.then_inc(S["pt_ps"], 1)
                flat = Sx[par].rearrange("p h k -> p (h k)")
                pe.wait_ge(S["p_ready"], n + 1)
                if there(n, 1):
                    pe.wait_ge(S["pt_ev"], n * J)
                for j in range(J):
                    probs(j)
                if there(n, 1):
                    pe.wait_ge(S["l0_x"], n)
                pe.wait_ge(S["vt_ev"], n + 1)
                for j in range(J):
                    pe.wait_ge(S["pt_ev"], n * J + j + 1)
                    for q in range(4):
                        b = 4 * j + q
                        i = mm(ps[:, 7, 0:VW * HEADS], PT[j][:, 128 * q:128 * q + 128],
                               block_values(par, b), start=(b == 0), stop=(b == BLOCKS - 1))
                i.then_inc(S["o_ready"], 1)

            def block_values(par, b):
                return Vm[par][:, VW * HEADS * b:VW * HEADS * (b + 1)]

            def slot(tr, tc, n):
                par = tc % 2
                if there(n):
                    pe.wait_ge(S["qm_ready"], n + 1)
                    if there(n, 1):
                        pe.wait_ge(S["s_sub"], n)
                    scores(tr, tc, range(HEADS // 2))
                if there(n, 2):
                    pe.wait_ge(S["o_norm"], n - 1)
                    nc.tensor.transpose(ps[:, 7, 136:264], On, ident).then_inc(S["ot_ps"], 1)
                if there(n):
                    scores(tr, tc, range(HEADS // 2, HEADS)).then_inc(S["s_ready"], 1)
                if there(n, 2):
                    pe.wait_ge(S["ot_ev"], n - 1)
                    mm(ps[:, 7, 264:392], sqT[:, 0, :], OT, start=True, stop=True).then_inc(S["pj_ps"], 1)
                if there(n):
                    transpose_values(n, par)
                if there(n, 1):
                    attend(n - 1, 1 - par)

            pe.wait_ge(S["kv_ev"], 12)
            slots(pe, slot)
            gn_mean(1)

            pe.wait_ge(S["gn_apply"], 2)
            pe.wait_ge(S["gn_dve_apply"], 2)
            pe.wait_ge(S["l1diag"], 1)

            def message(k, bank, src):
                mm(ps[:, bank, 0:W], shiftd[:], ones[:], start=True, stop=False)
                pe.wait_ge(S["row_new"], k)
                for t in range(9):
                    m = mm(ps[:, bank, 0:W], w1T[:, t, :], rows[:, src, t:t + W], start=False, stop=(t == 8))
                m.then_inc(S["row_ps"], 1)
            message(0, 0, slice(0, 1))
            with pe.Fori(0, (H - 2) // 2) as pair:
                i = pair * 2 + 1
                message(i, 1, bass.ds(i, 1))
                message(i + 1, 0, bass.ds(i + 1, 1))
            message(H - 1, 1, slice(H - 1, H))
            with pe.Fori(0, (H - 2) // 2) as pair:
                i = pair * 2 + 1
                message(i + (H - 1), 0, bass.ds(i * -1 + (H - 1), 1))
                message(i + H, 1, bass.ds(i * -1 + (H - 2), 1))
            gn_mean(2)

            pe.wait_ge(S["gn_apply"], 3)
            pe.wait_ge(S["gn_dve_apply"], 3)
            with pe.Fori(0, STEPS // 4) as r:
                for i in range(4):
                    pe.wait_ge(S["c2_x"], 1 + r * 4)
                    for t in range(9):
                        m = mm(ps[:, i, 0:384], w2T[:, t, :],
                               padm[:, bass.ds(r * 16 + (4 * i + t // 3), ROWS), t % 3:t % 3 + W],
                               start=(t == 0), stop=(t == 8))
                    m.then_inc(S["c2_ps"], 1)
            for hh in range(2):
                m = mm(ps[:, 5 + hh, :], sqT[:, 4, :], Fmap[:, 512 * hh:512 * hh + 512], start=True, stop=True)
            m.then_inc(S["y_ps"], 1)
            gn_mean(3)
            pe.wait_ge(S["gap_in"], 1)
            mm(ps[:, 7, 0:1], sqT[:, 2, :], gapn, start=True, stop=True).then_inc(S["att_ps"], 1)

            def arm(n, i):
                pe.wait_ge(S["xg_ready"], n + 1)
                mm(ps[:, i, 0:384], sqT[:, 1, :], xg[i], start=True, stop=True).then_inc(S["fa_ps"], 1)

            def off1(n, i):
                pe.wait_ge(S["fa_ev"], n + 1)
                mm(ps[:, 2 + i, 0:384], sqT[:, 3, :], fa[i], start=True, stop=True).then_inc(S["of_ps"], 1)
            arm(0, 0)
            with pe.Fori(0, (STEPS - 2) // 2) as pair:
                r = pair * 2 + 1
                arm(r, 1)
                off1(r - 1, 0)
                arm(r + 1, 0)
                off1(r, 1)
            arm(STEPS - 1, 1)
            off1(STEPS - 2, 0)
            off1(STEPS - 1, 1)
            pe.wait_ge(S["of_ev"], STEPS)
            with pe.Fori(0, STEPS) as r:
                pe.wait_ge(S["om_ev"], 1 + r)
                for hf in range(2):
                    for t in range(9):
                        m = mm(ps[0:108, hf, 0:384], wcmT[:, t, 108 * hf:108 * hf + 108],
                               padm[:, bass.ds(r * ROWS + t // 3, ROWS), t % 3:t % 3 + W],
                               start=(t == 0), stop=(t == 8))
                m.then_inc(S["om_ps"], 1)
                pe.wait_ge(S["om_sig"], 1 + r)
                pe.wait_ge(S["omt_xy"], 1 + r)
                pe.wait_ge(S["om_ev"], 1 + r + 1)
                for i in range(3):
                    for hf in range(2):
                        m = nc.tensor.transpose(
                            ps[:, 2 + i // 2, 256 * (i % 2) + 108 * hf:256 * (i % 2) + 108 * hf + 108],
                            oms[hf][0:108, 128 * i:128 * i + 128], ident[0:108, 0:108])
                m.then_inc(S["omt_ps"], 1)

            def turn(job, k, srcs, rows_out):
                if not (isinstance(job, int) and job + k < 2):
                    pe.wait_ge(S["t_ev"], job + (k - 1))
                for j, s in enumerate(srcs):
                    i = nc.tensor.transpose(ps[0:rows_out, 6 + k % 2, 128 * j:128 * j + 128], s, ident)
                return i

            def contract(n, c, jobs_done, between=None):
                if not (isinstance(n, int) and n < 2):
                    pe.wait_ge(S["g_used"], n - 1)
                pe.wait_ge(S["t_ev"], jobs_done)
                for j in range(CH):
                    if j == CH // 2 and between:
                        between()
                    s = CH * c + j
                    i = mm(ps[:, 3 * (c % 2) + j // 2, 256 * (j % 2):256 * (j % 2) + WINS * CPG],
                           PTS[(2 * c + j // 3) % 4][0:WK, 128 * (j % 3):128 * (j % 3) + 128],
                           Fwin[:, s // TAPS, :, :].rearrange("p w c -> p (w c)"), start=True, stop=True)
                i.then_inc(S["g_ready"], 1)

            def values_of(par, job, k, j):
                turn(job, k, [val[par][:, 128 * (3 * j + i):128 * (3 * j + i) + 128] for i in range(3)],
                     C).then_inc(S["t_ps"], 1)

            def output_of(job, k):
                pe.wait_ge(S["t_ev"], job + k)
                for j in range(9):
                    i = mm(ps[:, 6 + k % 2, 0:128], wdT[:, j, :], valT[:, 128 * j:128 * j + 128],
                           start=(j == 0), stop=(j == 8))
                i.then_inc(S["t_ps"], 1)

            def tile(t, par, first=False):
                job = first_job(t)
                k = 0
                for c in range(CHUNKS):
                    n = t * CHUNKS + c
                    pe.wait_ge(S["pr_ready"], n + 1)
                    for j in range(2):
                        src = [PR[c % 2][:, WK * (3 * j + i):WK * (3 * j + i + 1)] for i in range(3)]
                        i = turn(job, k, src, WK)
                        i.then_inc(S["t_ps"], 1)
                        k += 1
                    if c == 0:
                        if not first:
                            contract(n - 1, CHUNKS - 1, job)
                    else:
                        between = None
                        if 3 <= c < 6 and not first:
                            between = lambda: values_of(1 - par, job, k, c - 3)
                        elif c == 6 and not first:
                            between = lambda: output_of(job, k)
                        if c == 3 and not first:
                            pe.wait_ge(S["summed"], t * CHUNKS)
                        contract(n - 1, c - 1, job + (chunk_job(c - 1, first) + 2), between)
                        k += 1 if between else 0
            tile(0, 0, first=True)
            with pe.Fori(0, (TILES - 2) // 2) as pair:
                t = pair * 2 + 1
                tile(t, 1)
                tile(t + 1, 0)
            tile(TILES - 1, 1)
            job = TILES * 28 - 4
            contract(TILES * CHUNKS - 1, CHUNKS - 1, job)
            pe.wait_ge(S["summed"], TILES * CHUNKS)
            for j in range(3):
                values_of(1, job, j, j)
            output_of(job, 3)

        @block.vector
        def _(v):
            V = nc.vector

            def gn_stats(n):
                v.drain()
                for i in range(18):
                    V.bn_stats(stats[:, i, :], X[:, 512 * i:512 * i + 512])
                v.drain()
                V.bn_aggr(mv, stats[:].rearrange("p a b -> p (a b)"))
                v.drain()
                V.tensor_copy(t2[:, 0:1], mv[:, 0:1])
                V.scalar_tensor_tensor(out=t2[:, 1:2], in0=mv[:, 0:1], scalar=mv[:, 0:1], in1=mv[:, 1:2],
                                       op0=ALU.mult, op1=ALU.add).then_inc(S["gn_stats"], 1)
                v.wait_ge(S["gn_mean"], n + 1)
                V.tensor_copy(gm, ps[:, 7, 0:2])
                v.drain()
                V.scalar_tensor_tensor(out=nv, in0=gm[:, 0:1], scalar=gm[:, 0:1], in1=gm[:, 1:2],
                                       op0=ALU.mult, op1=ALU.subtract)
                v.drain()
                V.tensor_scalar(var, nv, -1.0, EPS, ALU.mult, ALU.add).then_inc(S["gn_var"], 1)
                v.wait_ge(S["gn_sd"], n + 1)
                V.reciprocal(rstd, sd)
                v.drain()
                V.scalar_tensor_tensor(out=nb, in0=gm[:, 0:1], scalar=-1.0, in1=rstd, op0=ALU.mult,
                                       op1=ALU.mult).then_inc(S["gn_scale"], 1)
                v.drain()

            def gn_apply(dst):
                V.tensor_scalar(dst[:, 0:DVE_ROWS, :], Xr[:, 0:DVE_ROWS, :], rstd, nb, ALU.mult,
                                ALU.add).then_inc(S["gn_dve_apply"], 1)

            def zero_border():
                V.memset(padm[:, 0:1, :], 0.0)
                V.memset(padm[:, H + 1:H + 2, :], 0.0)
                V.memset(padm[:, 1:H + 1, 0:1], 0.0)
                V.memset(padm[:, 1:H + 1, PW - 1:PW], 0.0)
            V.memset(ones[:], 1.0)
            V.memset(tiny[:, 40:44], 0.0)
            v.wait_ge(S["c_in"], 16)
            v.wait_ge(S["w_in"], W_IN)
            V.tensor_scalar(lv, rvar, EPS, None, ALU.add).then_inc(S["l1c_var"], 1)
            V.memset(Fpad, 0.0)
            V.tensor_copy(wdr.rearrange("p (g k c) -> p g c k", g=DG, c=CPG),
                          raw["wd"].rearrange("p (g c k) -> p g c k", g=DG, c=CPG))
            V.tensor_scalar(Fmap[:], fs[:, 0, :], BATCHW[0], None, ALU.mult)
            for b in range(1, 8):
                v.drain()
                V.scalar_tensor_tensor(out=Fmap[:], in0=fs[:, b, :], scalar=BATCHW[b], in1=Fmap[:],
                                       op0=ALU.mult, op1=ALU.add)
            v.drain()
            V.tensor_copy(Fpad[:, 0:FH, 0:FH], Fmap[:].rearrange("p (a b) -> p a b", b=FH))
            v.drain()
            for w in range(WINS):
                V.tensor_copy(Fcut[:, w, :].rearrange("p (a b) -> p a b", b=WB),
                              Fpad[:, :, WSTEP * w:WSTEP * w + WB])
            v.wait_ge(S["l1c_sd"], 1)
            V.reciprocal(lrs, lsd)
            v.drain()
            V.tensor_tensor(lsc, gam, lrs, ALU.mult)
            v.drain()
            V.tensor_scalar(raw["w1"], raw["w1"], lsc, None, ALU.mult).then_inc(S["wprep"], 1)
            V.scalar_tensor_tensor(out=lsh, in0=rmean, scalar=lsc, in1=bet, op0=ALU.mult, op1=ALU.subtract)
            v.drain()
            V.tensor_scalar(shiftd[:], ident, lsh, -1.0, ALU.mult, ALU.mult).then_inc(S["l1diag"], 1)
            for a, b in ((mrow16[:].rearrange("p a b -> p (a b)"), "mrow"),
                         (mcol16[:].rearrange("p a b -> p (a b)"), "mcol"), (inrow16[:], "inrow"),
                         (incol16[:], "incol")):
                V.tensor_copy(a, con[b])
            v.wait_ge(S["x_in"], 64)
            gn_stats(0)
            v.wait_ge(S["wt_ev"], len(JOBS))
            V.tensor_tensor(qkvT.rearrange("p t o -> p o t"), raw["qkv"].rearrange("p (o t) -> p o t", t=9),
                            con["own3"].unsqueeze(2).broadcast_to([C, 3 * C, 9]), ALU.mult)
            v.drain()
            zero_border()
            v.drain().then_inc(S["raw_done"], 1)
            gn_apply(padm[:, 1:H + 1, 1:W + 1])
            with v.Fori(0, STEPS // 4) as r:
                for i in range(4):
                    n = r * 4 + i
                    v.wait_ge(S["cv_ps"], n + 1)
                    V.tensor_scalar(Q[:, bass.ts(n, 384)], ps[:, i, 0:384], qb, None,
                                    ALU.add).then_inc(S["cv_ev"], 1)
            v.wait_ge(S["kv_ps"], 12)
            for b in range(2):
                V.memset(Sx[b][:, :, KEYS:KPAD], 0.0)
                V.memset(Vm[b], 0.0)
            v.drain()
            for b in range(2):
                vm = Vm[b].rearrange("p (m x) -> p m x", x=PAIR)
                B = VW * HEADS
                V.memset(vm[:, :, HD:HD + 1], 1.0)
                V.memset(vm[0:64, :, B + HD:B + HD + 1], 1.0)
                V.memset(vm[64:C, :, B + VW + HD:B + VW + HD + 1], 1.0)
                V.memset(vm[:, :, 2 * B + VW + HD:2 * B + VW + HD + 1], 1.0)
            v.drain().then_inc(S["vm_ready"], 1)

            def softmax_max(n, par):
                sc = ps[:, 0:4, :].rearrange("p b (h k) -> p (b h) k", h=2)[:, :, 0:KEYS]
                v.drain()
                v.wait_ge(S["s_ready"], n + 1)
                V.tensor_reduce(smax, sc, AX.X, ALU.max)
                v.drain()
                V.tensor_tensor(Sx[par][:, :, 0:KEYS], sc, smax.unsqueeze(2).broadcast_to([C, HEADS, KEYS]),
                                ALU.subtract).then_inc(S["s_sub"], 1)

            def normalise(n):
                O = ps[:, 7, 0:VW * HEADS].rearrange("p (h d) -> p h d", h=HEADS)
                v.wait_ge(S["o_ready"], n + 1)
                V.reciprocal(srec.unsqueeze(2), O[:, :, HD:HD + 1])
                v.drain()
                V.tensor_tensor(On.rearrange("p (h d) -> p h d", h=HEADS), O[:, :, 0:HD],
                                srec.unsqueeze(2).broadcast_to([C, HEADS, HD]), ALU.mult).then_inc(S["o_norm"], 1)

            def add_attention(tr, tc, n):
                v.wait_ge(S["pj_ps"], n + 1)
                xw = Xr[:, bass.ds(tr * 8, 8), 16 * tc:16 * tc + 16]
                V.scalar_tensor_tensor(out=xw, in0=ps[:, 7, 264:392].rearrange("p (a b) -> p a b", b=16),
                                       scalar=pjb, in1=xw, op0=ALU.add, op1=ALU.add).then_inc(S["l0_x"], 1)

            def slot(tr, tc, n):
                if there(n, 2):
                    add_attention(*before(tr, tc, 2), n - 2)
                if there(n):
                    softmax_max(n, tc % 2)
                if there(n, 1):
                    normalise(n - 1)
            slots(v, slot)

            gn_stats(1)
            V.memset(rows[:, :, 0:4], 0.0)
            V.memset(rows[:, :, 4 + W:RP], 0.0)
            gn_apply(rows[:, :, 4:4 + W])
            v.drain()
            v.wait_ge(S["gn_apply"], 2)

            def add_row(k, bank, dst):
                v.wait_ge(S["row_ps"], k + 1)
                rw = rows[:, dst, 4:4 + W]
                V.scalar_tensor_tensor(out=rw, in0=ps[:, bank, 0:W].unsqueeze(1), scalar=0.0, in1=rw, op0=ALU.max,
                                       op1=ALU.add).then_inc(S["row_new"], 1)
            add_row(0, 0, slice(1, 2))
            with v.Fori(0, (H - 2) // 2) as pair:
                i = pair * 2 + 1
                add_row(i, 1, bass.ds(i + 1, 1))
                add_row(i + 1, 0, bass.ds(i + 2, 1))
            add_row(H - 1, 1, slice(H - 2, H - 1))
            with v.Fori(0, (H - 2) // 2) as pair:
                i = pair * 2 + 1
                add_row(i + (H - 1), 0, bass.ds(i * -1 + (H - 2), 1))
                add_row(i + H, 1, bass.ds(i * -1 + (H - 3), 1))
            v.drain()
            V.tensor_tensor(Xr, Xr, rows[:, :, 4:4 + W], ALU.add)
            gn_stats(2)
            zero_border()
            gn_apply(padm[:, 1:H + 1, 1:W + 1])
            with v.Fori(0, STEPS // 4) as r:
                for i in range(4):
                    n = r * 4 + i
                    v.wait_ge(S["c2_ps"], n + 1)
                    xw = X[:, bass.ts(n, 384)]
                    V.scalar_tensor_tensor(out=xw, in0=ps[:, i, 0:384], scalar=b2, in1=xw, op0=ALU.add,
                                           op1=ALU.add).then_inc(S["c2_x"], 1)
            gn_stats(3)
            V.scalar_tensor_tensor(out=gapn, in0=mv[:, 0:1], scalar=rstd, in1=nb, op0=ALU.mult,
                                   op1=ALU.add).then_inc(S["gap_in"], 1)
            third = 1.0 / 3.0

            def upsample(src, diff, dst):
                V.tensor_tensor(diff[:, 0:FH - 1], src[:, 1:FH], src[:, 0:FH - 1], ALU.subtract)
                V.tensor_copy(dst[:, 1:3 * FH:3], src)
                V.tensor_copy(dst[:, 0:1], src[:, 0:1])
                V.tensor_copy(dst[:, 3 * FH - 1:3 * FH], src[:, FH - 1:FH])
                v.drain()
                for k in (1, 2):
                    V.scalar_tensor_tensor(out=dst[:, 1 + k:3 * FH - 1:3], in0=diff[:, 0:FH - 1],
                                           scalar=k * third, in1=src[:, 0:FH - 1], op0=ALU.mult, op1=ALU.add)
                v.drain()
            v.wait_ge(S["y_ev"], 1)
            upsample(ys, yd, yr)
            upsample(yr.rearrange("p a b -> p b a"), cd.rearrange("p a b -> p b a"),
                     padm[:, 1:H + 1, 1:W + 1].rearrange("p a b -> p b a"))
            v.wait_ge(S["att_sg"], 1)
            V.tensor_scalar(att1, att, 1.0, None, ALU.add)
            v.drain()
            V.tensor_tensor(s3, rstd, att1, ALU.mult)
            V.tensor_tensor(b3, nb, att1, ALU.mult)
            v.drain()

            def gated(n, i):
                V.tensor_scalar(xg[i], X[:, bass.ts(n, 384)], s3, b3, ALU.mult, ALU.add).then_inc(S["xg_ready"], 1)

            def add_arm(n, i):
                v.wait_ge(S["fa_ev"], n + 1)
                xw = X[:, bass.ts(n, 384)]
                V.tensor_tensor(xw, xw, fa[i], ALU.add)
                v.wait_ge(S["of_ps"], n + 1)
                m = padm[:, bass.ds(n * ROWS + 1, ROWS), 1:W + 1]
                V.tensor_tensor(m, ps[:, 2 + i, 0:384].rearrange("p (a b) -> p a b", b=W), m,
                                ALU.add).then_inc(S["of_ev"], 1)
                v.drain().then_inc(S["fx"], 1)
            gated(0, 0)
            gated(1, 1)
            with v.Fori(0, (STEPS - 2) // 2) as pair:
                for i in range(2):
                    add_arm(pair * 2 + i, i)
                    gated(pair * 2 + (2 + i), i)
            add_arm(STEPS - 2, 0)
            add_arm(STEPS - 1, 1)
            v.drain()
            by = con["basey"].rearrange("p (i s) -> p i s", i=3)
            bx = con["basex"].rearrange("p (i s) -> p i s", i=3)
            with v.Fori(0, STEPS) as r:
                pt = ps[:, 2:4, :].rearrange("p b (i s) -> p (b i) s", i=2)[:, 0:3, :]
                v.wait_ge(S["omt_ps"], r + 1)
                V.tensor_tensor(yx[:, 0, :].rearrange("p (i s) -> p i s", i=3), pt[:, :, 0:SAMP], by, ALU.add)
                V.tensor_tensor(yx[:, 1, :].rearrange("p (i s) -> p i s", i=3), pt[:, :, SAMP:2 * SAMP], bx,
                                ALU.add)
                v.drain()
                V.tensor_scalar(con["basey"], con["basey"], float(ROWS), None, ALU.add)
                V.tensor_scalar(ee, yx, -47.5, None, ALU.add).then_inc(S["omt_xy"], 1)
                V.tensor_scalar(uv, yx, 1.0, float(H - 2), ALU.max, ALU.min)
                v.drain()
                V.tensor_scalar(uv, uv, 1.0, third, ALU.subtract, ALU.mult)
                v.drain()
                V.tensor_copy(UL[:, bass.ts(r, 216)], uv[:, 0, :])
                V.tensor_scalar(wja, uv[:, 1, :], third, -0.5, ALU.mult, ALU.add)
                v.drain()
                V.tensor_scalar(wja, wja, ROUND, None, ALU.add)
                v.drain()
                V.tensor_scalar(wja, wja, -ROUND, None, ALU.add)
                v.drain()
                V.scalar_tensor_tensor(out=VL[:, bass.ts(r, 216)], in0=wja, scalar=-float(WSTEP),
                                       in1=uv[:, 1, :], op0=ALU.mult, op1=ALU.add)
                V.tensor_copy(WI[:, bass.ts(r, 216)], wja)
                v.wait_ge(S["om_sig"], 1 + r + 1)
                v.wait_ge(S["om_abs"], r + 1)
                V.tensor_scalar(ee, ee, -1.0, 48.5, ALU.mult, ALU.add)
                v.drain()
                V.tensor_scalar(ee, ee, 0.0, 1.0, ALU.max, ALU.min)
                v.drain()
                V.tensor_tensor(ma, sg, ee[:, 0, :], ALU.mult)
                v.drain()
                V.tensor_tensor(MS[:, bass.ts(r, 216)], ma, ee[:, 1, :], ALU.mult).then_inc(S["coord"], 1)
                v.drain()

            oh3 = OH.rearrange("p (s w) -> p s w", w=WINS)

            def window_sum(n, par, c):
                v.wait_ge(S["g_used"], n + 1)
                V.tensor_reduce(
                    val[par][:, CH * CPG * c:CH * CPG * (c + 1)].rearrange("p (s c) -> p s c", s=CH),
                    GM[c % 2].rearrange("p (s w c) -> p s c w", s=CH, w=WINS), AX.X,
                    ALU.add).then_inc(S["summed"], 1)

            def one_hot(t, half):
                k = SAMP // 2
                V.tensor_tensor(oh3[:, k * half:k * half + k, :],
                                WI[:, bass.ds(t * SAMP + k * half, k)].unsqueeze(2).broadcast_to([C, k, WINS]),
                                con["iota"][:, 0:WINS].unsqueeze(1).broadcast_to([C, k, WINS]),
                                ALU.is_equal).then_inc(S["onehot"], 1)

            def tile(t, par, first=False, last=False):
                for c in range(CHUNKS):
                    n = t * CHUNKS + c
                    if c % (CHUNKS // 2) == 0:
                        v.wait_ge(S["onehot"], t * 2 + (1 + c // (CHUNKS // 2)))
                    if not (first and c < 2):
                        v.wait_ge(S["summed"], n - 1)
                    v.wait_ge(S["g_ready"], n + 1)
                    V.tensor_tensor(
                        GM[c % 2].rearrange("p (s w c) -> p s w c", s=CH, w=WINS),
                        ps[:, 3 * (c % 2):3 * (c % 2) + 3, :].rearrange("p b (s n) -> p (b s) n", s=2)
                        [:, :, 0:WINS * CPG].rearrange("p s (w c) -> p s w c", w=WINS),
                        oh3[:, CH * c:CH * c + CH, :].unsqueeze(3).broadcast_to([C, CH, WINS, CPG]),
                        ALU.mult).then_inc(S["g_used"], 1)
                    if c >= 1:
                        window_sum(n - 1, par, c - 1)
                    elif not first:
                        window_sum(n - 1, 1 - par, CHUNKS - 1)
                    if c == 2:
                        v.wait_ge(S["g_used"], n)
                        one_hot(t, 1)
                    if c == 8 and not last:
                        v.wait_ge(S["g_used"], n)
                        one_hot(t + 1, 0)
            one_hot(0, 0)
            tile(0, 0, first=True)
            with v.Fori(0, (TILES - 2) // 2) as pair:
                t = pair * 2 + 1
                tile(t, 1)
                tile(t + 1, 0)
            tile(TILES - 1, 1, last=True)
            window_sum(TILES * CHUNKS - 1, 1, CHUNKS - 1)


_INS = ["x", "L0_conv_qkv_w", "L0_conv_qkv_b", "L0_conv_proj_w", "L0_conv_proj_b", "L1_conv_conv_w",
        "L1_conv_gamma", "L1_conv_beta", "L1_conv_run_mean", "L1_conv_run_var", "L2_conv_weight", "L2_conv_bias",
        "L3_conv_feat_s", "L3_conv_w_atten", "L3_conv_w_fsm", "L3_conv_w_off", "L3_conv_w_cm", "L3_conv_b_cm",
        "L3_conv_w_dcn", "L3_conv_b_dcn"]


def kernel(**inputs):
    import concourse.bacc as bacc
    from concourse.bass_utils import run_bass_kernel_spmd

    nc = bacc.Bacc("TRN2", target_bir_lowering=False, num_devices=1)
    arrays, d = {}, {}
    for name in _INS:
        a = np.ascontiguousarray(inputs[name])
        arrays[f"in_{name}"] = a
        d[name] = nc.dram_tensor(f"in_{name}", a.shape, mybir.dt.from_np(a.dtype), kind="ExternalInput").ap()
    made = shape_constants()
    arrays["in_consts"] = np.ascontiguousarray(np.concatenate([made[n] for n in CONSTS], axis=1))
    consts = nc.dram_tensor("in_consts", arrays["in_consts"].shape, F32, kind="ExternalInput").ap()
    out = nc.dram_tensor("out_0_dram", (1, C, H, W), F32, kind="ExternalOutput").ap()
    build_program(nc, d, consts, out)
    r = run_bass_kernel_spmd(nc, [arrays], core_ids=[0])
    return r.results[0]["out_0_dram"]
```

```python
from contextlib import ExitStack

import numpy as np

import concourse.bass as bass
from concourse import mybir

ALU = mybir.AluOpType
ACT = mybir.ActivationFunctionType
AX = mybir.AxisListType
F32 = mybir.dt.float32

C, H, W = 128, 96, 96
PIX = H * W
PW = W + 2
ROWS = 4
STEPS = H // ROWS
BAND = 16
BANDS = H // BAND
HEADS, HD, KS = 8, 16, 8
SUB = 48
QR, QC = 4, 8
TR, TC = SUB // QR, SUB // QC
KR, KC = QR + KS, QC + KS - 1
KEYS = KR * KC
KPAD = 192
BLOCKS = HEADS * KPAD // 128
VW = HD + 1
TILES0 = TR * TC
PADK = 4
KPH, KPW = PADK + SUB + 4, 3 + SUB + 4
FAR = -float(2 ** 99)
RP = W + 8
FH = 32
WA, WB = FH, 4
WSTEP = WB - 1
WINS = -(-(FH - 1) // WSTEP)
WK = WA * WB
FPW = WSTEP * WINS + 1
ROUND = 1.5 * 2 ** 23
DG, TAPS = 8, 9
SAMP = DG * TAPS
TILES = PIX // 128
OUT_PARTS = 8
CH = 6
PARTS = 8
PS = SAMP // PARTS
CHUNKS = SAMP // CH
CPG = C // DG
EPS = 1e-5


def attention_masks():
    row = np.full((C, TR, KR), 0.0, np.float32)
    col = np.full((C, TC, KC), 0.0, np.float32)
    for q in range(C):
        a, b = (q // 16) // 2, (q % 16) // 2
        for t in range(TR):
            start = min(max(QR * t + a - 3, 0), SUB - KS)
            for r in range(KR):
                if not start <= QR * t - PADK + r < start + KS:
                    row[q, t, r] = FAR
        for t in range(TC):
            start = min(max(QC * t + b - 3, 0), SUB - KS)
            for r in range(KC):
                if not start <= QC * t - 3 + r < start + KS:
                    col[q, t, r] = FAR
    return row, col


def shape_constants():
    p = np.arange(C)
    out = {}
    out["ident"] = np.eye(C, dtype=np.float32)
    out["gmean"] = (p[:, None] // 4 == p[None, :] // 4).astype(np.float32) / 4
    o = np.arange(3 * C)
    out["own3"] = (o[None, :] // 3 == p[:, None]).astype(np.float32)
    out["headq"] = (p[:, None] // HD == np.arange(HEADS)[None, :]).astype(np.float32) * HD ** -0.5
    row, col = attention_masks()
    out["mrow"], out["mcol"] = row.reshape(C, -1), col.reshape(C, -1)
    lin = 128 * np.arange(3)[None, :, None] + p[:, None, None]
    k = (np.arange(SAMP) % TAPS)[None, None, :]
    out["basey"] = (lin // W + k // 3 - 1).astype(np.float32).reshape(C, -1)
    out["basex"] = (lin % W + k % 3 - 1).astype(np.float32).reshape(C, -1)
    out["iota"] = np.tile(np.arange(WA, dtype=np.float32)[None, :], (C, 1))
    return out


CONSTS = ["ident", "gmean", "own3", "headq", "mrow", "mcol", "basey", "basex", "iota"]
CWIDTH = dict(ident=C, gmean=C, own3=3 * C, headq=HEADS, mrow=TR * KR, mcol=TC * KC,
              basey=3 * SAMP, basex=3 * SAMP, iota=WA)
BATCHW = [1 - abs(i - 3.5) / 8 for i in range(8)]
BATCHW = [w / sum(BATCHW) for w in BATCHW]


def build_program(nc, d, consts, out):
    with ExitStack() as ctx:
        def sb(name, shape, dt=F32):
            return ctx.enter_context(nc.sbuf_tensor(name, shape, dt))

        def sem(name):
            return ctx.enter_context(nc.semaphore(name))

        X = sb("X", [C, PIX])
        pad = sb("pad", [C, H * RP])
        work = sb("work", [C, 22000])
        w1T = sb("w1T", [C, TAPS, C])
        wofs = sb("wofs", [C, C])
        w2T = sb("w2T", [C, TAPS, C])
        wcmT = sb("wcmT", [C, TAPS, 3 * SAMP])
        wdT = sb("wdT", [C, TAPS, C])
        sqT = sb("sqT", [C, 5, C])
        Fwin = sb("Fwin", [WK, DG, WINS, CPG])
        cst = sb("cst", [C, sum(CWIDTH.values())])
        vec = sb("vec", [C, 12])
        qw = sb("qw", [C, TAPS])
        wextra = sb("wextra", [C, 2 * 3 * SAMP])
        mask = [sb(f"mask{i}", [C, KR, KC]) for i in range(2)]
        tiny = sb("tiny", [C, 64])
        stats = sb("stats", [C, H, 6])
        shiftd = sb("shiftd", [C, C])
        ones = sb("ones", [C, W])
        ps = ctx.enter_context(nc.psum_tensor("ps", [C, 8, 512], F32))

        off = 0
        con = {}
        for name in CONSTS:
            con[name] = cst[:, off:off + CWIDTH[name]]
            off += CWIDTH[name]
        ident = con["ident"]

        Xr = X[:].rearrange("p (h w) -> p h w", w=W)
        padm = pad[:, 0:(H + 2) * PW].rearrange("p (h w) -> p h w", w=PW)
        rows = pad[:].rearrange("p (h w) -> p h w", w=RP)

        Q = work[:, 0:PIX]
        Qr = Q.rearrange("p (h w) -> p h w", w=W)
        kP = work[:, PIX:PIX + KPH * KPW].rearrange("p (h w) -> p h w", w=KPW)
        o2 = PIX + KPH * KPW
        vP = work[:, o2:o2 + KPH * KPW].rearrange("p (h w) -> p h w", w=KPW)
        o3 = o2 + KPH * KPW
        kvT = [w1T, w2T]
        raw = {"kv": work[:, 0:2 * C * TAPS], "w1": Fwin[:].rearrange("p g w c -> p (g w c)")[:, 0:TAPS * C],
               "w2": wdT[:].rearrange("p a b -> p (a b)")}
        fs = work[:, 0:8 * FH * FH].rearrange("p (b n) -> p b n", b=8)
        Fpad = work[:, 8192:8192 + FH * FPW].rearrange("p (h w) -> p h w", w=FPW)
        wdr = work[:, 9600:9600 + 1152]
        Fcut = work[:, 10752:10752 + WINS * WK].rearrange("p (w k) -> p w k", w=WINS)
        o4 = 10752 + WINS * WK
        for name in ("wd", "cma", "cmb"):
            raw[name] = work[:, o4:o4 + TAPS * C]
            o4 += TAPS * C
        o5 = o3 + HEADS * (3 * (HD + 1) * HEADS + 2 * (HD + 1))
        for name, n in (("fsm", C), ("att", C), ("off", 2 * C), ("proj", C)):
            raw[name] = work[:, o5:o5 + n]
            o5 += n
        BW = (BAND + 2) * PW
        band = [wcmT[:].rearrange("p a b -> p (a b)")[:, 0:BW], work[:, o5:o5 + BW]]
        assert o5 + BW <= 22000
        Fmap = sb("Fmap", [C, FH * FH])
        ao = [0]

        def carve(n, base=pad):
            v = base[:, ao[0]:ao[0] + n]
            ao[0] += n
            return v
        Qm = [carve(HEADS * 128).rearrange("p (h q) -> p h q", h=HEADS) for _ in range(2)]
        vw = [carve(KPAD) for _ in range(2)]
        Sx = [carve(HEADS * KPAD).rearrange("p (h k) -> p h k", h=HEADS) for _ in range(2)]
        PT = [carve(512) for _ in range(BLOCKS // 4)]
        On = carve(128)
        OT = carve(128)
        smax = carve(HEADS)
        srec = carve(HEADS)
        assert ao[0] <= H * RP
        PAIR = 3 * VW * HEADS + 2 * VW
        Vm = [work[:, o3 + HEADS // 2 * PAIR * i:o3 + HEADS // 2 * PAIR * (i + 1)] for i in range(2)]
        w2U = work[:, 17408 + 8 * ROWS * PW:17408 + 8 * ROWS * PW + 6 * C].rearrange("p (k x o) -> p k x o", k=2, x=3)
        R2 = 2 * ROWS
        rows2 = [work[:, 17408 + 4 * ROWS * PW * i:17408 + 4 * ROWS * PW * (i + 1)]
                 .rearrange("p (k a w) -> p k a w", k=4, w=PW) for i in range(2)]
        Xp = X[:].rearrange("p (a e w) -> p a e w", e=2, w=W)
        padp = pad[:, 0:(H + 2) * PW].rearrange("p (a e w) -> p a e w", e=2, w=PW)
        Ux = [Fmap[:, 216 * i:216 * i + 216] for i in range(4)] + [wextra[:, 216 * i:216 * i + 216] for i in range(2)]
        w3U = [Ux[0:3], Ux[3:6]]
        n3 = ROWS // 2 * PW
        sqf = sqT[:].rearrange("p a b -> p (a b)")
        stf = stats[:].rearrange("p a b -> p (a b)")
        rows3 = [[sqf[:, 0:n3], sqf[:, n3:2 * n3], sqf[:, 2 * n3:3 * n3], pad[:, (H + 2) * PW:(H + 2) * PW + n3]],
                 [stf[:, 0:n3], stf[:, n3:2 * n3], work[:, 21600:21600 + n3], work[:, 21600 + n3:21600 + 2 * n3]]]
        rows3 = [[m.rearrange("p (a w) -> p a w", w=PW) for m in b] for b in rows3]
        yr = work[:, 0:H * FH].rearrange("p (h w) -> p h w", w=FH)
        ys = work[:, 3072:3072 + FH * FH].rearrange("p (h w) -> p h w", w=FH)
        yd = work[:, 4096:4096 + FH * FH].rearrange("p (h w) -> p h w", w=FH)
        cd = work[:, 5120:5120 + H * FH].rearrange("p (h w) -> p h w", w=FH)
        Y = work[:, 8192:8192 + PIX].rearrange("p (h w) -> p h w", w=W)
        xg = [work[:, 8192 + PIX + 384 * i:8192 + PIX + 384 * (i + 1)] for i in range(2)]
        NS = TILES * SAMP
        UL, VL, MS, WI = (work[:, i * NS:(i + 1) * NS] for i in range(4))
        flat1 = w1T[:].rearrange("p a b -> p (a b)")
        flat2 = w2T[:].rearrange("p a b -> p (a b)")
        oms = [flat1[:, 384 * i:384 * (i + 1)] for i in range(2)]
        yx = flat2[:, 0:432].rearrange("p (a n) -> p a n", a=2)
        ee = flat2[:, 432:864].rearrange("p (a n) -> p a n", a=2)
        sg = flat1[:, 768:984]
        wja = work[:, 4 * NS:4 * NS + 216]
        uv = work[:, 4 * NS + 216:4 * NS + 648].rearrange("p (a n) -> p a n", a=2)
        ma = work[:, 4 * NS + 648:4 * NS + 864]
        ao[0] = 0
        HU = [carve(SAMP * WA).rearrange("p (s a) -> p s a", a=WA) for _ in range(2)]
        DV = carve(SAMP * WB)
        HV = [carve(SAMP * WB).rearrange("p (s a) -> p s a", a=WB) for _ in range(2)]
        PR = [carve(CH * WK) for _ in range(2)]
        PTS = [carve(384) for _ in range(4)]
        val0 = carve(SAMP * CPG)
        mst = carve(SAMP)
        orelu = carve(128)
        assert ao[0] <= H * RP
        val = [val0, work[:, 4 * NS:4 * NS + SAMP * CPG]]
        valT = flat1
        flatc = wcmT[:].rearrange("p a b -> p (a b)")
        GM = [flat2[:, 0:CH * WINS * CPG], flatc[:, 0:CH * WINS * CPG]]
        OH = flatc[:, CH * WINS * CPG:CH * WINS * CPG + SAMP * WINS]

        names = """x_in0 x_in1 x_in2 x_in3 w_in c_in f_in zeroed
        gn_stats gn_mean gn_var gn_sd gn_apply gn_dve_apply l1c_var l1c_sd
        kvw_ready wt_ps wt_ev wprep fs_scaled f_cut l1diag
        band_ps band_copied band_ready q_ready kv_ps kv_ev
        vm_zeroed vm_ready qm_ready s_ready s_read vt_ps vt_ev s_sub p_ready pt_ps pt_ev o_ready o_norm ot_ps ot_ev pj_ps l0_x
        row_ps row_new
        u2_sums u2_ready r2_ready c2_ps c2_x gap_in att_ps att_sg gn_scale y_ps y_ev u3_sums u3_ready r3_ready xg_ready arm_ps arm_added
        om_ps om_act om_ev omt_ps omt_xy om_sig om_abs coord
        pr_ready t_ps t_ev g_ready g_used onehot summed du_ready dv_ready u_hat v_hat x_out stored""".split()
        S = {n: sem(n) for n in names}
        PRIMED = "coord om_sig omt_ps omt_xy".split()
        AHEAD = 3
        TURNS = (0, 4, 6)
        UNROLL = 6

        def offset_steps(e, step):
            for i in range(UNROLL):
                step(i, i)
            with e.Fori(1, STEPS // UNROLL) as group:
                for i in range(UNROLL):
                    step(group * UNROLL + i, i)

        block = ctx.enter_context(nc.Block())

        def weight_jobs():
            jobs = []
            for src, dst in (("w1", w1T), ("w2", w2T)):
                v = raw[src].rearrange("p (c t) -> p c t", t=9)
                for j in range(3):
                    jobs.append(([(v[:, :, 3 * j + i], 128 * i) for i in range(3)],
                                 dst[:, 3 * j:3 * j + 3, :].rearrange("p a b -> p (a b)"), C, 384))
            ro = raw["off"]
            jobs.append(([(raw["proj"], 0), (raw["fsm"], 128), (raw["att"], 256)],
                         sqT[:, 0:3, :].rearrange("p a b -> p (a b)"), C, 384))
            jobs.append(([(ro[:, 0:C], 0), (ro[:, C:2 * C], 128)],
                         sqT[:, 3:5, :].rearrange("p a b -> p (a b)"), C, 256))
            early = len(jobs)
            for j in range(3):
                jobs.append(([(wdr[:, 128 * (3 * j + i):128 * (3 * j + i + 1)], 128 * i) for i in range(3)],
                             wdT[:, 3 * j:3 * j + 3, :].rearrange("p a b -> p (a b)"), C, 384))
            va = raw["cma"].rearrange("p (c t) -> p c t", t=9)
            vb = raw["cmb"].rearrange("p (c t) -> p c t", t=9)
            for j in range(5):
                ts = [t for t in (2 * j, 2 * j + 1) if t < 9]
                src = []
                for n, t in enumerate(ts):
                    src += [(va[:, :, t], 216 * n), (vb[0:88, :, t], 216 * n + 128)]
                jobs.append((src, wcmT[:, ts[0]:ts[-1] + 1, :].rearrange("p a b -> p (a b)"), C, 216 * len(ts)))
            for j in range(3):
                src = []
                ws = range(4 * j, min(4 * j + 4, WINS))
                for i, w in enumerate(ws):
                    src.append((Fcut[:, w, :], 128 * i))
                jobs.append((src, Fwin[:, :, ws[0]:ws[-1] + 1, :].rearrange("p g w c -> p w g c"), None,
                             128 * len(ws)))
            return jobs, early
        JOBS, EARLY = weight_jobs()
        LATE_STEPS = 12
        assert len(JOBS) - EARLY <= LATE_STEPS

        def job_bank(n):
            return n % 4 if n < EARLY else 2 + n % 4

        EXTRA = (2, 4, 6, 8)

        def first_job(t):
            return 0 if isinstance(t, int) and t == 0 else t * 28 - 4

        def chunk_job(c, first):
            return 2 * c + (0 if first else sum(c > e for e in EXTRA))

        def slots(e, slot):
            for tc in range(TC):
                slot(0, tc, tc)
            with e.Fori(1, TR) as tr:
                for tc in range(TC):
                    slot(tr, tc, tr * TC + tc)
            slot(TR, 0, TILES0)
            slot(TR, 1, TILES0 + 1)

        L0_ORDER = [(0, None), (None, 0)]
        for b in range(1, BANDS):
            L0_ORDER += [(b, None), (None, 2 * b - 1), (None, 2 * b)]
        L0_ORDER.append((None, 2 * BANDS - 1))
        BAND_ROWS = [(lo, min(lo + 5, BAND + 2)) for lo in range(0, BAND + 2, 5)]

        def before(tr, tc, k):
            return (tr, tc - k) if tc >= k else (tr - 1, tc - k + TC)

        def there(n, k=0):
            return not isinstance(n, int) or 0 <= n - k < TILES0

        @block.sync
        def _(sp):
            for n in PRIMED:
                sp.sem_inc(S[n], 1)
            for n in ("om_ps", "om_ev"):
                sp.sem_inc(S[n], AHEAD)
            xf = d["x"].rearrange("a c h w -> (a c) (h w)")
            for h in range(4):
                sp.dma_start(X[:, 2304 * h:2304 * (h + 1)], xf[:, 2304 * h:2304 * (h + 1)]).then_inc(S[f"x_in{h}"], 16)
            sp.dma_start(cst[:], consts).then_inc(S["c_in"], 16)
            sp.dma_start(raw["kv"], d["L0_conv_qkv_w"].rearrange("o a b c -> (o a b c)")[C * TAPS:3 * C * TAPS]
                         .partition_broadcast(C)).then_inc(S["c_in"], 16)
            sp.dma_start(qw[:], d["L0_conv_qkv_w"].rearrange("o a b c -> o (a b c)")[0:C, :]).then_inc(S["c_in"], 16)
            sp.dma_start(vec[:, 0:3], d["L0_conv_qkv_b"].rearrange("(t c) -> c t", t=3),
                         allow_slow_non_contiguous=True).then_inc(S["c_in"], 16)
            sp.dma_start(raw["w1"], d["L1_conv_conv_w"].rearrange("o c t -> o (c t)")).then_inc(S["w_in"], 16)
            sp.dma_start(raw["w2"], d["L2_conv_weight"].rearrange("o c a b -> o (c a b)")).then_inc(S["w_in"], 16)
            sp.dma_start(raw["fsm"], d["L3_conv_w_fsm"]).then_inc(S["w_in"], 16)
            sp.dma_start(raw["att"], d["L3_conv_w_atten"]).then_inc(S["w_in"], 16)
            sp.dma_start(raw["off"], d["L3_conv_w_off"]).then_inc(S["w_in"], 16)
            sp.dma_start(raw["proj"], d["L0_conv_proj_w"].rearrange("o c a b -> o (c a b)")).then_inc(S["w_in"], 16)
            for i, n in enumerate(("L0_conv_proj_b", "L1_conv_gamma", "L1_conv_beta", "L1_conv_run_mean",
                                   "L1_conv_run_var", "L2_conv_bias", "L3_conv_b_dcn")):
                sp.dma_start(vec[:, 3 + i:4 + i], d[n].rearrange("(c a) -> c a", a=1)).then_inc(S["w_in"], 16)
            bcm = d["L3_conv_b_cm"].rearrange("(a c) -> c a", a=2)
            sp.dma_start(vec[0:108, 10:12], bcm, allow_slow_non_contiguous=True).then_inc(S["w_in"], 16)
            sp.wait_ge(S["l0_x"], TILES0)
            sp.dma_start(fs, d["L3_conv_feat_s"].rearrange("b c h w -> c b (h w)")).then_inc(S["f_in"], 16)
            sp.dma_start(raw["wd"], d["L3_conv_w_dcn"].rearrange("o c a b -> o (c a b)")).then_inc(S["f_in"], 16)
            cm = d["L3_conv_w_cm"].rearrange("o c a b -> o (c a b)")
            sp.dma_start(raw["cma"], cm[0:C, :]).then_inc(S["f_in"], 16)
            sp.dma_start(raw["cmb"][0:88, :], cm[C:216, :]).then_inc(S["f_in"], 16)
            o = out.rearrange("a c h w -> (a c) (h w)")
            for k in range(OUT_PARTS):
                sp.wait_ge(S["x_out"], TILES // OUT_PARTS * (k + 1))
                n = PIX // OUT_PARTS
                sp.dma_start(o[:, n * k:n * k + n], X[:, n * k:n * k + n]).then_inc(S["stored"], 16)
            sp.wait_ge(S["stored"], 16 * OUT_PARTS)
        C_IN, W_IN, F_IN = 16 * 4, 16 * 14, 16 * 4
        qb, kb, vb_ = vec[:, 0:1], vec[:, 1:2], vec[:, 2:3]
        pjb, gam, bet, rmean, rvar = (vec[:, i:i + 1] for i in range(3, 8))
        b2, bdc = vec[:, 8:9], vec[:, 9:10]
        T = lambda i, n=1: tiny[:, i:i + n]
        mv, t2, gm, nv, var, sd, rstd, nb = T(0, 2), T(2, 2), T(4, 2), T(6), T(7), T(8), T(9), T(10)
        s3, b3, gapn, att, att1 = T(11), T(12), T(13), T(14), T(15)
        lv, lsd, lrs, lsc, lsh = T(16), T(17), T(18), T(19), T(20)
        DVE_ROWS = 60

        @block.gpsimd
        def _(g):
            nc.gpsimd.memset(kP, 0.0)
            nc.gpsimd.memset(vP, 0.0).then_inc(S["zeroed"], 1)
            g.wait_ge(S["c_in"], C_IN)
            for kv in range(2):
                i = nc.gpsimd.tensor_tensor(
                    kvT[kv][:].rearrange("p t o -> p o t"),
                    raw["kv"][:, TAPS * C * kv:TAPS * C * (kv + 1)].rearrange("p (o t) -> p o t", t=TAPS),
                    con["own3"][:, C * (kv + 1):C * (kv + 2)].unsqueeze(2).broadcast_to([C, C, TAPS]), ALU.mult)
            i.then_inc(S["kvw_ready"], 1)
            for b in range(2):
                i = nc.gpsimd.memset(Vm[b], 0.0)
            i.then_inc(S["vm_zeroed"], 1)
            g.wait_ge(S["kv_ev"], 12)
            for b in range(2):
                nc.gpsimd.memset(vw[b][:, KEYS:KPAD], 0.0)

            def prepare(tr, tc, n):
                if not there(n):
                    return
                par = tc % 2
                if not there(n, 2):
                    g.wait_ge(S["q_ready"], BANDS if n else 1)
                if there(n, 2):
                    g.drain()
                    g.wait_ge(S["vt_ps"], n - 1)
                    g.wait_ge(S["s_read"], n * 2 - 2)
                    nc.gpsimd.tensor_tensor(T(40), T(41), T(41), ALU.mult)
                nc.gpsimd.tensor_copy(
                    vw[par][:, 0:KEYS].rearrange("p (a b) -> p a b", b=KC),
                    vP[:, bass.ds(tr * QR, KR), bass.ds(QC * tc, KC)])
                nc.gpsimd.tensor_tensor(
                    mask[par][:],
                    con["mrow"].rearrange("p (t r) -> p t r", r=KR)[:, bass.ds(tr, 1), :]
                    .rearrange("p a r -> p (a r)").unsqueeze(2).broadcast_to([C, KR, KC]),
                    con["mcol"].rearrange("p (t r) -> p t r", r=KC)[:, tc, :].unsqueeze(1)
                    .broadcast_to([C, KR, KC]), ALU.add)
                nc.gpsimd.tensor_tensor(
                    Qm[par].rearrange("p h (a b) -> p h a b", b=16),
                    Qr[:, bass.ds(tr * (2 * QR), 8), 16 * tc:16 * tc + 16].unsqueeze(1)
                    .broadcast_to([C, HEADS, 8, 16]),
                    con["headq"].unsqueeze(2).unsqueeze(3).broadcast_to([C, HEADS, 8, 16]),
                    ALU.mult).then_inc(S["qm_ready"], 1)
            slots(g, prepare)
            g.wait_ge(S["f_in"], F_IN)
            nc.gpsimd.tensor_copy(wdr.rearrange("p (g k c) -> p g c k", g=DG, c=CPG),
                                  raw["wd"].rearrange("p (g c k) -> p g c k", g=DG, c=CPG))
            nc.gpsimd.memset(Fpad, 0.0)
            g.wait_ge(S["fs_scaled"], 1)
            nc.gpsimd.tensor_tensor(Fmap[:], fs[:, 0, :], fs[:, 1, :], ALU.add)
            for b in range(2, 8):
                g.drain()
                nc.gpsimd.tensor_tensor(Fmap[:], Fmap[:], fs[:, b, :], ALU.add)
            g.drain()
            nc.gpsimd.tensor_copy(Fpad[:, 0:FH, 0:FH], Fmap[:].rearrange("p (a b) -> p a b", b=FH))
            g.drain()
            for w in range(WINS):
                i = nc.gpsimd.tensor_copy(Fcut[:, w, :].rearrange("p (a b) -> p a b", b=WB),
                                          Fpad[:, :, WSTEP * w:WSTEP * w + WB])
            i.then_inc(S["f_cut"], 1)

            def kernel_sums(U, wT):
                for x in range(3):
                    nc.gpsimd.tensor_tensor(U[1][x], wT[:, x, :], wT[:, 6 + x, :], ALU.add)
                g.drain()
                for x in range(3):
                    nc.gpsimd.tensor_tensor(U[0][x], U[1][x], wT[:, 3 + x, :], ALU.add)
                g.drain()
                for x in range(3):
                    i = nc.gpsimd.tensor_tensor(U[1][x], U[1][x], wT[:, 3 + x, :], ALU.subtract)
                return i

            def row_maps(dsts, at, pairs):
                d = [padp[:, bass.ds(at + k // 2, pairs), k % 2, :] for k in range(4)]
                for k, (a, b, op) in enumerate(((0, 2, ALU.subtract), (1, 2, ALU.add), (2, 1, ALU.subtract),
                                                (1, 3, ALU.subtract))):
                    i = nc.gpsimd.tensor_tensor(dsts[k], d[a], d[b], op)
                return i
            kernel_sums([[w2U[:, k, x, :] for x in range(3)] for k in range(2)], w2T).then_inc(S["u2_sums"], 1)
            g.wait_ge(S["gn_apply"], 3)
            g.wait_ge(S["gn_dve_apply"], 3)

            def maps2(n, par):
                if not (isinstance(n, int) and n < 2):
                    g.drain()
                    g.wait_ge(S["c2_ps"], n - 1)
                    nc.gpsimd.tensor_tensor(T(40), T(41), T(41), ALU.mult)
                row_maps([rows2[par][:, k] for k in range(4)], n * ROWS, ROWS).then_inc(S["r2_ready"], 1)
            maps2(0, 0)
            maps2(1, 1)
            with g.Fori(1, H // R2 // 2) as pair:
                maps2(pair * 2, 0)
                maps2(pair * 2 + 1, 1)
            g.wait_ge(S["wt_ev"], len(JOBS) + 1)
            g.wait_ge(S["y_ps"], 1)
            kernel_sums(w3U, wcmT).then_inc(S["u3_sums"], 1)
            g.wait_ge(S["arm_added"], STEPS)

            def maps3(n, par):
                g.drain()
                g.wait_ge(S["om_ps"], AHEAD - 2 + n * 2)
                nc.gpsimd.tensor_tensor(T(40), T(41), T(41), ALU.mult)
                row_maps(rows3[par], n * (ROWS // 2), ROWS // 2).then_inc(S["r3_ready"], 1)
            with g.Fori(0, STEPS // 2) as pair:
                maps3(pair * 2, 0)
                maps3(pair * 2 + 1, 1)

            def column_offsets(t):
                g.drain()
                nc.gpsimd.tensor_copy(mst, MS[:, bass.ts(t, SAMP)])
                nc.gpsimd.tensor_tensor(
                    DV.rearrange("p (s a) -> p s a", a=WB),
                    VL[:, bass.ts(t, SAMP)].unsqueeze(2).broadcast_to([C, SAMP, WB]),
                    con["iota"][:, 0:WB].unsqueeze(1).broadcast_to([C, SAMP, WB]),
                    ALU.subtract).then_inc(S["dv_ready"], 1)

            def row_offsets(t, par, j):
                nc.gpsimd.tensor_tensor(
                    HU[par][:, PS * j:PS * j + PS, :],
                    UL[:, bass.ds(t * SAMP + PS * j, PS)].unsqueeze(2).broadcast_to([C, PS, WA]),
                    con["iota"].unsqueeze(1).broadcast_to([C, PS, WA]), ALU.subtract).then_inc(S["du_ready"], 1)

            def masked_hat(t, par):
                g.wait_ge(S["v_hat"], t + 1)
                nc.gpsimd.tensor_tensor(HV[par], DV.rearrange("p (s a) -> p s a", a=WB),
                                        mst.unsqueeze(2).broadcast_to([C, SAMP, WB]), ALU.mult)

            def add_out(t, job):
                g.drain()
                g.wait_ge(S["t_ev"], job)
                xw = X[:, bass.ts(t, 128)]
                nc.gpsimd.tensor_tensor(xw, xw, orelu, ALU.add).then_inc(S["x_out"], 1)

            def tile(t, par, first=False, last=False):
                job = first_job(t)
                g.drain()
                g.wait_ge(S["u_hat"], t + 1)
                for c in range(CHUNKS):
                    if c >= 2:
                        g.wait_ge(S["t_ps"], job + (chunk_job(c - 2, first) + 2))
                    elif not first:
                        g.wait_ge(S["t_ps"], job - (2 - 2 * c))
                    sl = slice(CH * c, CH * c + CH)
                    nc.gpsimd.tensor_tensor(
                        PR[c % 2].rearrange("p (s a b) -> p s a b", a=WA, b=WB),
                        HU[par][:, sl, :].unsqueeze(3).broadcast_to([C, CH, WA, WB]),
                        HV[par][:, sl, :].unsqueeze(2).broadcast_to([C, CH, WA, WB]),
                        ALU.mult).then_inc(S["pr_ready"], 1)
                    if c == 0 and not last:
                        column_offsets(t + 1)
                    if 1 <= c <= PARTS and not last:
                        row_offsets(t + 1, 1 - par, c - 1)
                    if c == 4 and not last:
                        masked_hat(t + 1, 1 - par)
                    if c == CHUNKS - 1 and not first:
                        add_out(t - 1, job + (chunk_job(EXTRA[3], False) + 3))
            g.wait_ge(S["om_ps"], AHEAD + (STEPS - 1) * 2)
            g.wait_ge(S["coord"], 1 + 1)
            column_offsets(0)
            for j in range(PARTS):
                row_offsets(0, 0, j)
            masked_hat(0, 0)
            tile(0, 0, first=True)
            g.wait_ge(S["coord"], 1 + STEPS)
            with g.Fori(0, (TILES - 2) // 2) as pair:
                t = pair * 2 + 1
                tile(t, 1)
                tile(t + 1, 0)
            tile(TILES - 1, 1, last=True)
            add_out(TILES - 1, TILES * 28)

        @block.scalar
        def _(act):
            def gn_root(n):
                act.wait_ge(S["gn_var"], n + 1)
                nc.scalar.activation(sd, var, ACT.Sqrt).then_inc(S["gn_sd"], 1)

            def gn_apply(n, dst):
                act.wait_ge(S["gn_scale"], n + 1)
                nc.scalar.activation(dst[:, DVE_ROWS:H, :], Xr[:, DVE_ROWS:H, :], ACT.Identity, scale=rstd,
                                     bias=nb).then_inc(S["gn_apply"], 1)
            def transposed(ns):
                for n in ns:
                    src, dst, m, width = JOBS[n]
                    bank = job_bank(n)
                    act.wait_ge(S["wt_ps"], n + (1 if n < EARLY else 2))
                    if m is None:
                        sv = ps[:, bank, 0:width].rearrange("p (w g c) -> p w g c", g=DG, c=CPG)
                        for w in range(width // 128):
                            i = nc.scalar.activation(dst[:, w], sv[:, w], ACT.Copy)
                        i.then_inc(S["wt_ev"], 1)
                    else:
                        nc.scalar.activation(dst, ps[:, bank, 0:width], ACT.Copy).then_inc(S["wt_ev"], 1)
            gn_root(0)
            gn_apply(0, padm[:, 1:H + 1, 1:W + 1])
            act.wait_ge(S["zeroed"], 1)
            for b, n in L0_ORDER:
                if b == BANDS - 1:
                    act.wait_ge(S["l1c_var"], 1)
                    nc.scalar.activation(lsd, lv, ACT.Sqrt).then_inc(S["l1c_sd"], 1)
                if n is None:
                    act.wait_ge(S["band_ps"], b + 1)
                    if b >= 2:
                        act.wait_ge(S["q_ready"], b - 1)
                    for k, (lo, hi) in enumerate(BAND_ROWS):
                        i = nc.scalar.activation(band[b % 2][:, PW * lo:PW * hi], ps[:, k, 0:PW * (hi - lo)],
                                                 ACT.Copy)
                    i.then_inc(S["band_copied"], 1)
                    act.drain()
                    if b == 0:
                        act.wait_ge(S["kvw_ready"], 1)
                    nc.scalar.activation(Qr[:, BAND * b:BAND * b + BAND, :],
                                         band[b % 2].rearrange("p (h w) -> p h w", w=PW)[:, 0:BAND, 0:W],
                                         ACT.Identity, scale=qw[:, 0:1], bias=qb).then_inc(S["band_ready"], 1)
                else:
                    i, kv = n // 2, n % 2
                    act.wait_ge(S["kv_ps"], n + 1)
                    nc.scalar.activation((kP, vP)[kv][:, PADK + 8 * i:PADK + 8 * i + 8, 3:3 + SUB],
                                         ps[:, 4 + n % 4, 0:384].rearrange("p (a b) -> p a b", b=SUB),
                                         ACT.Identity, bias=(kb, vb_)[kv]).then_inc(S["kv_ev"], 1)
            def values(n, par):
                act.wait_ge(S["vt_ps"], n + 1)
                tv = ps[:, 6, 0:384].rearrange("p (k m d) -> p k m d", k=3, m=HEADS // 2)
                vm = Vm[par].rearrange("p (m x) -> p m x", x=PAIR)
                B = VW * HEADS
                for dst, at, rows_, k, odd in ((slice(0, C), 0, slice(0, C), 0, 0),
                                               (slice(0, 64), B, slice(0, 64), 1, 0),
                                               (slice(64, C), B + VW, slice(0, 64), 0, 1),
                                               (slice(0, C), 2 * B + VW, slice(0, C), 2, 1)):
                    i = nc.scalar.activation(vm[dst, :, at:at + HD],
                                             tv[rows_, k, :, HD * odd:HD * odd + HD], ACT.Copy)
                i.then_inc(S["vt_ev"], 1)

            def slot(tr, tc, n):
                par = tc % 2
                if there(n, 2):
                    act.wait_ge(S["ot_ps"], n - 1)
                    nc.scalar.activation(OT, ps[:, 7, 136:264], ACT.Copy).then_inc(S["ot_ev"], 1)
                for j in range(BLOCKS // 4):
                    if there(n, 1):
                        act.wait_ge(S["pt_ps"], (n - 1) * (BLOCKS // 4) + j + 1)
                        nc.scalar.activation(PT[j], ps[:, 4 + j % 2, 0:512], ACT.Copy).then_inc(S["pt_ev"], 1)
                    if j == 1 and there(n):
                        values(n, par)
                if there(n):
                    act.wait_ge(S["s_sub"], n + 1)
                    nc.scalar.activation(Sx[par][:, :, 0:KEYS], Sx[par][:, :, 0:KEYS],
                                         ACT.Exp).then_inc(S["p_ready"], 1)
            transposed(range(EARLY))
            act.wait_ge(S["wt_ps"], EARLY + 1)
            nc.scalar.activation(wofs[:], ps[:, 0, 0:C], ACT.Copy).then_inc(S["wt_ev"], 1)
            act.wait_ge(S["vm_ready"], 1)
            slots(act, slot)
            gn_root(1)
            gn_apply(1, rows[:, :, 4:4 + W])
            act.wait_ge(S["f_in"], F_IN)
            for b in range(8):
                i = nc.scalar.activation(fs[:, b, :], fs[:, b, :], ACT.Copy, scale=BATCHW[b])
            i.then_inc(S["fs_scaled"], 1)
            act.wait_ge(S["u2_sums"], 1)
            u = w2U.rearrange("p k x o -> p (k x o)")
            nc.scalar.activation(u, u, ACT.Copy, scale=0.5).then_inc(S["u2_ready"], 1)
            transposed(range(EARLY, len(JOBS)))
            gn_root(2)
            gn_apply(2, padm[:, 1:H + 1, 1:W + 1])
            act.wait_ge(S["y_ps"], 1)
            for hh in range(2):
                i = nc.scalar.activation(ys[:, 16 * hh:16 * hh + 16, :].rearrange("p a b -> p (a b)"),
                                         ps[:, 5 + hh, :], ACT.Copy, scale=2.0)
            i.then_inc(S["y_ev"], 1)
            gn_root(3)
            act.wait_ge(S["att_ps"], 1)
            nc.scalar.activation(att, ps[:, 7, 0:1], ACT.Sigmoid).then_inc(S["att_sg"], 1)

            for u in (Fmap[:, 0:864], wextra[:]):
                act.wait_ge(S["u3_sums"], 1)
                i = nc.scalar.activation(u, u, ACT.Copy, scale=0.5)
            i.then_inc(S["u3_ready"], 1)

            def bias_and_ends(r, i):
                act.wait_ge(S["omt_ps"], 1 + r)
                for hf in range(2):
                    act.wait_ge(S["om_ps"], AHEAD + 1 + hf + r * 2)
                    o = oms[hf].rearrange("p (a e w) -> p a e w", e=2, w=W)
                    for e in range(2):
                        m = ps[0:108, TURNS[(2 * i + hf) % 3], 256 * e:256 * e + 192]
                        k = nc.scalar.activation(o[0:108, :, e, :], m.rearrange("p (a w) -> p a w", w=W),
                                                 ACT.Identity, bias=vec[0:108, 10 + hf:11 + hf],
                                                 scale=1.0 - 2.0 * e)
                    k.then_inc(S["om_act"], 1)

            def masks(r):
                act.wait_ge(S["coord"], 1 + r)
                act.wait_ge(S["omt_xy"], 1 + r + 1)
                for hf in range(3):
                    i = nc.scalar.activation(sg[:, SAMP * hf:SAMP * hf + SAMP],
                                             ps[:, 2 + hf // 2, 256 * (hf % 2) + 144:256 * (hf % 2) + 216],
                                             ACT.Sigmoid)
                i.then_inc(S["om_sig"], 1)
                nc.scalar.activation(ee, ee, ACT.Abs).then_inc(S["om_abs"], 1)

            def step(r, i):
                bias_and_ends(r, i)
                if not (isinstance(r, int) and r == 0):
                    masks(r - 1)
            offset_steps(act, step)

            def hat(part):
                nc.scalar.activation(part, part, ACT.Abs)
                act.drain()
                return nc.scalar.activation(part, part, ACT.Relu, scale=-1.0, bias=1.0)

            def column_hats(t):
                act.wait_ge(S["dv_ready"], t + 1)
                hat(DV).then_inc(S["v_hat"], 1)

            column_hats(0)
            act.wait_ge(S["du_ready"], PARTS)
            hat(HU[0].rearrange("p s a -> p (s a)")).then_inc(S["u_hat"], 1)
            masks(STEPS - 1)

            def row_hats(t, par, j):
                act.wait_ge(S["du_ready"], t * PARTS + (j + 1))
                i = hat(HU[par][:, PS * j:PS * j + PS, :].rearrange("p s a -> p (s a)"))
                if j == PARTS - 1:
                    i.then_inc(S["u_hat"], 1)

            def evac(job, dst, src):
                act.wait_ge(S["t_ps"], job + 1)
                nc.scalar.activation(dst, src, ACT.Copy).then_inc(S["t_ev"], 1)

            def value_jobs(job):
                for j in range(3):
                    evac(job + j, valT[:, 384 * j:384 * (j + 1)], ps[:, 6 + j % 2, 0:384])

            def out_job(t, job, bank):
                if not (isinstance(t, int) and t == 0):
                    act.wait_ge(S["x_out"], t)
                act.wait_ge(S["t_ps"], job + 1)
                nc.scalar.activation(orelu, ps[:, bank, 0:128], ACT.Relu, bias=bdc).then_inc(S["t_ev"], 1)

            def tile(t, par, first=False, last=False):
                job = first_job(t)
                k = 0
                for c in range(CHUNKS):
                    if not (first and c < 2):
                        act.wait_ge(S["g_ready"], t * CHUNKS + c - 1)
                    for j in range(2):
                        evac(job + k, PTS[(2 * c + j) % 4][0:WK, :], ps[0:WK, 6 + k % 2, 0:384])
                        k += 1
                    if c in EXTRA[:3] and not first:
                        j = EXTRA.index(c)
                        evac(job + k, valT[:, 384 * j:384 * (j + 1)], ps[:, 6 + k % 2, 0:384])
                        k += 1
                    if c == EXTRA[3] and not first:
                        out_job(t - 1, job + k, 6 + k % 2)
                        k += 1
                    if c == 2 and not last:
                        column_hats(t + 1)
                    if 3 <= c < 3 + PARTS and not last:
                        row_hats(t + 1, 1 - par, c - 3)
            tile(0, 0, first=True)
            with act.Fori(0, (TILES - 2) // 2) as pair:
                t = pair * 2 + 1
                tile(t, 1)
                tile(t + 1, 0)
            tile(TILES - 1, 1, last=True)
            job = TILES * 28 - 4
            value_jobs(job)
            out_job(TILES - 1, job + 3, 7)

        @block.tensor
        def _(pe):
            mm = nc.tensor.matmul

            def gn_mean(n):
                pe.wait_ge(S["gn_stats"], n + 1)
                mm(ps[:, 7, 0:2], con["gmean"], t2, start=True, stop=True).then_inc(S["gn_mean"], 1)
            def transpose_weights(n):
                src, dst, m, width = JOBS[n]
                for w, col in src:
                    k = w.shape[0]
                    i = nc.tensor.transpose(ps[:, job_bank(n), col:col + k], w, ident[0:k, 0:k])
                i.then_inc(S["wt_ps"], 1)
            pe.wait_ge(S["c_in"], C_IN)
            gn_mean(0)
            pe.wait_ge(S["gn_apply"], 1)
            pe.wait_ge(S["gn_dve_apply"], 1)
            pe.wait_ge(S["kvw_ready"], 1)
            for b, n in L0_ORDER:
                if n is None:
                    if b >= 1:
                        pe.wait_ge(S["band_copied"], b)
                    for k, (lo, hi) in enumerate(BAND_ROWS):
                        m = mm(ps[:, k, 0:PW * (hi - lo)], con["own3"][:, 0:C],
                               padm[:, BAND * b + lo:BAND * b + hi, :], start=True, stop=True)
                    m.then_inc(S["band_ps"], 1)
                else:
                    i, kv = n // 2, n % 2
                    if n >= 4:
                        pe.wait_ge(S["kv_ev"], n - 3)
                    for t in range(TAPS):
                        a, b = 16 * i + t // 3, t % 3
                        m = mm(ps[:, 4 + n % 4, 0:384], kvT[kv][:, t, :],
                               padm[:, a:a + 15:2, b:b + 95:2], start=(t == 0), stop=(t == 8))
                    m.then_inc(S["kv_ps"], 1)

            pe.wait_ge(S["band_copied"], BANDS)
            pe.wait_ge(S["w_in"], W_IN)
            pe.wait_ge(S["wprep"], 1)
            for n in range(EARLY):
                if n >= 4:
                    pe.wait_ge(S["wt_ev"], n - 3)
                transpose_weights(n)
            pe.wait_ge(S["wt_ev"], EARLY)
            mm(ps[:, 0, 0:C], raw["fsm"], sqT[:, 3, :], start=True, stop=True).then_inc(S["wt_ps"], 1)
            pe.wait_ge(S["wt_ev"], EARLY + 1)

            def scores(tr, tc, heads):
                for h in heads:
                    o = ps[:, h // 2, 256 * (h % 2):256 * (h % 2) + KEYS]
                    i = mm(o, Qm[tc % 2][:, h, :], kP[:, bass.ds(tr * QR, KR), QC * tc:QC * tc + KC],
                           start=True, stop=True)
                i.then_inc(S["s_ready"], 1)

            def transpose_values(n, par):
                if there(n, 1):
                    pe.wait_ge(S["vt_ev"], n)
                for k, (a, b) in enumerate(((0, 128), (128, KPAD), (64, KPAD))):
                    i = nc.tensor.transpose(ps[0:b - a, 6, 128 * k:128 * k + 128], vw[par][:, a:b], ident)
                i.then_inc(S["vt_ps"], 1)

            def attend(n, par, between):
                J = BLOCKS // 4

                def probs(j):
                    if j == 2:
                        pe.wait_ge(S["pt_ev"], n * J + 1)
                    for q in range(4):
                        i = nc.tensor.transpose(ps[:, 4 + j % 2, 128 * q:128 * q + 128],
                                                flat[:, 128 * (4 * j + q):128 * (4 * j + q + 1)], ident)
                    i.then_inc(S["pt_ps"], 1)
                flat = Sx[par].rearrange("p h k -> p (h k)")
                pe.wait_ge(S["p_ready"], n + 1)
                if there(n, 1):
                    pe.wait_ge(S["pt_ev"], n * J)
                probs(0)
                probs(1)
                between()
                probs(2)
                if there(n, 1):
                    pe.wait_ge(S["l0_x"], n)
                pe.wait_ge(S["vt_ev"], n + 1)
                for j in range(J):
                    pe.wait_ge(S["pt_ev"], n * J + j + 1)
                    for q in range(4):
                        b = 4 * j + q
                        i = mm(ps[:, 7, 0:VW * HEADS], PT[j][:, 128 * q:128 * q + 128],
                               block_values(par, b), start=(b == 0), stop=(b == BLOCKS - 1))
                i.then_inc(S["o_ready"], 1)

            def block_values(par, b):
                return Vm[par][:, VW * HEADS * b:VW * HEADS * (b + 1)]

            def slot(tr, tc, n):
                par = tc % 2
                if there(n):
                    pe.wait_ge(S["qm_ready"], n + 1)
                    if there(n, 1):
                        pe.wait_ge(S["s_read"], n * 2 - 1)
                    scores(tr, tc, range(HEADS // 2))
                if there(n, 2):
                    pe.wait_ge(S["o_norm"], n - 1)
                    nc.tensor.transpose(ps[:, 7, 136:264], On, ident).then_inc(S["ot_ps"], 1)
                if there(n):
                    if there(n, 1):
                        pe.wait_ge(S["s_read"], n * 2)
                    scores(tr, tc, range(HEADS // 2, HEADS))
                if there(n, 2):
                    pe.wait_ge(S["ot_ev"], n - 1)
                    mm(ps[:, 7, 264:392], sqT[:, 0, :], OT, start=True, stop=True).then_inc(S["pj_ps"], 1)
                values = (lambda: transpose_values(n, par)) if there(n) else (lambda: None)
                if there(n, 1):
                    attend(n - 1, 1 - par, values)
                else:
                    values()

            pe.wait_ge(S["kv_ev"], 12)
            slots(pe, slot)
            gn_mean(1)

            pe.wait_ge(S["gn_apply"], 2)
            pe.wait_ge(S["gn_dve_apply"], 2)
            pe.wait_ge(S["l1diag"], 1)

            def message(k, bank, src, job=None):
                mm(ps[:, bank, 0:W], shiftd[:], ones[:], start=True, stop=False)
                if job is not None:
                    if job - EARLY >= 4:
                        pe.wait_ge(S["wt_ev"], job - 2)
                    transpose_weights(job)
                pe.wait_ge(S["row_new"], k)
                for t in range(9):
                    m = mm(ps[:, bank, 0:W], w1T[:, t, :], rows[:, src, t:t + W], start=False, stop=(t == 8))
                m.then_inc(S["row_ps"], 1)
            message(0, 0, slice(0, 1))
            with pe.Fori(0, (H - 2) // 2) as pair:
                i = pair * 2 + 1
                message(i, 1, bass.ds(i, 1))
                message(i + 1, 0, bass.ds(i + 1, 1))
            message(H - 1, 1, slice(H - 1, H))
            pe.wait_ge(S["f_cut"], 1)
            for j in range(LATE_STEPS):
                n = EARLY + j
                message(H + j, j % 2, slice(H - 2 - j, H - 1 - j), n if n < len(JOBS) else None)
            with pe.Fori(LATE_STEPS // 2, (H - 2) // 2) as pair:
                i = pair * 2 + 1
                message(i + (H - 1), 0, bass.ds(i * -1 + (H - 1), 1))
                message(i + H, 1, bass.ds(i * -1 + (H - 2), 1))
            gn_mean(2)

            pe.wait_ge(S["wt_ev"], len(JOBS) + 1)
            for hh in range(2):
                m = mm(ps[:, 5 + hh, :], sqT[:, 4, :], Fmap[:, 512 * hh:512 * hh + 512], start=True, stop=True)
            m.then_inc(S["y_ps"], 1)
            pe.wait_ge(S["gn_apply"], 3)
            pe.wait_ge(S["gn_dve_apply"], 3)
            pe.wait_ge(S["u2_ready"], 1)
            pe.wait_ge(S["y_ev"], 1)

            def conv2(n, par):
                pe.wait_ge(S["r2_ready"], n + 1)
                if not (isinstance(n, int) and n < 2):
                    pe.wait_ge(S["c2_x"], n - 1)
                for k in range(4):
                    for x in range(3):
                        wt = w2T[:, (0, 6)[k // 3] + x, :] if k in (0, 3) else w2U[:, k - 1, x, :]
                        m = mm(ps[:, 4 * par + k, 0:384], wt, rows2[par][:, k, :, x:x + W],
                               start=(x == 0), stop=(x == 2))
                m.then_inc(S["c2_ps"], 1)
            conv2(0, 0)
            conv2(1, 1)
            with pe.Fori(1, H // R2 // 2) as pair:
                conv2(pair * 2, 0)
                conv2(pair * 2 + 1, 1)
            gn_mean(3)
            pe.wait_ge(S["gap_in"], 1)
            mm(ps[:, 7, 0:1], sqT[:, 2, :], gapn, start=True, stop=True).then_inc(S["att_ps"], 1)

            def arm(n, i):
                pe.wait_ge(S["xg_ready"], n + 1)
                if there(n, 2):
                    pe.wait_ge(S["arm_added"], n - 1)
                mm(ps[:, i, 0:384], sqT[:, 1, :], xg[i], start=True, stop=True)
                mm(ps[:, 2 + i, 0:384], wofs[:], xg[i], start=True, stop=True).then_inc(S["arm_ps"], 1)
            arm(0, 0)
            arm(1, 1)
            with pe.Fori(1, STEPS // 2) as pair:
                arm(pair * 2, 0)
                arm(pair * 2 + 1, 1)

            def offset_conv(r, i):
                pe.wait_ge(S["r3_ready"], r + 1)
                for hf in range(2):
                    pe.wait_ge(S["om_ev"], AHEAD - 2 + hf + r * 2)
                    bank = TURNS[(2 * i + hf) % 3]
                    sl = slice(108 * hf, 108 * hf + 108)
                    for k in range(4):
                        at = (bank, 0), (bank + 1, 0), (bank + 1, 256), (bank, 256)
                        for x in range(3):
                            wt = wcmT[:, 2 * k + x, sl] if k in (0, 3) else w3U[k - 1][x][:, sl]
                            m = mm(ps[0:108, at[k][0], at[k][1]:at[k][1] + 192], wt,
                                   rows3[i % 2][k][:, :, x:x + W], start=(x == 0), stop=(x == 2))
                    m.then_inc(S["om_ps"], 1)

            def pixels_first(r):
                pe.wait_ge(S["om_sig"], 1 + r)
                pe.wait_ge(S["omt_xy"], 1 + r)
                pe.wait_ge(S["om_ev"], AHEAD + 2 + r * 2)
                for i in range(3):
                    for hf in range(2):
                        m = nc.tensor.transpose(
                            ps[:, 2 + i // 2, 256 * (i % 2) + 108 * hf:256 * (i % 2) + 108 * hf + 108],
                            oms[hf][0:108, 128 * i:128 * i + 128], ident[0:108, 0:108])
                m.then_inc(S["omt_ps"], 1)

            def step(r, i):
                offset_conv(r, i)
                if not (isinstance(r, int) and r == 0):
                    pixels_first(r - 1)
            pe.wait_ge(S["u3_ready"], 1)
            offset_steps(pe, step)
            pixels_first(STEPS - 1)

            def turn(job, k, srcs, rows_out):
                if not (isinstance(job, int) and job + k < 2):
                    pe.wait_ge(S["t_ev"], job + (k - 1))
                for j, s in enumerate(srcs):
                    i = nc.tensor.transpose(ps[0:rows_out, 6 + k % 2, 128 * j:128 * j + 128], s, ident)
                return i

            def contract(n, c, jobs_done, between=None):
                if not (isinstance(n, int) and n < 2):
                    pe.wait_ge(S["g_used"], n - 1)
                pe.wait_ge(S["t_ev"], jobs_done)
                for j in range(CH):
                    if j == CH // 2 and between:
                        between()
                    s = CH * c + j
                    i = mm(ps[:, 3 * (c % 2) + j // 2, 256 * (j % 2):256 * (j % 2) + WINS * CPG],
                           PTS[(2 * c + j // 3) % 4][0:WK, 128 * (j % 3):128 * (j % 3) + 128],
                           Fwin[:, s // TAPS, :, :].rearrange("p w c -> p (w c)"), start=True, stop=True)
                i.then_inc(S["g_ready"], 1)

            def values_of(par, job, k, j):
                turn(job, k, [val[par][:, 128 * (3 * j + i):128 * (3 * j + i) + 128] for i in range(3)],
                     C).then_inc(S["t_ps"], 1)

            def output_of(job, k):
                pe.wait_ge(S["t_ev"], job + k)
                for j in range(9):
                    i = mm(ps[:, 6 + k % 2, 0:128], wdT[:, j, :], valT[:, 128 * j:128 * j + 128],
                           start=(j == 0), stop=(j == 8))
                i.then_inc(S["t_ps"], 1)

            def tile(t, par, first=False):
                job = first_job(t)
                k = 0
                for c in range(CHUNKS):
                    n = t * CHUNKS + c
                    pe.wait_ge(S["pr_ready"], n + 1)
                    for j in range(2):
                        src = [PR[c % 2][:, WK * (3 * j + i):WK * (3 * j + i + 1)] for i in range(3)]
                        i = turn(job, k, src, WK)
                        i.then_inc(S["t_ps"], 1)
                        k += 1
                    if c == 0:
                        if not first:
                            contract(n - 1, CHUNKS - 1, job)
                    else:
                        between = None
                        if c in EXTRA[:3] and not first:
                            j = EXTRA.index(c)
                            between = lambda: values_of(1 - par, job, k, j)
                            pe.wait_ge(S["summed"], t * CHUNKS - (2 - j) * (CHUNKS // 3))
                        elif c == EXTRA[3] and not first:
                            between = lambda: output_of(job, k)
                        contract(n - 1, c - 1, job + (chunk_job(c - 1, first) + 2), between)
                        k += 1 if between else 0
            tile(0, 0, first=True)
            with pe.Fori(0, (TILES - 2) // 2) as pair:
                t = pair * 2 + 1
                tile(t, 1)
                tile(t + 1, 0)
            tile(TILES - 1, 1)
            job = TILES * 28 - 4
            contract(TILES * CHUNKS - 1, CHUNKS - 1, job)
            pe.wait_ge(S["summed"], TILES * CHUNKS)
            for j in range(3):
                values_of(1, job, j, j)
            output_of(job, 3)

        @block.vector
        def _(v):
            V = nc.vector

            def gn_stats(n, parts):
                v.drain()
                V.bn_aggr(mv, stats[:, 0:parts, :].rearrange("p a b -> p (a b)"))
                v.drain()
                V.tensor_copy(t2[:, 0:1], mv[:, 0:1])
                V.scalar_tensor_tensor(out=t2[:, 1:2], in0=mv[:, 0:1], scalar=mv[:, 0:1], in1=mv[:, 1:2],
                                       op0=ALU.mult, op1=ALU.add).then_inc(S["gn_stats"], 1)
                v.wait_ge(S["gn_mean"], n + 1)
                V.tensor_copy(gm, ps[:, 7, 0:2])
                v.drain()
                V.scalar_tensor_tensor(out=nv, in0=gm[:, 0:1], scalar=gm[:, 0:1], in1=gm[:, 1:2],
                                       op0=ALU.mult, op1=ALU.subtract)
                v.drain()
                V.tensor_scalar(var, nv, -1.0, EPS, ALU.mult, ALU.add).then_inc(S["gn_var"], 1)
                v.wait_ge(S["gn_sd"], n + 1)
                V.reciprocal(rstd, sd)
                v.drain()
                V.scalar_tensor_tensor(out=nb, in0=gm[:, 0:1], scalar=-1.0, in1=rstd, op0=ALU.mult,
                                       op1=ALU.mult).then_inc(S["gn_scale"], 1)
                v.drain()

            def gn_apply(dst):
                V.tensor_scalar(dst[:, 0:DVE_ROWS, :], Xr[:, 0:DVE_ROWS, :], rstd, nb, ALU.mult,
                                ALU.add).then_inc(S["gn_dve_apply"], 1)

            def zero_border():
                V.memset(padm[:, 0:1, :], 0.0)
                V.memset(padm[:, H + 1:H + 2, :], 0.0)
                V.memset(padm[:, 1:H + 1, 0:1], 0.0)
                V.memset(padm[:, 1:H + 1, PW - 1:PW], 0.0)
            V.memset(ones[:], 1.0)
            V.memset(tiny[:, 40:44], 0.0)
            zero_border()
            for h in range(4):
                v.wait_ge(S[f"x_in{h}"], 16)
                for i in range(6 * h, 6 * h + 6):
                    V.bn_stats(stats[:, i, :], X[:, 384 * i:384 * i + 384])
            gn_stats(0, STEPS)
            gn_apply(padm[:, 1:H + 1, 1:W + 1])
            v.wait_ge(S["c_in"], C_IN)
            for b in range(BANDS):
                v.wait_ge(S["band_ready"], b + 1)
                src = band[b % 2].rearrange("p (h w) -> p h w", w=PW)
                dst = Qr[:, BAND * b:BAND * b + BAND, :]
                for t in range(1, TAPS):
                    tap = src[:, t // 3:t // 3 + BAND, t % 3:t % 3 + W]
                    if t > 1:
                        v.drain()
                    i = V.scalar_tensor_tensor(out=dst, in0=tap, scalar=qw[:, t:t + 1], in1=dst, op0=ALU.mult,
                                               op1=ALU.add)
                i.then_inc(S["q_ready"], 1)
                if b == 3:
                    v.wait_ge(S["w_in"], W_IN)
                    V.tensor_scalar(lv, rvar, EPS, None, ALU.add).then_inc(S["l1c_var"], 1)
                    v.wait_ge(S["l1c_sd"], 1)
                    V.reciprocal(lrs, lsd)
                    v.drain()
                    V.tensor_tensor(lsc, gam, lrs, ALU.mult)
                    v.drain()
                    V.tensor_scalar(raw["w1"], raw["w1"], lsc, None, ALU.mult).then_inc(S["wprep"], 1)
                    V.scalar_tensor_tensor(out=lsh, in0=rmean, scalar=lsc, in1=bet, op0=ALU.mult, op1=ALU.subtract)
                    v.drain()
                    V.tensor_scalar(shiftd[:], ident, lsh, -1.0, ALU.mult, ALU.mult).then_inc(S["l1diag"], 1)
            v.wait_ge(S["kv_ps"], 12)
            for b in range(2):
                V.memset(Sx[b][:, :, KEYS:KPAD], 0.0)
            v.wait_ge(S["vm_zeroed"], 1)
            for b in range(2):
                vm = Vm[b].rearrange("p (m x) -> p m x", x=PAIR)
                B = VW * HEADS
                V.memset(vm[:, :, HD:HD + 1], 1.0)
                V.memset(vm[0:64, :, B + HD:B + HD + 1], 1.0)
                V.memset(vm[64:C, :, B + VW + HD:B + VW + HD + 1], 1.0)
                V.memset(vm[:, :, 2 * B + VW + HD:2 * B + VW + HD + 1], 1.0)
            v.drain().then_inc(S["vm_ready"], 1)

            def masked(n, par, half):
                k = HEADS // 2
                sc = ps[:, 2 * half:2 * half + 2, :].rearrange("p b (h k) -> p (b h) k", h=2)[:, :, 0:KEYS]
                v.drain()
                v.wait_ge(S["s_ready"], n * 2 + (half + 1))
                V.tensor_tensor(
                    Sx[par][:, k * half:k * half + k, 0:KEYS], sc,
                    mask[par][:].rearrange("p a b -> p (a b)").unsqueeze(1).broadcast_to([C, k, KEYS]),
                    ALU.add).then_inc(S["s_read"], 1)

            def softmax_max(par):
                sx = Sx[par][:, :, 0:KEYS]
                v.drain()
                V.tensor_reduce(smax, sx, AX.X, ALU.max)
                v.drain()
                V.tensor_tensor(sx, sx, smax.unsqueeze(2).broadcast_to([C, HEADS, KEYS]),
                                ALU.subtract).then_inc(S["s_sub"], 1)

            def normalise(n):
                O = ps[:, 7, 0:VW * HEADS].rearrange("p (h d) -> p h d", h=HEADS)
                v.wait_ge(S["o_ready"], n + 1)
                V.reciprocal(srec.unsqueeze(2), O[:, :, HD:HD + 1])
                v.drain()
                V.tensor_tensor(On.rearrange("p (h d) -> p h d", h=HEADS), O[:, :, 0:HD],
                                srec.unsqueeze(2).broadcast_to([C, HEADS, HD]), ALU.mult).then_inc(S["o_norm"], 1)

            def add_attention(tr, tc, n):
                v.wait_ge(S["pj_ps"], n + 1)
                xw = Xr[:, bass.ds(tr * 8, 8), 16 * tc:16 * tc + 16]
                V.scalar_tensor_tensor(out=xw, in0=ps[:, 7, 264:392].rearrange("p (a b) -> p a b", b=16),
                                       scalar=pjb, in1=xw, op0=ALU.add, op1=ALU.add).then_inc(S["l0_x"], 1)

            def tile_stats(tr, tc, n):
                V.bn_stats(stats[:, bass.ds(n, 1), :].rearrange("p a b -> p (a b)"),
                           Xr[:, bass.ds(tr * 8, 8), 16 * tc:16 * tc + 16])

            def slot(tr, tc, n):
                if there(n):
                    masked(n, tc % 2, 0)
                    masked(n, tc % 2, 1)
                if there(n, 3):
                    tile_stats(*before(tr, tc, 3), n - 3)
                if there(n, 2):
                    add_attention(*before(tr, tc, 2), n - 2)
                if there(n):
                    softmax_max(tc % 2)
                if there(n, 1):
                    normalise(n - 1)
            slots(v, slot)
            v.drain()

            tile_stats(TR - 1, TC - 1, TILES0 - 1)
            gn_stats(1, TILES0)
            V.memset(rows[:, :, 0:4], 0.0)
            V.memset(rows[:, :, 4 + W:RP], 0.0)
            gn_apply(rows[:, :, 4:4 + W])
            v.drain()
            v.wait_ge(S["gn_apply"], 2)

            def add_row(k, bank, dst):
                v.wait_ge(S["row_ps"], k + 1)
                rw = rows[:, dst, 4:4 + W]
                V.scalar_tensor_tensor(out=rw, in0=ps[:, bank, 0:W].unsqueeze(1), scalar=0.0, in1=rw, op0=ALU.max,
                                       op1=ALU.add).then_inc(S["row_new"], 1)
            add_row(0, 0, slice(1, 2))
            with v.Fori(0, (H - 2) // 2) as pair:
                i = pair * 2 + 1
                add_row(i, 1, bass.ds(i + 1, 1))
                add_row(i + 1, 0, bass.ds(i + 2, 1))

            def add_to_x(row):
                v.drain()
                V.tensor_tensor(Xr[:, row, :], Xr[:, row, :], rows[:, row, 4:4 + W], ALU.add)
                v.drain()
                V.bn_stats(stats[:, row, :].rearrange("p a b -> p (a b)"),
                           Xr[:, row, :].rearrange("p a b -> p (a b)"))
            add_to_x(slice(H - 1, H))
            add_row(H - 1, 1, slice(H - 2, H - 1))
            add_to_x(slice(H - 2, H - 1))
            with v.Fori(0, (H - 2) // 2) as pair:
                i = pair * 2 + 1
                add_row(i + (H - 1), 0, bass.ds(i * -1 + (H - 2), 1))
                add_to_x(bass.ds(i * -1 + (H - 2), 1))
                add_row(i + H, 1, bass.ds(i * -1 + (H - 3), 1))
                add_to_x(bass.ds(i * -1 + (H - 3), 1))
            gn_stats(2, H)
            zero_border()
            gn_apply(padm[:, 1:H + 1, 1:W + 1])
            third = 1.0 / 3.0

            def upsample(src, diff, dst):
                V.tensor_tensor(diff[:, 0:FH - 1], src[:, 1:FH], src[:, 0:FH - 1], ALU.subtract)
                V.tensor_copy(dst[:, 1:3 * FH:3], src)
                V.tensor_copy(dst[:, 0:1], src[:, 0:1])
                V.tensor_copy(dst[:, 3 * FH - 1:3 * FH], src[:, FH - 1:FH])
                v.drain()
                for k in (1, 2):
                    V.scalar_tensor_tensor(out=dst[:, 1 + k:3 * FH - 1:3], in0=diff[:, 0:FH - 1],
                                           scalar=k * third, in1=src[:, 0:FH - 1], op0=ALU.mult, op1=ALU.add)
                v.drain()
            v.wait_ge(S["y_ev"], 1)
            upsample(ys, yd, yr)
            upsample(yr.rearrange("p a b -> p b a"), cd.rearrange("p a b -> p b a"),
                     Y.rearrange("p a b -> p b a"))
            def add_conv2(n, par):
                v.wait_ge(S["c2_ps"], n + 1)
                xs = [Xp[:, bass.ds(n * ROWS, ROWS), e, :] for e in range(2)]
                m = [ps[:, 4 * par + k, 0:384].rearrange("p (a w) -> p a w", w=W) for k in range(4)]
                for e in range(2):
                    V.scalar_tensor_tensor(out=xs[e], in0=m[e], scalar=b2, in1=xs[e], op0=ALU.add, op1=ALU.add)
                for k in (1, 2):
                    v.drain()
                    V.tensor_tensor(xs[0], xs[0], m[k], ALU.add)
                    i = V.tensor_tensor(xs[1], xs[1], m[k + 1], ALU.subtract)
                i.then_inc(S["c2_x"], 1)
                v.drain()
                for k in range(2):
                    V.bn_stats(stats[:, bass.ds(n * 2 + k, 1), :].rearrange("p a b -> p (a b)"),
                               X[:, bass.ds(n * 768 + 384 * k, 384)])
                v.drain()
            with v.Fori(0, H // R2 // 2) as pair:
                add_conv2(pair * 2, 0)
                add_conv2(pair * 2 + 1, 1)
            gn_stats(3, STEPS)
            V.scalar_tensor_tensor(out=gapn, in0=mv[:, 0:1], scalar=rstd, in1=nb, op0=ALU.mult,
                                   op1=ALU.add).then_inc(S["gap_in"], 1)
            v.wait_ge(S["att_sg"], 1)
            V.tensor_scalar(att1, att, 1.0, None, ALU.add)
            v.drain()
            V.tensor_tensor(s3, rstd, att1, ALU.mult)
            V.tensor_tensor(b3, nb, att1, ALU.mult)
            v.drain()

            def gated(n, i):
                V.tensor_scalar(xg[i], X[:, bass.ts(n, 384)], s3, b3, ALU.mult, ALU.add).then_inc(S["xg_ready"], 1)

            def add_arm(n, i):
                v.wait_ge(S["arm_ps"], n + 1)
                xw = X[:, bass.ts(n, 384)]
                V.tensor_tensor(xw, ps[:, i, 0:384], xw, ALU.add)
                m = padm[:, bass.ds(n * ROWS + 1, ROWS), 1:W + 1]
                V.tensor_tensor(m, ps[:, 2 + i, 0:384].rearrange("p (a b) -> p a b", b=W),
                                Y[:, bass.ts(n, ROWS), :], ALU.add).then_inc(S["arm_added"], 1)
            gated(0, 0)
            gated(1, 1)
            with v.Fori(0, (STEPS - 2) // 2) as pair:
                for i in range(2):
                    add_arm(pair * 2 + i, i)
                    gated(pair * 2 + (2 + i), i)
            add_arm(STEPS - 2, 0)
            add_arm(STEPS - 1, 1)
            v.drain()
            by = con["basey"].rearrange("p (i s) -> p i s", i=3)
            bx = con["basex"].rearrange("p (i s) -> p i s", i=3)

            def middles(r, i):
                for hf in range(2):
                    v.wait_ge(S["om_act"], 1 + hf + r * 2)
                    o = oms[hf].rearrange("p (a e w) -> p a e w", e=2, w=W)
                    for k, ops in enumerate(((ALU.add, ALU.add), (ALU.add, ALU.subtract))):
                        m = ps[0:108, TURNS[(2 * i + hf) % 3] + 1, 256 * k:256 * k + 192]
                        for e in range(2):
                            j = V.tensor_tensor(o[0:108, :, e, :], o[0:108, :, e, :],
                                                m.rearrange("p (a w) -> p a w", w=W), ops[e])
                        if k == 0:
                            v.drain()
                    j.then_inc(S["om_ev"], 1)

            def coordinates(r):
                pt = ps[:, 2:4, :].rearrange("p b (i s) -> p (b i) s", i=2)[:, 0:3, :]
                v.wait_ge(S["omt_ps"], 1 + r + 1)
                V.tensor_tensor(yx[:, 0, :].rearrange("p (i s) -> p i s", i=3), pt[:, :, 0:SAMP], by, ALU.add)
                V.tensor_tensor(yx[:, 1, :].rearrange("p (i s) -> p i s", i=3), pt[:, :, SAMP:2 * SAMP], bx,
                                ALU.add)
                v.drain()
                V.tensor_scalar(con["basey"], con["basey"], float(ROWS), None, ALU.add)
                V.tensor_scalar(ee, yx, -47.5, None, ALU.add).then_inc(S["omt_xy"], 1)
                V.tensor_scalar(uv, yx, 1.0, float(H - 2), ALU.max, ALU.min)
                v.drain()
                V.tensor_scalar(uv, uv, 1.0, third, ALU.subtract, ALU.mult)
                v.drain()
                V.tensor_copy(UL[:, bass.ts(r, 216)], uv[:, 0, :])
                V.tensor_scalar(wja, uv[:, 1, :], third, -0.5, ALU.mult, ALU.add)
                v.drain()
                V.tensor_scalar(wja, wja, ROUND, None, ALU.add)
                v.drain()
                V.tensor_scalar(wja, wja, -ROUND, None, ALU.add)
                v.drain()
                V.scalar_tensor_tensor(out=VL[:, bass.ts(r, 216)], in0=wja, scalar=-float(WSTEP),
                                       in1=uv[:, 1, :], op0=ALU.mult, op1=ALU.add)
                V.tensor_copy(WI[:, bass.ts(r, 216)], wja)
                v.wait_ge(S["om_sig"], 1 + r + 1)
                v.wait_ge(S["om_abs"], r + 1)
                V.tensor_scalar(ee, ee, -1.0, 48.5, ALU.mult, ALU.add)
                v.drain()
                V.tensor_scalar(ee, ee, 0.0, 1.0, ALU.max, ALU.min)
                v.drain()
                V.tensor_tensor(ma, sg, ee[:, 0, :], ALU.mult)
                v.drain()
                V.tensor_tensor(MS[:, bass.ts(r, 216)], ma, ee[:, 1, :], ALU.mult).then_inc(S["coord"], 1)
                v.drain()

            def step(r, i):
                middles(r, i)
                if not (isinstance(r, int) and r == 0):
                    coordinates(r - 1)
            offset_steps(v, step)
            coordinates(STEPS - 1)

            oh3 = OH.rearrange("p (s w) -> p s w", w=WINS)

            def window_sum(n, par, c):
                v.wait_ge(S["g_used"], n + 1)
                V.tensor_reduce(
                    val[par][:, CH * CPG * c:CH * CPG * (c + 1)].rearrange("p (s c) -> p s c", s=CH),
                    GM[c % 2].rearrange("p (s w c) -> p s c w", s=CH, w=WINS), AX.X,
                    ALU.add).then_inc(S["summed"], 1)

            def one_hot(t, half):
                k = SAMP // 2
                V.tensor_tensor(oh3[:, k * half:k * half + k, :],
                                WI[:, bass.ds(t * SAMP + k * half, k)].unsqueeze(2).broadcast_to([C, k, WINS]),
                                con["iota"][:, 0:WINS].unsqueeze(1).broadcast_to([C, k, WINS]),
                                ALU.is_equal).then_inc(S["onehot"], 1)

            def tile(t, par, first=False, last=False):
                for c in range(CHUNKS):
                    n = t * CHUNKS + c
                    if c % (CHUNKS // 2) == 0:
                        v.wait_ge(S["onehot"], t * 2 + (1 + c // (CHUNKS // 2)))
                    if not (first and c < 2):
                        v.wait_ge(S["summed"], n - 1)
                    v.wait_ge(S["g_ready"], n + 1)
                    V.tensor_tensor(
                        GM[c % 2].rearrange("p (s w c) -> p s w c", s=CH, w=WINS),
                        ps[:, 3 * (c % 2):3 * (c % 2) + 3, :].rearrange("p b (s n) -> p (b s) n", s=2)
                        [:, :, 0:WINS * CPG].rearrange("p s (w c) -> p s w c", w=WINS),
                        oh3[:, CH * c:CH * c + CH, :].unsqueeze(3).broadcast_to([C, CH, WINS, CPG]),
                        ALU.mult).then_inc(S["g_used"], 1)
                    if c >= 1:
                        window_sum(n - 1, par, c - 1)
                    elif not first:
                        window_sum(n - 1, 1 - par, CHUNKS - 1)
                    if c == 2:
                        v.wait_ge(S["g_used"], n)
                        one_hot(t, 1)
                    if c == 8 and not last:
                        v.wait_ge(S["g_used"], n)
                        one_hot(t + 1, 0)
            one_hot(0, 0)
            tile(0, 0, first=True)
            with v.Fori(0, (TILES - 2) // 2) as pair:
                t = pair * 2 + 1
                tile(t, 1)
                tile(t + 1, 0)
            tile(TILES - 1, 1, last=True)
            window_sum(TILES * CHUNKS - 1, 1, CHUNKS - 1)


_INS = ["x", "L0_conv_qkv_w", "L0_conv_qkv_b", "L0_conv_proj_w", "L0_conv_proj_b", "L1_conv_conv_w",
        "L1_conv_gamma", "L1_conv_beta", "L1_conv_run_mean", "L1_conv_run_var", "L2_conv_weight", "L2_conv_bias",
        "L3_conv_feat_s", "L3_conv_w_atten", "L3_conv_w_fsm", "L3_conv_w_off", "L3_conv_w_cm", "L3_conv_b_cm",
        "L3_conv_w_dcn", "L3_conv_b_dcn"]


def kernel(**inputs):
    import concourse.bacc as bacc
    from concourse.bass_utils import run_bass_kernel_spmd

    nc = bacc.Bacc("TRN2", target_bir_lowering=False, num_devices=1)
    arrays, d = {}, {}
    for name in _INS:
        a = np.ascontiguousarray(inputs[name])
        arrays[f"in_{name}"] = a
        d[name] = nc.dram_tensor(f"in_{name}", a.shape, mybir.dt.from_np(a.dtype), kind="ExternalInput").ap()
    made = shape_constants()
    arrays["in_consts"] = np.ascontiguousarray(np.concatenate([made[n] for n in CONSTS], axis=1))
    consts = nc.dram_tensor("in_consts", arrays["in_consts"].shape, F32, kind="ExternalInput").ap()
    out = nc.dram_tensor("out_0_dram", (1, C, H, W), F32, kind="ExternalOutput").ap()
    build_program(nc, d, consts, out)
    r = run_bass_kernel_spmd(nc, [arrays], core_ids=[0])
    return r.results[0]["out_0_dram"]
```
